# Optimizing a Trainium2 kernel written in Bass

```python
import numpy as np
import jax
import jax.numpy as jnp

def _softmax(x, axis=-1):
    return jax.nn.softmax(x, axis=axis)

def _gelu(x):
    return jax.nn.gelu(x, approximate=True)

def _silu(x):
    return jax.nn.silu(x)

def _sigmoid(x):
    return jax.nn.sigmoid(x)

def _layernorm(x, axis=-1, eps=1e-05):
    m = jnp.mean(x, axis=axis, keepdims=True)
    v = jnp.var(x, axis=axis, keepdims=True)
    return (x - m) / jnp.sqrt(v + eps)

def _scatter_add(tgt, idx, src, axis=0):
    return tgt.at[idx].add(src)

def _segment_sum(src, seg, n):
    return jax.ops.segment_sum(src, seg, n)
kernel_name = 'mk_macaron_d2_jaxref_r8_fcd4b0'

def setup_inputs(seed: int=0):
    np.random.seed(seed)
    _w = jnp.asarray

    def _L0_attn_setup():
        import jax, jax.numpy as jnp
        import numpy as np
        import math
        D_MODEL = 128
        N_HEADS = 16
        HEAD_DIM = D_MODEL // N_HEADS
        LAMBDA_INIT = 0.8 - 0.6 * math.exp(-0.3 * 0)
        EPS = 1e-06

        def _rope_cache(seq_len, head_dim, dtype):
            half = head_dim // 2
            inv_freq = 1.0 / 10000.0 ** (jnp.arange(half, dtype=jnp.float32) / max(half, 1))
            ang = jnp.arange(seq_len, dtype=jnp.float32)[:, None] * inv_freq[None, :]
            return (jnp.cos(ang).astype(dtype)[None, None], jnp.sin(ang).astype(dtype)[None, None])

        def _apply_rope(x, cos, sin):
            half = x.shape[-1] // 2
            x1, x2 = (x[..., :half], x[..., half:])
            return jnp.concatenate([x1 * cos - x2 * sin, x1 * sin + x2 * cos], axis=-1)
        key = jax.random.key(seed)
        ks = jax.random.split(key, 16)
        B, S, D = (2, 256, D_MODEL)
        s = 0.02
        return {'x': jax.random.normal(ks[0], (B, S, D), jnp.float32), 'Wq': jax.random.normal(ks[1], (2 * D, D), jnp.float32) * s, 'bq': jnp.zeros((2 * D,), jnp.float32), 'Wk': jax.random.normal(ks[2], (2 * D, D), jnp.float32) * s, 'bk': jnp.zeros((2 * D,), jnp.float32), 'Wv': jax.random.normal(ks[3], (D, D), jnp.float32) * s, 'bv': jnp.zeros((D,), jnp.float32), 'Wo': jax.random.normal(ks[4], (D, D), jnp.float32) * s, 'bo': jnp.zeros((D,), jnp.float32), 'head_norm_w': jnp.ones((N_HEADS, HEAD_DIM), jnp.float32), 'lq1': jax.random.normal(ks[5], (N_HEADS, HEAD_DIM), jnp.float32) * 0.1, 'lk1': jax.random.normal(ks[6], (N_HEADS, HEAD_DIM), jnp.float32) * 0.1, 'lq2': jax.random.normal(ks[7], (N_HEADS, HEAD_DIM), jnp.float32) * 0.1, 'lk2': jax.random.normal(ks[8], (N_HEADS, HEAD_DIM), jnp.float32) * 0.1}
    _L0_attn_in = _L0_attn_setup()

    def _L0_ffn_setup():
        import jax, jax.numpy as jnp
        import numpy as np
        D, H, E, K, S = (128, 256, 8, 2, 1)
        B, L = (4, 256)
        key = jax.random.key(seed)
        ks = jax.random.split(key, 9)
        std = 0.02
        return {'x': jax.random.normal(ks[0], (B, L, D), dtype=jnp.float32), 'router_w': jax.random.normal(ks[1], (E, D), dtype=jnp.float32) * std, 'experts_bias': jnp.zeros((E,), dtype=jnp.float32), 'w1': jax.random.normal(ks[2], (E, D, H), dtype=jnp.float32) * std, 'w3': jax.random.normal(ks[3], (E, D, H), dtype=jnp.float32) * std, 'w2': jax.random.normal(ks[4], (E, H, D), dtype=jnp.float32) * std, 'sw1': jax.random.normal(ks[5], (S, D, H), dtype=jnp.float32) * std, 'sw3': jax.random.normal(ks[6], (S, D, H), dtype=jnp.float32) * std, 'sw2': jax.random.normal(ks[7], (S, H, D), dtype=jnp.float32) * std}
    _L0_ffn_in = _L0_ffn_setup()

    def _L1_attn_setup():
        import jax, jax.numpy as jnp
        import numpy as np
        B, T, D, H = (4, 256, 128, 16)
        E = D // H
        DH = D // 4
        key = jax.random.key(seed)
        ks = jax.random.split(key, 9)
        s = D ** (-0.5)
        return {'x': jax.random.normal(ks[0], (B, T, D), jnp.float32), 'q_w': jax.random.normal(ks[1], (D, D), jnp.float32) * s, 'k_w': jax.random.normal(ks[2], (D, D), jnp.float32) * s, 'v_w': jax.random.normal(ks[3], (D, D), jnp.float32) * s, 'o_w': jax.random.normal(ks[4], (D, D), jnp.float32) * s, 'cs_w1': jax.random.normal(ks[5], (DH, D), jnp.float32) * s, 'cs_b1': jnp.zeros((DH,), jnp.float32), 'cs_w2': jax.random.normal(ks[6], (H, DH), jnp.float32) * DH ** (-0.5), 'cs_b2': jnp.zeros((H,), jnp.float32), 'decay_params': jax.random.normal(ks[7], (H, E), jnp.float32) + 3.0}
    _L1_attn_in = _L1_attn_setup()

    def _L1_ffn_setup():
        import jax, jax.numpy as jnp
        import numpy as np
        B, S, H, F, G = (8, 256, 128, 512, 128)
        EPS = 1e-05

        def _dequant(q, scales, g):
            K, N = q.shape
            w = (q.astype(jnp.float32) - 128.0).reshape(K // g, g, N) * scales[:, None, :]
            return w.reshape(K, N)
        key = jax.random.key(seed)
        ks = jax.random.split(key, 8)
        x = jax.random.normal(ks[0], (B, S, H), dtype=jnp.float32)
        ln_gamma = jnp.ones((H,), jnp.float32)
        ln_beta = jnp.zeros((H,), jnp.float32)
        fc1_q = jax.random.randint(ks[1], (H, F), 0, 32, dtype=jnp.int32)
        fc2_q = jax.random.randint(ks[2], (F, H), 0, 32, dtype=jnp.int32)
        fc1_scales = jax.random.uniform(ks[3], (H // G, F), jnp.float32) * 0.02 + 0.001
        fc2_scales = jax.random.uniform(ks[4], (F // G, H), jnp.float32) * 0.02 + 0.001
        fc1_bias = jax.random.normal(ks[5], (F,), jnp.float32) * 0.02
        fc2_bias = jax.random.normal(ks[6], (H,), jnp.float32) * 0.02
        return {'x': x, 'ln_gamma': ln_gamma, 'ln_beta': ln_beta, 'fc1_q': fc1_q, 'fc1_scales': fc1_scales, 'fc1_bias': fc1_bias, 'fc2_q': fc2_q, 'fc2_scales': fc2_scales, 'fc2_bias': fc2_bias}
    _L1_ffn_in = _L1_ffn_setup()
    _d = {'L0_attn_x': _L0_attn_in['x'], 'L0_attn_Wq': _L0_attn_in['Wq'], 'L0_attn_bq': _L0_attn_in['bq'], 'L0_attn_Wk': _L0_attn_in['Wk'], 'L0_attn_bk': _L0_attn_in['bk'], 'L0_attn_Wv': _L0_attn_in['Wv'], 'L0_attn_bv': _L0_attn_in['bv'], 'L0_attn_Wo': _L0_attn_in['Wo'], 'L0_attn_bo': _L0_attn_in['bo'], 'L0_attn_head_norm_w': _L0_attn_in['head_norm_w'], 'L0_attn_lq1': _L0_attn_in['lq1'], 'L0_attn_lk1': _L0_attn_in['lk1'], 'L0_attn_lq2': _L0_attn_in['lq2'], 'L0_attn_lk2': _L0_attn_in['lk2'], 'L0_ffn_router_w': _L0_ffn_in['router_w'], 'L0_ffn_experts_bias': _L0_ffn_in['experts_bias'], 'L0_ffn_w1': _L0_ffn_in['w1'], 'L0_ffn_w3': _L0_ffn_in['w3'], 'L0_ffn_w2': _L0_ffn_in['w2'], 'L0_ffn_sw1': _L0_ffn_in['sw1'], 'L0_ffn_sw3': _L0_ffn_in['sw3'], 'L0_ffn_sw2': _L0_ffn_in['sw2'], 'L1_attn_q_w': _L1_attn_in['q_w'], 'L1_attn_k_w': _L1_attn_in['k_w'], 'L1_attn_v_w': _L1_attn_in['v_w'], 'L1_attn_o_w': _L1_attn_in['o_w'], 'L1_attn_cs_w1': _L1_attn_in['cs_w1'], 'L1_attn_cs_b1': _L1_attn_in['cs_b1'], 'L1_attn_cs_w2': _L1_attn_in['cs_w2'], 'L1_attn_cs_b2': _L1_attn_in['cs_b2'], 'L1_attn_decay_params': _L1_attn_in['decay_params'], 'L1_ffn_ln_gamma': _L1_ffn_in['ln_gamma'], 'L1_ffn_ln_beta': _L1_ffn_in['ln_beta'], 'L1_ffn_fc1_q': _L1_ffn_in['fc1_q'], 'L1_ffn_fc1_scales': _L1_ffn_in['fc1_scales'], 'L1_ffn_fc1_bias': _L1_ffn_in['fc1_bias'], 'L1_ffn_fc2_q': _L1_ffn_in['fc2_q'], 'L1_ffn_fc2_scales': _L1_ffn_in['fc2_scales'], 'L1_ffn_fc2_bias': _L1_ffn_in['fc2_bias']}
    _x0 = _d['L0_attn_x']
    _d['L0_attn_x'] = jax.random.normal(jax.random.fold_in(jax.random.key(seed), 1), (16, 256, 128), dtype=_x0.dtype)
    del _x0
    return _d

def reference(L0_attn_x, L0_attn_Wq, L0_attn_bq, L0_attn_Wk, L0_attn_bk, L0_attn_Wv, L0_attn_bv, L0_attn_Wo, L0_attn_bo, L0_attn_head_norm_w, L0_attn_lq1, L0_attn_lk1, L0_attn_lq2, L0_attn_lk2, L0_ffn_router_w, L0_ffn_experts_bias, L0_ffn_w1, L0_ffn_w3, L0_ffn_w2, L0_ffn_sw1, L0_ffn_sw3, L0_ffn_sw2, L1_attn_q_w, L1_attn_k_w, L1_attn_v_w, L1_attn_o_w, L1_attn_cs_w1, L1_attn_cs_b1, L1_attn_cs_w2, L1_attn_cs_b2, L1_attn_decay_params, L1_ffn_ln_gamma, L1_ffn_ln_beta, L1_ffn_fc1_q, L1_ffn_fc1_scales, L1_ffn_fc1_bias, L1_ffn_fc2_q, L1_ffn_fc2_scales, L1_ffn_fc2_bias):

    def _L0_attn_ref(x, Wq, bq, Wk, bk, Wv, bv, Wo, bo, head_norm_w, lq1, lk1, lq2, lk2):
        import jax, jax.numpy as jnp
        import numpy as np
        import math
        D_MODEL = 128
        N_HEADS = 16
        HEAD_DIM = D_MODEL // N_HEADS
        LAMBDA_INIT = 0.8 - 0.6 * math.exp(-0.3 * 0)
        EPS = 1e-06

        def _rope_cache(seq_len, head_dim, dtype):
            half = head_dim // 2
            inv_freq = 1.0 / 10000.0 ** (jnp.arange(half, dtype=jnp.float32) / max(half, 1))
            ang = jnp.arange(seq_len, dtype=jnp.float32)[:, None] * inv_freq[None, :]
            return (jnp.cos(ang).astype(dtype)[None, None], jnp.sin(ang).astype(dtype)[None, None])

        def _apply_rope(x, cos, sin):
            half = x.shape[-1] // 2
            x1, x2 = (x[..., :half], x[..., half:])
            return jnp.concatenate([x1 * cos - x2 * sin, x1 * sin + x2 * cos], axis=-1)
        B, S, D = x.shape
        H, hd = (N_HEADS, HEAD_DIM)
        dtype = x.dtype
        q = (x @ Wq.T + bq).reshape(B, S, H, 2 * hd).transpose(0, 2, 1, 3)
        k = (x @ Wk.T + bk).reshape(B, S, H, 2 * hd).transpose(0, 2, 1, 3)
        v = (x @ Wv.T + bv).reshape(B, S, H, hd).transpose(0, 2, 1, 3)
        q1, q2 = (q[..., :hd], q[..., hd:])
        k1, k2 = (k[..., :hd], k[..., hd:])
        cos, sin = _rope_cache(S, hd, dtype)
        q1, q2 = (_apply_rope(q1, cos, sin), _apply_rope(q2, cos, sin))
        k1, k2 = (_apply_rope(k1, cos, sin), _apply_rope(k2, cos, sin))
        scale = 1.0 / math.sqrt(hd)
        s1 = jnp.einsum('bhqd,bhkd->bhqk', q1, k1) * scale
        s2 = jnp.einsum('bhqd,bhkd->bhqk', q2, k2) * scale
        causal = jnp.triu(jnp.ones((S, S), bool), k=1)
        neg = jnp.finfo(dtype).min
        s1 = jnp.where(causal, neg, s1)
        s2 = jnp.where(causal, neg, s2)
        a1 = jax.nn.softmax(s1, axis=-1)
        a2 = jax.nn.softmax(s2, axis=-1)
        lam = LAMBDA_INIT + jnp.exp(jnp.sum(lq1 * lk1, -1)) - jnp.exp(jnp.sum(lq2 * lk2, -1))
        attn = a1 - lam.astype(dtype)[None, :, None, None] * a2
        out = jnp.einsum('bhqk,bhkd->bhqd', attn, v)
        rms = jnp.mean(out * out, axis=-1, keepdims=True)
        out = out * jax.lax.rsqrt(rms + EPS)
        out = out * head_norm_w[None, :, None, :]
        out = out * (1.0 - LAMBDA_INIT)
        out = out.transpose(0, 2, 1, 3).reshape(B, S, D)
        return out @ Wo.T + bo

    def _L0_ffn_ref(x, router_w, experts_bias, w1, w3, w2, sw1, sw3, sw2):
        import jax, jax.numpy as jnp
        import numpy as np
        D, H, E, K, S = (128, 256, 8, 2, 1)
        B, L = (4, 256)
        b, l, d = x.shape
        xf = x.reshape(-1, d)
        sg = jnp.einsum('td,sdh->tsh', xf, sw1)
        su = jnp.einsum('td,sdh->tsh', xf, sw3)
        shared_out = jnp.einsum('tsh,shd->td', jax.nn.silu(sg) * su, sw2)
        logits = xf @ router_w.T + experts_bias
        rw, sel = jax.lax.top_k(logits, K)
        rw = jax.nn.softmax(rw.astype(jnp.float32), axis=-1).astype(x.dtype)
        cw = (jax.nn.one_hot(sel, E, dtype=x.dtype) * rw[..., None]).sum(axis=1)
        g = jnp.einsum('td,edh->teh', xf, w1)
        u = jnp.einsum('td,edh->teh', xf, w3)
        eo = jax.nn.silu(g) * u
        moe_out = jnp.einsum('te,teh,ehd->td', cw, eo, w2)
        return (moe_out + shared_out).reshape(b, l, d)

    def _L1_attn_ref(x, q_w, k_w, v_w, o_w, cs_w1, cs_b1, cs_w2, cs_b2, decay_params):
        import jax, jax.numpy as jnp
        import numpy as np
        B, T, D, H = (4, 256, 128, 16)
        E = D // H
        DH = D // 4
        Bx, Tx, Dx = x.shape
        q = (x @ q_w.T).reshape(Bx, Tx, H, E)
        k = (x @ k_w.T).reshape(Bx, Tx, H, E)
        v = (x @ v_w.T).reshape(Bx, Tx, H, E)
        lc = jax.nn.sigmoid(jnp.tanh(x @ cs_w1.T + cs_b1) @ cs_w2.T + cs_b2)
        base = jax.nn.sigmoid(decay_params)[None, None]
        lam = jnp.clip(base * (1.0 + 0.2 * lc[..., None]), 0.0, 0.9995)

        def step(state, inp):
            qt, kt, vt, dt = inp
            state = state * dt[..., None] + kt[..., None] * vt[:, :, None, :]
            out_t = jnp.einsum('bhe,bhef->bhf', qt, state)
            return (state, out_t)
        init = jnp.zeros((Bx, H, E, E), x.dtype)
        xs = (jnp.swapaxes(q, 0, 1), jnp.swapaxes(k, 0, 1), jnp.swapaxes(v, 0, 1), jnp.swapaxes(lam, 0, 1))
        _, ys = jax.lax.scan(step, init, xs)
        y = jnp.swapaxes(ys, 0, 1).reshape(Bx, Tx, Dx)
        return y @ o_w.T

    def _L1_ffn_ref(x, ln_gamma, ln_beta, fc1_q, fc1_scales, fc1_bias, fc2_q, fc2_scales, fc2_bias):
        import jax, jax.numpy as jnp
        import numpy as np
        B, S, H, F, G = (8, 256, 128, 512, 128)
        EPS = 1e-05

        def _dequant(q, scales, g):
            K, N = q.shape
            w = (q.astype(jnp.float32) - 128.0).reshape(K // g, g, N) * scales[:, None, :]
            return w.reshape(K, N)
        residual = x
        mu = jnp.mean(x, axis=-1, keepdims=True)
        var = jnp.mean(jnp.square(x - mu), axis=-1, keepdims=True)
        h = (x - mu) * jax.lax.rsqrt(var + EPS) * ln_gamma + ln_beta
        hf = h.reshape(-1, H)
        w1 = _dequant(fc1_q, fc1_scales, G)
        y = hf @ w1 + fc1_bias
        y = jax.nn.silu(y)
        w2 = _dequant(fc2_q, fc2_scales, G)
        z = y @ w2 + fc2_bias
        return residual + 0.5 * z.reshape(residual.shape)
    x = L0_attn_x
    x = x + 0.5 * _L0_ffn_ref(_layernorm(x, axis=-1), L0_ffn_router_w, L0_ffn_experts_bias, L0_ffn_w1, L0_ffn_w3, L0_ffn_w2, L0_ffn_sw1, L0_ffn_sw3, L0_ffn_sw2)
    x = x + _L0_attn_ref(_layernorm(x, axis=-1), L0_attn_Wq, L0_attn_bq, L0_attn_Wk, L0_attn_bk, L0_attn_Wv, L0_attn_bv, L0_attn_Wo, L0_attn_bo, L0_attn_head_norm_w, L0_attn_lq1, L0_attn_lk1, L0_attn_lq2, L0_attn_lk2)
    x = x + 0.5 * _L0_ffn_ref(_layernorm(x, axis=-1), L0_ffn_router_w, L0_ffn_experts_bias, L0_ffn_w1, L0_ffn_w3, L0_ffn_w2, L0_ffn_sw1, L0_ffn_sw3, L0_ffn_sw2)
    x = x + 0.5 * _L1_ffn_ref(_layernorm(x, axis=-1), L1_ffn_ln_gamma, L1_ffn_ln_beta, L1_ffn_fc1_q, L1_ffn_fc1_scales, L1_ffn_fc1_bias, L1_ffn_fc2_q, L1_ffn_fc2_scales, L1_ffn_fc2_bias)
    x = x + _L1_attn_ref(_layernorm(x, axis=-1), L1_attn_q_w, L1_attn_k_w, L1_attn_v_w, L1_attn_o_w, L1_attn_cs_w1, L1_attn_cs_b1, L1_attn_cs_w2, L1_attn_cs_b2, L1_attn_decay_params)
    x = x + 0.5 * _L1_ffn_ref(_layernorm(x, axis=-1), L1_ffn_ln_gamma, L1_ffn_ln_beta, L1_ffn_fc1_q, L1_ffn_fc1_scales, L1_ffn_fc1_bias, L1_ffn_fc2_q, L1_ffn_fc2_scales, L1_ffn_fc2_bias)
    return x

_drawn_inputs = setup_inputs


def setup_inputs(seed=0):
    import zlib

    import numpy as np

    out = dict(_drawn_inputs(seed))
    spreads = {'L0_attn_bq': (0.0, 0.8),
     'L0_attn_bk': (0.0, 0.8),
     'L0_attn_bv': (0.0, 0.1),
     'L0_attn_bo': (0.0, 0.1),
     'L0_attn_head_norm_w': (1.0, 0.2),
     'L0_ffn_experts_bias': (0.0, 0.8),
     'L1_attn_cs_b1': (0.0, 2.0),
     'L1_attn_cs_b2': (0.0, 0.78),
     'L1_ffn_ln_gamma': (1.0, 0.2),
     'L1_ffn_ln_beta': (0.0, 0.1)}
    factors = {'L0_attn_Wq': 8.0,
     'L0_attn_Wk': 8.0,
     'L0_attn_lq1': 8.0,
     'L0_attn_lk1': 8.0,
     'L0_attn_lq2': 8.0,
     'L0_attn_lk2': 8.0,
     'L0_ffn_router_w': 8.0,
     'L0_ffn_w1': 7.148,
     'L0_ffn_w3': 7.001,
     'L0_ffn_w2': 7.821,
     'L0_ffn_sw1': 4.877,
     'L0_ffn_sw3': 4.727,
     'L0_ffn_sw2': 5.048,
     'L1_attn_cs_w1': 3.302,
     'L1_ffn_fc1_bias': 64.0,
     'L1_ffn_fc2_bias': 64.0}
    for name, (base, spread) in spreads.items():
        noise = np.random.default_rng([zlib.crc32(name.encode()), seed]).standard_normal(out[name].shape)
        drawn = base * np.exp(spread * noise) if base else spread * noise
        out[name] = jnp.asarray(drawn.astype(out[name].dtype))
    for name, factor in factors.items():
        out[name] = (out[name] * factor).astype(out[name].dtype)
    return out
```

```python
from contextlib import ExitStack

import numpy as np
import concourse.bass as bass
from concourse import mybir

F32 = mybir.dt.float32
F32R = mybir.dt.float32r
F16 = mybir.dt.float16
BF16 = mybir.dt.bfloat16
I32 = mybir.dt.int32
ALU = mybir.AluOpType
ACT = mybir.ActivationFunctionType
AX = mybir.AxisListType

P = 128
TG = 4
GN = TG * P
LN_EPS = 1e-5
LAMBDA_INIT = 0.8 - 0.6


class Names:

    def __init__(self, nc, ctx, prefix):
        self.nc, self.ctx, self.prefix = nc, ctx, prefix
        self.sems = []
        ctx.callback(self.clear)

    def clear(self):
        self.nc.clear_and_free_semaphores(self.sems)
        self.nc.all_engine_barrier()

    def sem(self, name):
        sem = self.nc.alloc_semaphore(f"{self.prefix}_{name}")
        self.sems.append(sem)
        return sem

    def sb(self, name, shape, dt):
        return self.ctx.enter_context(self.nc.sbuf_tensor(f"{self.prefix}_{name}", shape, dt))

    def ps(self, name, shape, dt):
        return self.ctx.enter_context(self.nc.psum_tensor(f"{self.prefix}_{name}", shape, dt))


def wait_apart(engine, sem, value, made):
    if not isinstance(value, int):
        value = engine.compute_val(value)
        engine.wait_ge(made, 1)
    engine.wait_ge(sem, value)


class Steps:

    def __init__(self, engine, sem, per_round):
        self.engine, self.sem, self.per_round = engine, sem, per_round

    def begin(self, g):
        self.g, self.k = g, 0

    def __call__(self, instruction, apart=None):
        instruction.then_inc(self.sem, 1)
        self.k += 1
        value = self.g * self.per_round + self.k
        if apart is None:
            self.engine.wait_ge(self.sem, value)
        else:
            wait_apart(self.engine, self.sem, value, apart)

    def end(self):
        assert self.k == self.per_round, self.k


def moe_ffn(nc, tag, x, ident, neghalf, made, w):
    E = w["router_T"].shape[1]
    NE = E + 1
    H = w["w1"].shape[2]
    NC = H // P
    NG = x.shape[1] // TG - 1

    with ExitStack() as ctx:
        nm = Names(nc, ctx, tag)
        up = nm.sb("up", [P, NE, 2, H], F32)
        up_hi = nm.sb("up_hi", [P, NE, 2, H], F32R)
        up_lo = nm.sb("up_lo", [P, NE, 2, H], F32R)
        down = nm.sb("down", [P, NE, NC, P], F32)
        down_hi = nm.sb("down_hi", [P, NE, NC, P], F16)
        down_lo = nm.sb("down_lo", [P, NE, NC, P], F16)
        router = nm.sb("router", [P, E], F32)
        router_hi = nm.sb("router_hi", [P, E], F32R)
        router_lo = nm.sb("router_lo", [P, E], F32R)
        rbias = nm.sb("rbias", [E, 1], F32)
        earlier = nm.sb("earlier", [P, E, E], F32)
        xT_hi = nm.sb("xT_hi", [P, NG, GN], F32R)
        xT_lo = nm.sb("xT_lo", [P, NG, GN], F32R)
        gate = nm.sb("gate", [P, NG, TG, E], F32)
        stats = nm.sb("stats", [P, TG, 6], F32)
        mv = nm.sb("mv", [P, TG, 2], F32)
        var = nm.sb("var", [P, TG], F32)
        rstd = nm.sb("rstd", [P, TG], F32)
        xn = nm.sb("xn", [P, TG, P], F32)
        logT = nm.sb("logT", [E, GN], F32)
        logits = nm.sb("logits", [P, TG, E], F32)
        above = nm.sb("above", [P, TG, E, E], F32)
        equal = nm.sb("equal", [P, TG, E, E], F32)
        rank = nm.sb("rank", [P, TG, E], F32)
        first = nm.sb("first", [P, TG, E], F32)
        second = nm.sb("second", [P, TG, E], F32)
        either = nm.sb("either", [P, TG, E], F32)
        signed = nm.sb("signed", [P, TG, E], F32)
        prod = nm.sb("prod", [P, TG, E], F32)
        gap = nm.sb("gap", [P, TG], F32)
        tgap = nm.sb("tgap", [P, TG], F32)
        mix = nm.sb("mix", [P, TG, E], F32)
        act = nm.sb("act", [P, NC, GN], F32)
        h = nm.sb("h", [P, NC, GN], F32)
        h_hi = nm.sb("h_hi", [P, 2, NC, GN], F16)
        h_lo = nm.sb("h_lo", [P, 2, NC, GN], F16)

        g_ps = nm.ps("g_ps", [P, NC, GN], F32)
        u_ps = nm.ps("u_ps", [P, NC, GN], F32)
        o_ps = nm.ps("o_ps", [P, 2, GN], F32)
        t_ps = nm.ps("t_ps", [P, GN], F32)
        r_ps = nm.ps("r_ps", [P, GN], F32)

        up_in = [nm.sem(f"up_in{e}") for e in range(NE)]
        down_in = nm.sem("down_in")
        router_in = nm.sem("router_in")
        up_hi_done = nm.sem("up_hi_done")
        up_split = nm.sem("up_split")
        down_hi_done = nm.sem("down_hi_done")
        down_split = nm.sem("down_split")
        router_split = nm.sem("router_split")
        consts = nm.sem("consts")
        dve_own = nm.sem("dve_own")
        dve_once = nm.sem("dve_once")
        var_ready = nm.sem("var_ready")
        rstd_ready = nm.sem("rstd_ready")
        xn_ready = nm.sem("xn_ready")
        xT_in_psum = nm.sem("xT_in_psum")
        xT_hi_ready = nm.sem("xT_hi_ready")
        xT_ready = nm.sem("xT_ready")
        logT_in_psum = nm.sem("logT_in_psum")
        logT_ready = nm.sem("logT_ready")
        logits_in_psum = nm.sem("logits_in_psum")
        gap_ready = nm.sem("gap_ready")
        tgap_ready = nm.sem("tgap_ready")
        g_ready = nm.sem("g_ready")
        u_ready = nm.sem("u_ready")
        act_ready = nm.sem("act_ready")
        h_ready = nm.sem("h_ready")
        h_hi_ready = nm.sem("h_hi_ready")
        h_lo_ready = nm.sem("h_lo_ready")
        down_done = nm.sem("down_done")
        added = nm.sem("added")
        block = ctx.enter_context(nc.Block())

        def groups(engine, group):
            group(0, True, True)
            with engine.Fori(1, NG - 1) as g:
                group(g, False, True)
            group(NG - 1, False, False)

        @block.sync
        def _(sp):
            for e in range(NE):
                w1, w3 = (w["sw1"][0], w["sw3"][0]) if e == E else (w["w1"][e], w["w3"][e])
                sp.dma_start(up[:, e, 0, :], w1).then_inc(up_in[e], 16)
                sp.dma_start(up[:, e, 1, :], w3).then_inc(up_in[e], 16)
                if e == 0:
                    sp.dma_start(router[:, :], w["router_T"]).then_inc(router_in, 16)
                    sp.dma_start(rbias[:, :], w["router_bias"]).then_inc(router_in, 16)
            sp.dma_start(down[:, 0:E, :, :], w["w2"].rearrange("e (c p) d -> p e c d", p=P)).then_inc(down_in, 16)
            sp.dma_start(down[:, E, :, :], w["sw2"][0].rearrange("(c p) d -> p c d", p=P)).then_inc(down_in, 16)

        @block.gpsimd
        def _(pool):
            def rstd_of(g):
                pool.wait_ge(var_ready, g + 1)
                nc.gpsimd.tensor_tensor(rstd[:, :], var[:, :], neghalf[:, 0:TG], ALU.pow).then_inc(rstd_ready, 1)

            rstd_of(0)
            for e in range(NE):
                pool.wait_ge(up_hi_done, e + 1)
                nc.gpsimd.tensor_tensor(up_lo[:, e], up[:, e], up_hi[:, e].bitcast(F32), ALU.subtract).then_inc(up_split, 1)
            pool.wait_ge(down_hi_done, 1)
            nc.gpsimd.tensor_tensor(down_lo[:], down[:], down_hi[:], ALU.subtract).then_inc(down_split, 1)

            def group(g, is_first, prepares):
                for e in range(NE):
                    for c in range(NC):
                        k = NC * e + c
                        pool.wait_ge(h_hi_ready, g * (NC * NE) + k + 1)
                        if not (is_first and e < 2):
                            pool.wait_ge(down_done, g * NE + (e - 1 if e >= 2 else 0 if e == 0 else -1))
                        nc.gpsimd.tensor_tensor(h_lo[:, e % 2, c], h[:, c], h_hi[:, e % 2, c],
                                                ALU.subtract).then_inc(h_lo_ready, 1)
                    if e == 0 and prepares:
                        rstd_of(g + 1)

            groups(pool, group)

        @block.scalar
        def _(a):
            def xT_high(g):
                a.wait_ge(xT_in_psum, g + 1)
                nc.scalar.activation(xT_hi[:, g], t_ps[:, :], ACT.Copy).then_inc(xT_hi_ready, 1)

            def gate_tanh(g):
                a.wait_ge(gap_ready, g + 1)
                nc.scalar.activation(tgap[:, :], gap[:, :], ACT.Tanh, scale=0.5).then_inc(tgap_ready, 1)

            for e in range(NE):
                a.wait_ge(up_in[e], 32)
                nc.scalar.activation(up_hi[:, e], up[:, e], ACT.Copy).then_inc(up_hi_done, 1)
                if e == 0:
                    xT_high(0)
            a.wait_ge(down_in, 32)
            nc.scalar.activation(down_hi[:], down[:], ACT.Copy).then_inc(down_hi_done, 1)
            gate_tanh(0)

            def group(g, is_first, prepares):
                for e in range(NE):
                    for c in range(NC):
                        k = NC * e + c
                        a.wait_ge(g_ready, g * (NC * NE) + k + 1)
                        if not (is_first and e == 0):
                            a.wait_ge(h_ready, g * (NC * NE) + k + 1 - NC)
                        nc.scalar.activation(act[:, c], g_ps[:, c], ACT.Silu).then_inc(act_ready, 1)
                    for c in range(NC):
                        k = NC * e + c
                        a.wait_ge(h_ready, g * (NC * NE) + k + 1)
                        if not (is_first and e < 2):
                            a.wait_ge(down_done, g * NE + (e - 1 if e >= 2 else 0 if e == 0 else -1))
                        nc.scalar.activation(h_hi[:, e % 2, c], h[:, c], ACT.Copy).then_inc(h_hi_ready, 1)
                    if prepares:
                        if e == 2:
                            xT_high(g + 1)
                        if e == 6:
                            gate_tanh(g + 1)

            groups(a, group)

        @block.vector
        def _(dve):
            once = Steps(dve, dve_once, 0)
            once.begin(0)
            step = Steps(dve, dve_own, 13)

            def norm_stats(g):
                step.begin(g)
                for t in range(TG):
                    last = nc.vector.bn_stats(stats[:, t], x[:, g * TG + t])
                step(last, made)
                for t in range(TG):
                    last = nc.vector.bn_aggr(mv[:, t], stats[:, t])
                step(last)
                nc.vector.tensor_scalar(var[:, :], mv[:, :, 1], LN_EPS, None, ALU.add).then_inc(var_ready, 1)

            def norm(g):
                dve.wait_ge(rstd_ready, g + 1)
                for t in range(TG):
                    last = nc.vector.tensor_scalar(xn[:, t], x[:, g * TG + t], mv[:, t, 0:1], rstd[:, t:t + 1],
                                                   ALU.subtract, ALU.mult)
                last.then_inc(xn_ready, 1)

            def xT_low(g):
                dve.wait_ge(xT_hi_ready, g + 1)
                nc.vector.tensor_tensor(xT_lo[:, g], t_ps[:, :], xT_hi[:, g].bitcast(F32),
                                        ALU.subtract).then_inc(xT_ready, 1)

            def add_router_bias(g):
                dve.wait_ge(logT_in_psum, g + 1)
                nc.vector.tensor_scalar(logT[:, :], r_ps[0:E, :], rbias[:, 0:1], None, ALU.add).then_inc(logT_ready, 1)

            def choose(g):
                dve.wait_ge(logits_in_psum, g + 1)
                step(nc.vector.tensor_copy(logits[:], t_ps[:, 0:TG * E].rearrange("p (t e) -> p t e", e=E)))
                of_e = logits[:].unsqueeze(3).broadcast_to([P, TG, E, E])
                of_j = logits[:].unsqueeze(2).broadcast_to([P, TG, E, E])
                nc.vector.tensor_tensor(above[:], of_j, of_e, ALU.is_gt)
                step(nc.vector.tensor_tensor(equal[:], of_j, of_e, ALU.is_equal))
                step(nc.vector.tensor_tensor(equal[:], equal[:], earlier[:].unsqueeze(1).broadcast_to([P, TG, E, E]), ALU.mult))
                step(nc.vector.tensor_tensor(above[:], above[:], equal[:], ALU.add))
                step(nc.vector.tensor_reduce(rank[:], above[:], op=ALU.add, axis=AX.X))
                nc.vector.tensor_scalar(first[:], rank[:], 0.0, None, ALU.is_equal)
                step(nc.vector.tensor_scalar(second[:], rank[:], 1.0, None, ALU.is_equal))
                nc.vector.tensor_tensor(either[:], first[:], second[:], ALU.add)
                step(nc.vector.tensor_tensor(signed[:], first[:], second[:], ALU.subtract))
                step(nc.vector.tensor_tensor(prod[:], signed[:], logits[:], ALU.mult))
                nc.vector.tensor_reduce(gap[:], prod[:], op=ALU.add, axis=AX.X).then_inc(gap_ready, 1)

            def make_gate(g):
                dve.wait_ge(tgap_ready, g + 1)
                step(nc.vector.tensor_tensor(mix[:], signed[:], tgap[:].unsqueeze(2).broadcast_to([P, TG, E]), ALU.mult))
                step(nc.vector.tensor_tensor(mix[:], mix[:], either[:], ALU.add))
                step(nc.vector.tensor_scalar(gate[:, g], mix[:], 0.25, None, ALU.mult))
                step.end()

            norm_stats(0)
            for e in range(E):
                last = nc.vector.memset(earlier[:, e, :], 0.0)
            once(last)
            for e in range(1, E):
                last = nc.vector.memset(earlier[:, e, 0:e], 1.0)
            once(last)
            dve.wait_ge(router_in, 32)
            once(nc.vector.tensor_copy(router_hi[:], router[:]))
            nc.vector.tensor_tensor(router_lo[:], router[:], router_hi[:].bitcast(F32), ALU.subtract).then_inc(router_split, 1)
            norm(0)
            xT_low(0)
            add_router_bias(0)
            choose(0)
            make_gate(0)

            def add_onto_x(g, e, value):
                dve.wait_ge(down_done, value)
                if not (isinstance(value, int) and value == 1):
                    dve.wait_ge(added, value - 1)
                o = o_ps[:, e % 2].rearrange("p (t d) -> p t d", d=P)
                for t in range(TG):
                    if e < E:
                        last = nc.vector.scalar_tensor_tensor(x[:, g * TG + t], o[:, t], gate[:, g, t, e:e + 1],
                                                              x[:, g * TG + t], ALU.mult, ALU.add)
                    else:
                        last = nc.vector.scalar_tensor_tensor(x[:, g * TG + t], o[:, t], 0.5, x[:, g * TG + t],
                                                              ALU.mult, ALU.add)
                last.then_inc(added, 1)

            def group(g, is_first, prepares):
                for e in range(NE):
                    for c in range(NC):
                        k = NC * e + c
                        dve.wait_ge(act_ready, g * (NC * NE) + k + 1)
                        dve.wait_ge(u_ready, g * (NC * NE) + k + 1)
                        if not (is_first and e == 0):
                            dve.wait_ge(h_lo_ready, g * (NC * NE) + k + 1 - NC)
                        nc.vector.tensor_tensor(h[:, c], act[:, c], u_ps[:, c], ALU.mult).then_inc(h_ready, 1)
                    if e >= 1:
                        add_onto_x(g, e - 1, g * NE + e)
                    elif not is_first:
                        add_onto_x(g - 1, NE - 1, g * NE)
                    if prepares:
                        if e == 0:
                            norm_stats(g + 1)
                        if e == 1:
                            norm(g + 1)
                        if e == 2:
                            xT_low(g + 1)
                        if e == 4:
                            add_router_bias(g + 1)
                        if e == 5:
                            choose(g + 1)
                        if e == 6:
                            make_gate(g + 1)

            groups(dve, group)
            add_onto_x(NG - 1, NE - 1, NG * NE)
            dve.wait_ge(added, NG * NE)

        @block.tensor
        def _(pe):
            def transpose_x(g):
                pe.wait_ge(xn_ready, g + 1)
                for t in range(TG):
                    last = nc.tensor.transpose(t_ps[:, t * P:(t + 1) * P], xn[:, t], ident[:, :])
                last.then_inc(xT_in_psum, 1)

            def route(g):
                pe.wait_ge(xT_ready, g + 1)
                parts = [(router_hi, xT_hi), (router_hi, xT_lo), (router_lo, xT_hi)]
                for i, (r, xt) in enumerate(parts):
                    last = nc.tensor.matmul(r_ps[0:E, :], r[:, :], xt[:, g], start=(i == 0), stop=(i == 2))
                last.then_inc(logT_in_psum, 1)

            def transpose_logits(g):
                wait_apart(pe, logT_ready, g + 1, made)
                for t in range(TG):
                    last = nc.tensor.transpose(t_ps[:, t * E:(t + 1) * E], logT[:, t * P:(t + 1) * P], ident[0:E, 0:E])
                last.then_inc(logits_in_psum, 1)

            def up_product(ps, which, g, e, c, done):
                cols = slice(c * P, (c + 1) * P)
                parts = [(up_hi, xT_hi), (up_hi, xT_lo), (up_lo, xT_hi)]
                for i, (wt, xt) in enumerate(parts):
                    last = nc.tensor.matmul(ps[:, c], wt[:, e, which, cols], xt[:, g], start=(i == 0), stop=(i == 2))
                last.then_inc(done, 1)

            def down_product(g, e, is_first):
                pe.wait_ge(h_lo_ready, g * (NC * NE) + NC * (e + 1))
                if not (is_first and e < 2):
                    pe.wait_ge(added, g * NE + (e - 1 if e >= 2 else 0 if e == 0 else -1))
                for t in range(TG):
                    n = 0
                    for c in range(NC):
                        for hp, wp in ((h_hi, down_hi), (h_hi, down_lo), (h_lo, down_hi)):
                            last = nc.tensor.matmul(o_ps[:, e % 2, t * P:(t + 1) * P],
                                                    hp[:, e % 2, c, t * P:(t + 1) * P], wp[:, e, c],
                                                    start=(n == 0), stop=(n == 3 * NC - 1))
                            n += 1
                last.then_inc(down_done, 1)

            transpose_x(0)
            pe.wait_ge(router_split, 1)
            route(0)
            transpose_logits(0)

            def group(g, is_first, prepares):
                for e in range(NE):
                    if is_first:
                        pe.wait_ge(up_split, e + 1)
                    for c in range(NC):
                        k = NC * e + c
                        if not (is_first and e == 0):
                            pe.wait_ge(act_ready, g * (NC * NE) + k + 1 - NC)
                        up_product(g_ps, 0, g, e, c, g_ready)
                        if not (is_first and e == 0):
                            pe.wait_ge(h_ready, g * (NC * NE) + k + 1 - NC)
                        up_product(u_ps, 1, g, e, c, u_ready)
                    if prepares:
                        if e == 2:
                            transpose_x(g + 1)
                        if e == 3:
                            route(g + 1)
                        if e == 5:
                            transpose_logits(g + 1)
                    if is_first and e == 1:
                        pe.wait_ge(down_split, 1)
                    if e >= 1:
                        down_product(g, e - 1, is_first)
                    elif not is_first:
                        down_product(g - 1, NE - 1, False)

            groups(pe, group)
            down_product(NG - 1, NE - 1, False)


def dequantized_weights(nc, ctx, w):
    F = w["fc1_q"].shape[1]
    NC = F // P
    nm = Names(nc, ctx, "deq")
    hi1 = nm.sb("fc1_hi", [P, F], F32R)
    lo1 = nm.sb("fc1_lo", [P, F], F32R)
    hi2 = nm.sb("fc2_hi", [P, NC, P], F16)
    lo2 = nm.sb("fc2_lo", [P, NC, P], F16)
    cols = nm.sb("cols", [P, 2 + NC], F32)
    bias2 = nm.sb("bias2", [P, P], F32)
    with ExitStack() as inner:
        tm = Names(nc, inner, "deq")
        q1 = tm.sb("q1", [P, F], I32)
        q2 = tm.sb("q2", [P, NC, P], I32)
        s1 = tm.sb("s1", [P, F], F32)
        s2 = tm.sb("s2", [P, NC, P], F32)
        w1 = tm.sb("w1", [P, F], F32)
        w2 = tm.sb("w2", [P, NC, P], F32)
        arrived = tm.sem("arrived")
        own = tm.sem("own")
        block = inner.enter_context(nc.Block())

        @block.sync
        def _(sp):
            sp.dma_start(q1[:], w["fc1_q"]).then_inc(arrived, 16)
            sp.dma_start(s1[:], w["fc1_scales"].broadcast_to([P, F])).then_inc(arrived, 16)
            sp.dma_start(q2[:], w["fc2_q"].rearrange("(c p) d -> p c d", p=P)).then_inc(arrived, 16)
            sp.dma_start(s2[:], w["fc2_scales"].unsqueeze(0).broadcast_to([P, NC, P])).then_inc(arrived, 16)
            sp.dma_start(cols[:], w["ffn1_cols"]).then_inc(arrived, 16)
            sp.dma_start(bias2[:], w["fc2_bias"].broadcast_to([P, P])).then_inc(arrived, 16)

        @block.vector
        def _(dve):
            dve.wait_ge(arrived, 16 * 6)
            nc.vector.scalar_tensor_tensor(w1[:], q1[:], -128.0, s1[:], ALU.add, ALU.mult).then_inc(own, 1)
            nc.vector.scalar_tensor_tensor(w2[:], q2[:], -128.0, s2[:], ALU.add, ALU.mult).then_inc(own, 1)
            nc.vector.tensor_scalar(bias2[:], bias2[:], 0.25, None, ALU.mult).then_inc(own, 1)
            dve.wait_ge(own, 3)
            nc.vector.tensor_copy(hi1[:], w1[:]).then_inc(own, 1)
            nc.vector.tensor_copy(hi2[:], w2[:]).then_inc(own, 1)
            dve.wait_ge(own, 5)
            nc.vector.tensor_tensor(lo1[:], w1[:], hi1[:].bitcast(F32), ALU.subtract).then_inc(own, 1)
            nc.vector.tensor_tensor(lo2[:], w2[:], hi2[:], ALU.subtract).then_inc(own, 1)
            dve.wait_ge(own, 7)
    return dict(hi1=hi1, lo1=lo1, hi2=hi2, lo2=lo2, cols=cols, bias2=bias2)


def quantized_ffn(nc, tag, x, ident, neghalf, made, w):
    NC = w["hi1"].shape[1] // P
    NG = x.shape[1] // TG - 1
    with ExitStack() as ctx:
        nm = Names(nc, ctx, tag)
        stats = nm.sb("stats", [P, TG, 6], F32)
        mv = nm.sb("mv", [P, 2, TG, 2], F32)
        var = nm.sb("var", [P, TG], F32)
        r0 = nm.sb("r0", [P, 2, TG], F32)
        r1 = nm.sb("r1", [P, 2, TG], F32)
        r01 = nm.sb("r01", [P, 2, TG], F32)
        v1 = nm.sb("v1", [P, TG], F32)
        keep = nm.sb("keep", [P, 2, TG], F32)
        shift = nm.sb("shift", [P, 2, TG], F32)
        hn = nm.sb("hn", [P, TG, P], F32)
        hT = nm.sb("hT", [P, GN], F32)
        hT_hi = nm.sb("hT_hi", [P, 2, GN], F32R)
        hT_lo = nm.sb("hT_lo", [P, 2, GN], F32R)
        y = nm.sb("y", [P, NC, GN], F32)
        y_hi = nm.sb("y_hi", [P, 2, NC, GN], F16)
        y_lo = nm.sb("y_lo", [P, 2, NC, GN], F16)
        y_ps = nm.ps("y_ps", [P, NC, GN], F32)
        z_ps = nm.ps("z_ps", [P, 2, GN], F32)
        t_ps = nm.ps("t_ps", [P, GN], F32)

        stats_own = nm.sem("stats_own")
        scales_own = nm.sem("scales_own")
        r01_ready = nm.sem("r01_ready")
        var_ready = nm.sem("var_ready")
        r0_ready = nm.sem("r0_ready")
        v1_ready = nm.sem("v1_ready")
        r1_ready = nm.sem("r1_ready")
        hn_ready = nm.sem("hn_ready")
        hT_in_psum = nm.sem("hT_in_psum")
        hT_copied = nm.sem("hT_copied")
        hT_hi_ready = nm.sem("hT_hi_ready")
        hT_ready = nm.sem("hT_ready")
        y_in_psum = nm.sem("y_in_psum")
        y_ready = nm.sem("y_ready")
        y_hi_ready = nm.sem("y_hi_ready")
        y_lo_pool = nm.sem("y_lo_pool")
        y_lo_dve = nm.sem("y_lo_dve")
        z_ready = nm.sem("z_ready")
        z_added = nm.sem("z_added")
        x_biased = nm.sem("x_biased")
        x_kept = nm.sem("x_kept")
        block = ctx.enter_context(nc.Block())
        POOL_C = NC - 1

        def pairs(engine, group):
            group(0, 0, True, True)
            group(1, 1, False, True)
            with engine.Fori(1, NG // 2 - 1) as i:
                group(i * 2, 0, False, True)
                group(i * 2 + 1, 1, False, True)
            group(NG - 2, 0, False, True)
            group(NG - 1, 1, False, False)

        @block.gpsimd
        def _(pool):
            def scale_0(g, b):
                pool.wait_ge(var_ready, g + 1)
                nc.gpsimd.tensor_tensor(r0[:, b], var[:], neghalf[:, 0:TG], ALU.pow).then_inc(r0_ready, 1)

            def scale_1(g, b):
                pool.wait_ge(v1_ready, g + 1)
                nc.gpsimd.tensor_tensor(r1[:, b], v1[:], neghalf[:, 0:TG], ALU.pow).then_inc(r1_ready, 1)

            def add_bias(g):
                pool.wait_ge(x_kept, g + 1)
                xs = x[:, bass.ds(g * TG, TG)]
                nc.gpsimd.tensor_tensor(xs, xs, w["bias2"][:].unsqueeze(1).broadcast_to([P, TG, P]),
                                        ALU.add).then_inc(x_biased, 1)

            for g in range(2):
                scale_0(g, g)
                scale_1(g, g)

            def group(g, b, is_first, prepares):
                for c in range(POOL_C):
                    pool.wait_ge(y_hi_ready, g * NC + c + 1)
                    if c == 0 and not (isinstance(g, int) and g < 2):
                        pool.wait_ge(z_ready, g - 1)
                    nc.gpsimd.tensor_tensor(y_lo[:, b, c], y[:, c], y_hi[:, b, c], ALU.subtract).then_inc(y_lo_pool, 1)
                    if c == 0 and prepares:
                        scale_0(g + 2, b)
                    if c == 1:
                        if prepares:
                            scale_1(g + 2, b)
                        add_bias(g)

            pairs(pool, group)

        @block.scalar
        def _(a):
            def high(g, b):
                a.wait_ge(hT_copied, g + 1)
                nc.scalar.activation(hT_hi[:, b], hT[:], ACT.Copy).then_inc(hT_hi_ready, 1)

            high(0, 0)

            def group(g, b, is_first, prepares):
                for c in range(NC):
                    a.wait_ge(y_in_psum, g * NC + c + 1)
                    if not is_first:
                        if c < POOL_C:
                            a.wait_ge(y_lo_pool, g * POOL_C + c + 1 - POOL_C)
                        else:
                            a.wait_ge(y_lo_dve, g)
                    nc.scalar.activation(y[:, c], y_ps[:, c], ACT.Silu, bias=w["cols"][:, 2 + c:3 + c]).then_inc(y_ready, 1)
                    a.wait_ge(y_ready, g * NC + c + 1)
                    if c == 0 and not (isinstance(g, int) and g < 2):
                        a.wait_ge(z_ready, g - 1)
                    nc.scalar.activation(y_hi[:, b, c], y[:, c], ACT.Copy).then_inc(y_hi_ready, 1)
                    if prepares and c == 1:
                        high(g + 1, 1 - b)

            pairs(a, group)

        @block.vector
        def _(dve):
            stats_step = Steps(dve, stats_own, 2)
            scales_step = Steps(dve, scales_own, 5)

            def statistics(g, b):
                stats_step.begin(g)
                for t in range(TG):
                    last = nc.vector.bn_stats(stats[:, t], x[:, g * TG + t])
                stats_step(last, made)
                for t in range(TG):
                    last = nc.vector.bn_aggr(mv[:, b, t], stats[:, t])
                stats_step(last)
                stats_step.end()
                nc.vector.tensor_scalar(var[:], mv[:, b, :, 1], LN_EPS, None, ALU.add).then_inc(var_ready, 1)

            def scales(g, b):
                dve.wait_ge(r0_ready, g + 1)
                scales_step.begin(g)
                scales_step(nc.vector.tensor_tensor(v1[:], r0[:, b], r0[:, b], ALU.mult))
                scales_step(nc.vector.tensor_tensor(v1[:], v1[:], mv[:, b, :, 1], ALU.mult))
                nc.vector.tensor_scalar(v1[:], v1[:], LN_EPS, None, ALU.add).then_inc(v1_ready, 1)
                scales_step(nc.vector.tensor_scalar(keep[:, b], r0[:, b], 0.5, None, ALU.mult))
                scales_step(nc.vector.scalar_tensor_tensor(shift[:, b], mv[:, b, :, 0], -1.0, keep[:, b], ALU.mult, ALU.mult))
                scales_step(nc.vector.tensor_scalar(keep[:, b], keep[:, b], 1.0, None, ALU.add))
                scales_step.end()

            def normalise(g, b):
                dve.wait_ge(r1_ready, g + 1)
                nc.vector.tensor_tensor(r01[:, b], r0[:, b], r1[:, b], ALU.mult).then_inc(r01_ready, 1)
                dve.wait_ge(r01_ready, g + 1)
                for t in range(TG):
                    last = nc.vector.tensor_scalar(hn[:, t], x[:, g * TG + t], mv[:, b, t, 0:1], r01[:, b, t:t + 1],
                                                   ALU.subtract, ALU.mult)
                last.then_inc(hn_ready, 1)

            def keep_x(g, b):
                for t in range(TG):
                    last = nc.vector.tensor_scalar(x[:, g * TG + t], x[:, g * TG + t], keep[:, b, t:t + 1],
                                                   shift[:, b, t:t + 1], ALU.mult, ALU.add)
                last.then_inc(x_kept, 1)

            def affine(g):
                dve.wait_ge(hT_in_psum, g + 1)
                nc.vector.tensor_scalar(hT[:], t_ps[:], w["cols"][:, 0:1], w["cols"][:, 1:2],
                                        ALU.mult, ALU.add).then_inc(hT_copied, 1)

            def low(g, b):
                dve.wait_ge(hT_hi_ready, g + 1)
                nc.vector.tensor_tensor(hT_lo[:, b], hT[:], hT_hi[:, b].bitcast(F32), ALU.subtract).then_inc(hT_ready, 1)

            def add_z(g, b):
                dve.wait_ge(z_ready, g + 1)
                dve.wait_ge(x_biased, g + 1)
                xs = x[:, bass.ds(g * TG, TG)].rearrange("p t d -> p (t d)")
                nc.vector.scalar_tensor_tensor(xs, z_ps[:, b], 0.25, xs, ALU.mult, ALU.add).then_inc(z_added, 1)

            for g in range(2):
                statistics(g, g)
                scales(g, g)
                if g == 0:
                    normalise(0, 0)
                    affine(0)
                    low(0, 0)
                    keep_x(0, 0)

            def group(g, b, is_first, prepares):
                if prepares:
                    normalise(g + 1, 1 - b)
                    statistics(g + 2, b)
                    affine(g + 1)
                if not (isinstance(g, int) and g < 2):
                    add_z(g - 2, b)
                if prepares:
                    scales(g + 2, b)
                    low(g + 1, 1 - b)
                    keep_x(g + 1, 1 - b)
                c = NC - 1
                dve.wait_ge(y_hi_ready, g * NC + c + 1)
                if not (isinstance(g, int) and g < 2):
                    dve.wait_ge(z_ready, g - 1)
                nc.vector.tensor_tensor(y_lo[:, b, c], y[:, c], y_hi[:, b, c], ALU.subtract).then_inc(y_lo_dve, 1)

            pairs(dve, group)
            add_z(NG - 2, 0)
            add_z(NG - 1, 1)
            dve.wait_ge(z_added, NG)

        @block.tensor
        def _(pe):
            def transpose_h(g):
                pe.wait_ge(hn_ready, g + 1)
                if not (isinstance(g, int) and g == 0):
                    pe.wait_ge(hT_copied, g)
                for t in range(TG):
                    last = nc.tensor.transpose(t_ps[:, t * P:(t + 1) * P], hn[:, t], ident[:, :])
                last.then_inc(hT_in_psum, 1)

            def up(g, b, c, is_first):
                if c == 0:
                    pe.wait_ge(hT_ready, g + 1)
                if not is_first:
                    pe.wait_ge(y_ready, g * NC + c + 1 - NC)
                parts = [(w["hi1"], hT_hi), (w["hi1"], hT_lo), (w["lo1"], hT_hi)]
                for i, (wt, ht) in enumerate(parts):
                    last = nc.tensor.matmul(y_ps[:, c], wt[:, c * P:(c + 1) * P], ht[:, b], start=(i == 0), stop=(i == 2))
                last.then_inc(y_in_psum, 1)

            def down(g, b):
                pe.wait_ge(y_lo_pool, (g + 1) * POOL_C)
                pe.wait_ge(y_lo_dve, g + 1)
                if not (isinstance(g, int) and g < 2):
                    pe.wait_ge(z_added, g - 1)
                for t in range(TG):
                    n = 0
                    for c in range(NC):
                        for yp, wp in ((y_hi, w["hi2"]), (y_hi, w["lo2"]), (y_lo, w["hi2"])):
                            last = nc.tensor.matmul(z_ps[:, b, t * P:(t + 1) * P], yp[:, b, c, t * P:(t + 1) * P],
                                                    wp[:, c], start=(n == 0), stop=(n == 3 * NC - 1))
                            n += 1
                last.then_inc(z_ready, 1)

            transpose_h(0)

            def group(g, b, is_first, prepares):
                for c in range(NC):
                    up(g, b, c, is_first)
                    if c == 1 and prepares:
                        transpose_h(g + 1)
                if not is_first:
                    down(g - 1, 1 - b)

            pairs(pe, group)
            down(NG - 1, 1)


def diff_attention(nc, tag, x, ident, neghalf, made, w):
    HEADS, HD = 16, 8
    MAPS = 2 * HEADS
    CH = MAPS // 4
    S = 2 * P
    NB = (x.shape[1] - TG) // 2
    STEPS = 24
    HALF = 12
    LAG = 3
    RING = 4
    QKV = 3 * MAPS * HD - MAPS * HD // 2
    W2 = QKV // 2
    SCALE = HD ** -0.5
    PACK = 32
    RMS_EPS = 1e-6

    with ExitStack() as ctx:
        nm = Names(nc, ctx, tag)
        wqkv_hi = nm.sb("wqkv_hi", [P, QKV], F32R)
        wqkv_lo = nm.sb("wqkv_lo", [P, QKV], F32R)
        qkv_bias = nm.sb("qkv_bias", [P, QKV], F32)
        wo = nm.sb("wo", [P, P], F32)
        wo_bias = nm.sb("wo_bias", [P, P], F32)
        head_w = nm.sb("head_w", [P, 1], F32)
        rope_cos = nm.sb("rope_cos", [P, 2, HD], F32)
        rope_sin = nm.sb("rope_sin", [P, 2, HD], F32)
        ident_bf = nm.sb("ident_bf", [P, P], BF16)
        ident_h = nm.sb("ident_h", [P, P], F16)
        mask = nm.sb("mask", [P, 4, P], BF16)
        branch = nm.sb("branch", [P, HEADS, 2], F32)
        lam_in = nm.sb("lam_in", [P, 4, HEADS, HD], F32)
        lam_sum = nm.sb("lam_sum", [P, 2, HEADS], F32)
        lam_exp = nm.sb("lam_exp", [P, 2, HEADS], F32)

        stats = nm.sb("stats", [P, 2, 6], F32)
        mv = nm.sb("mv", [P, 2, 2], F32)
        var = nm.sb("var", [P, 2], F32)
        rstd = nm.sb("rstd", [P, 2], F32)
        xn = nm.sb("xn", [P, 2, P], F32)
        xT_hi = nm.sb("xT_hi", [P, S], F32R)
        xT_lo = nm.sb("xT_lo", [P, S], F32R)
        qk = nm.sb("qk", [P, 2, 2 * MAPS, HD], F32)
        v_new = nm.sb("v_new", [P, 2, HEADS, HD], F32)
        v = nm.sb("v", [P, 2, 2, HEADS, PACK], F32)
        by_cos = nm.sb("by_cos", [P, 2, 2 * MAPS, HD], F32)
        by_sin = nm.sb("by_sin", [P, 2, 2 * MAPS, HD], F32)
        rot = nm.sb("rot", [P, 2, 2 * MAPS, HD], F32)
        q_pack = nm.sb("q_pack", [P, 2, 2, MAPS, PACK], F16)
        k_pack = nm.sb("k_pack", [P, 2, MAPS, PACK], F16)
        qT = nm.sb("qT", [P, 2, CH, S], F16)
        qmT = nm.sb("qmT", [P, 2, CH, S], F16)
        kT = nm.sb("kT", [P, CH, S], F16)
        k_one = nm.sb("k_one", [P, 2, 4, CH, S], F16)
        prob = nm.sb("prob", [P, RING, 512], F32)
        oT = nm.sb("oT", [P, 2, 512], F32)
        inv = nm.sb("inv", [P, 2, MAPS // 2], F32)
        weighted = nm.sb("weighted", [P, 2, MAPS, HD], F32)
        o = nm.sb("o", [P, 2, HEADS, HD], F32)
        osq = nm.sb("osq", [P, 2, HEADS, HD], F32)
        ms = nm.sb("ms", [P, 2, HEADS], F32)
        rms = nm.sb("rms", [P, 2, HEADS], F32)
        on = nm.sb("on", [P, 2, HEADS, HD], F32)
        onT = nm.sb("onT", [P, S], F32)

        s_ps = nm.ps("s_ps", [P, 2, 512], F32)
        st_ps = nm.ps("st_ps", [P, 2, 512], F32)
        ot_ps = nm.ps("ot_ps", [P, 2, 512], F32)
        m_ps = nm.ps("m_ps", [P, 2, 512], F32)
        m16 = [m_ps[:, i].bitcast(F16) for i in range(2)]

        loaded = nm.sem("loaded")
        packs_ready = nm.sem("packs_ready")
        prepared = nm.sem("prepared")
        lam_summed = nm.sem("lam_summed")
        lam_exped = nm.sem("lam_exped")
        once_own = nm.sem("once_own")
        a_own = nm.sem("a_own")
        d_own = nm.sem("d_own")
        var_ready = nm.sem("var_ready")
        rstd_ready = nm.sem("rstd_ready")
        xn_ready = nm.sem("xn_ready")
        xT_in_psum = nm.sem("xT_in_psum")
        xT_hi_ready = nm.sem("xT_hi_ready")
        xT_ready = nm.sem("xT_ready")
        qkv_in_psum = nm.sem("qkv_in_psum")
        qkv_ready = nm.sem("qkv_ready")
        cos_ready = nm.sem("cos_ready")
        sin_ready = nm.sem("sin_ready")
        rot_ready = nm.sem("rot_ready")
        pack_hi = nm.sem("pack_hi")
        pack_lo = nm.sem("pack_lo")
        packT_in_psum = nm.sem("packT_in_psum")
        packT_ready = nm.sem("packT_ready")
        k_one_ready = [nm.sem("k_one_ready_0"), nm.sem("k_one_ready_1")]
        s_ready = nm.sem("s_ready")
        max_ready = nm.sem("max_ready")
        qmT_in_psum = nm.sem("qmT_in_psum")
        qmT_ready = nm.sem("qmT_ready")
        st_ready = nm.sem("st_ready")
        exp_ready = nm.sem("exp_ready")
        prob_ready = nm.sem("prob_ready")
        v_ready = nm.sem("v_ready")
        pv_done = nm.sem("pv_done")
        oT_copied = nm.sem("oT_copied")
        o_in_psum = nm.sem("o_in_psum")
        o_weighted = nm.sem("o_weighted")
        ms_ready = nm.sem("ms_ready")
        rms_ready = nm.sem("rms_ready")
        on_ready = nm.sem("on_ready")
        onT_in_psum = nm.sem("onT_in_psum")
        onT_ready = nm.sem("onT_ready")
        y_in_psum = nm.sem("y_in_psum")
        x_added = nm.sem("x_added")
        block = ctx.enter_context(nc.Block())

        def turns(engine, turn):
            def peeled(it):
                turn(*[b if 0 <= b < NB else None for b in (it, it - 1, it - 2, it - 3)], it % 2)

            for it in range(4):
                peeled(it)
            with engine.Fori(2, NB // 2) as i:
                for half in range(2):
                    it = i * 2 + half
                    turn(it, it - 1, it - 2, it - 3, half)
            for it in range(NB, NB + 3):
                peeled(it)

        def below(b, n):
            return isinstance(b, int) and b < n

        def unit(u):
            half, k = divmod(u, HALF)
            if k < 4:
                return 1, 16 * half + 4 * k, 4
            return 0, 16 * half + 2 * (k - 4), 2

        @block.sync
        def _(sp):
            sp.dma_start(by_cos[:].rearrange("p a b c -> p (a b c)")[:, 0:QKV], w["wqkv"]).then_inc(loaded, 16)
            sp.dma_start(qkv_bias[:], w["qkv_bias"].broadcast_to([P, QKV])).then_inc(loaded, 16)
            sp.dma_start(on[:, 0].rearrange("p a b -> p (a b)"), w["wo_T"]).then_inc(loaded, 16)
            sp.dma_start(wo_bias[:], w["wo_bias"].broadcast_to([P, P])).then_inc(loaded, 16)
            sp.dma_start(head_w[:], w["head_w"]).then_inc(loaded, 16)
            sp.dma_start(rope_cos[:], w["rope_cos"]).then_inc(loaded, 16)
            sp.dma_start(rope_sin[:], w["rope_sin"]).then_inc(loaded, 16)
            sp.dma_start(osq[:, 0].rearrange("p a b -> p (a b)"), w["causal"]).then_inc(loaded, 16)
            sp.dma_start(lam_in[:], w["lam"].unsqueeze(0).broadcast_to([P, 4, HEADS, HD])).then_inc(loaded, 16)

            sp.wait_ge(packs_ready, 6)

            def turn(A, B, C, D, par):
                if A is None:
                    return
                for half in range(2):
                    wait_apart(sp, packT_ready, A * 4 + (4 if half else 1), made)
                    if C is not None:
                        wait_apart(sp, st_ready, C * STEPS + HALF * (half + 1), made)
                    for r in range(4):
                        rows, ch = slice(32 * r, 32 * r + 32), slice(4 * half, 4 * half + 4)
                        sp.dma_start(k_one[rows, par, r, ch], kT[rows, ch]).then_inc(k_one_ready[half], 16)

            turns(sp, turn)
            for half in range(2):
                sp.wait_ge(k_one_ready[half], NB * 64)

        LOADS = 9

        @block.gpsimd
        def _(pool):
            nc.gpsimd.memset(k_one[:].bitcast(F32), 0.0).then_inc(packs_ready, 1)
            nc.gpsimd.memset(v[:], 0.0).then_inc(packs_ready, 1)
            nc.gpsimd.memset(q_pack[:], 0.0).then_inc(packs_ready, 1)
            nc.gpsimd.memset(k_pack[:], 0.0).then_inc(packs_ready, 1)
            pool.wait_ge(packs_ready, 4)
            nc.gpsimd.memset(v[:, :, :, :, HD:HD + 1].rearrange("p a b c d -> p (a b c) d"), 1.0).then_inc(packs_ready, 1)
            nc.gpsimd.memset(k_pack[:, :, :, 3 * HD:3 * HD + 1].rearrange("p a b c -> p (a b) c"), 1.0).then_inc(packs_ready, 1)
            pool.wait_ge(packs_ready, 6)

            def scale_of(b):
                pool.wait_ge(var_ready, b + 1)
                nc.gpsimd.tensor_tensor(rstd[:], var[:], neghalf[:, 0:2], ALU.pow).then_inc(rstd_ready, 1)

            def rms_of(b, half, j):
                if j == 0:
                    pool.wait_ge(ms_ready, b * 2 + half + 1)
                heads = slice(8 * half, 8 * half + 8)
                nc.gpsimd.tensor_tensor(rms[:, j, heads], ms[:, j, heads], neghalf[:, 0:8], ALU.pow).then_inc(rms_ready, 1)

            scale_of(0)

            def turn(A, B, C, D, par):
                for u in range(STEPS):
                    if C is not None:
                        key, m0, n = unit(u)
                        wait_apart(pool, exp_ready, C * STEPS + u + 1, made)
                        pr = prob[:, u % RING].rearrange("p (m q) -> p m q", m=n)[:, :, 0:P]
                        nc.gpsimd.affine_select(out=pr, in_=pr, compare_op=ALU.is_ge, fill=0.0, base=0,
                                                pattern=[[0, n], [1, P]], channel_multiplier=-1).then_inc(prob_ready, 1)
                    if A is not None:
                        if u == 21:
                            scale_of(A + 1)
                        if u in (9, 11):
                            j = (u - 9) // 2
                            pool.wait_ge(qkv_ready, A * 2 + j + 1)
                            nc.gpsimd.tensor_tensor(by_cos[:, j], qk[:, j],
                                                    rope_cos[:, j].unsqueeze(1).broadcast_to([P, 2 * MAPS, HD]),
                                                    ALU.mult).then_inc(cos_ready, 1)
                    if B is not None and u == 4:
                        if D is not None:
                            wait_apart(pool, pv_done, (D + 1) * STEPS, made)
                        wait_apart(pool, qkv_ready, B * 2 + 2, made)
                        nc.gpsimd.tensor_copy(v[:, 1 - par, :, :, 0:HD].rearrange("p j h d -> p (j h) d"),
                                              v_new[:].rearrange("p j h d -> p (j h) d")).then_inc(v_ready, 1)
                    if D is not None and u in (7, 8):
                        rms_of(D, 1, u - 7)
                    if C is not None and u in (20, 22):
                        rms_of(C, 0, (u - 20) // 2)

            turns(pool, turn)

        @block.scalar
        def _(a):
            a.wait_ge(lam_summed, 1)
            nc.scalar.activation(lam_exp[:], lam_sum[:], ACT.Exp).then_inc(lam_exped, 1)
            a.wait_ge(packs_ready, 6)

            def turn(A, B, C, D, par):
                for u in range(STEPS):
                    if D is not None and u == 2:
                        a.wait_ge(pv_done, (D + 1) * STEPS)
                        a.wait_ge(o_in_psum, D * 2 + 1)
                        nc.scalar.activation(oT[:, 0], ot_ps[:, 0], ACT.Copy).then_inc(oT_copied, 1)
                    if C is not None:
                        a.wait_ge(st_ready, C * STEPS + u + 1)
                        if not (below(C, 1) and u < RING):
                            a.wait_ge(pv_done, C * STEPS + u + 1 - RING)
                        nc.scalar.activation(prob[:, u % RING], st_ps[:, u % 2], ACT.Exp, scale=SCALE).then_inc(exp_ready, 1)
                        if u == 1:
                            a.wait_ge(qmT_in_psum, C * 2 + 2)
                            nc.scalar.activation(qmT[:, par, :, 0:P], m16[1].rearrange("p (c q) -> p c q", q=P),
                                                 ACT.Copy).then_inc(qmT_ready, 1)
                        if u == 14:
                            a.wait_ge(pv_done, C * STEPS + HALF)
                            if not below(C, 1):
                                a.wait_ge(o_in_psum, C * 2)
                            nc.scalar.activation(oT[:, 0], ot_ps[:, 0], ACT.Copy).then_inc(oT_copied, 1)
                    if D is not None:
                        if u == 12:
                            a.wait_ge(onT_in_psum, D + 1)
                            nc.scalar.activation(onT[:], m_ps[:, 0, 0:S], ACT.Copy).then_inc(onT_ready, 1)
                    if A is not None:
                        if u == 3:
                            a.wait_ge(xT_in_psum, A + 1)
                            nc.scalar.activation(xT_hi[:], m_ps[:, 0, 0:S], ACT.Copy).then_inc(xT_hi_ready, 1)
                        if u == 14:
                            a.wait_ge(rot_ready, A + 1)
                            if C is not None:
                                a.wait_ge(qmT_in_psum, C * 2 + 2)
                            for j in range(2):
                                src = rot[:, j, 0:MAPS].unsqueeze(2).broadcast_to([P, MAPS, 2, HD])
                                dst = q_pack[:, par, j].rearrange("p m (r d) -> p m r d", d=2 * HD)[:, :, :, 0:HD]
                                nc.scalar.activation(dst, src, ACT.Copy).then_inc(pack_hi, 1)
                        if u == 15:
                            if not below(A, 1):
                                a.wait_ge(packT_in_psum, A * 4)
                            for j in range(2):
                                src = rot[:, j, MAPS:].unsqueeze(2).broadcast_to([P, MAPS, 2, HD])
                                dst = k_pack[:, j, :, 0:2 * HD].rearrange("p m (r d) -> p m r d", d=HD)
                                nc.scalar.activation(dst, src, ACT.Copy).then_inc(pack_hi, 1)
                        if u == 19:
                            a.wait_ge(packT_in_psum, A * 4 + 1)
                            if not below(A, 1):
                                for half in range(2):
                                    a.wait_ge(k_one_ready[half], A * 64)
                            nc.scalar.activation(kT[:, 0:4], m16[0].rearrange("p (c q) -> p c q", q=S),
                                                 ACT.Copy).then_inc(packT_ready, 1)
                        if u in (20, 21):
                            j = u - 20
                            a.wait_ge(packT_in_psum, A * 4 + 2 + j)
                            nc.scalar.activation(qT[:, par, :, j * P:(j + 1) * P], m16[1 - j].rearrange("p (c q) -> p c q", q=P),
                                                 ACT.Copy).then_inc(packT_ready, 1)
                    if B is not None and u == 22:
                        a.wait_ge(qmT_in_psum, B * 2 + 1)
                        nc.scalar.activation(qmT[:, 1 - par, :, P:], m16[1].rearrange("p (c q) -> p c q", q=P),
                                             ACT.Copy).then_inc(qmT_ready, 1)
                    if A is not None and u == 23:
                        a.wait_ge(packT_in_psum, A * 4 + 4)
                        nc.scalar.activation(kT[:, 4:8], m16[0].rearrange("p (c q) -> p c q", q=S),
                                             ACT.Copy).then_inc(packT_ready, 1)

            turns(a, turn)

        @block.vector
        def _(dve):
            once = Steps(dve, once_own, 0)
            once.begin(0)
            dve.wait_ge(loaded, 16 * LOADS)
            wqkv = by_cos[:].rearrange("p a b c -> p (a b c)")[:, 0:QKV]
            wo_in = on[:, 0].rearrange("p a b -> p (a b)")
            causal = osq[:, 0].rearrange("p a b -> p (a b)")
            once(nc.vector.tensor_tensor(lam_in[:, 0:2], lam_in[:, 0:2], lam_in[:, 2:4], ALU.mult))
            nc.vector.tensor_reduce(lam_sum[:], lam_in[:, 0:2], op=ALU.add, axis=AX.X).then_inc(lam_summed, 1)
            once(nc.vector.tensor_copy(wqkv_hi[:], wqkv))
            once(nc.vector.tensor_tensor(wqkv_lo[:], wqkv, wqkv_hi[:].bitcast(F32), ALU.subtract))
            once(nc.vector.tensor_scalar(wo[:], wo_in, head_w[:, 0:1], 1.0 - LAMBDA_INIT, ALU.mult, ALU.mult))
            once(nc.vector.tensor_copy(ident_bf[:], ident[:]))
            once(nc.vector.tensor_copy(ident_h[:], ident[:]))
            once(nc.vector.memset(branch[:, :, 0], 1.0))
            for i in range(4):
                once(nc.vector.tensor_copy(mask[:, i], causal))
            dve.wait_ge(lam_exped, 1)
            once(nc.vector.tensor_tensor(branch[:, :, 1], lam_exp[:, 1], lam_exp[:, 0], ALU.subtract))
            nc.vector.tensor_scalar(branch[:, :, 1], branch[:, :, 1], -LAMBDA_INIT, None, ALU.add).then_inc(prepared, 1)
            dve.wait_ge(prepared, 1)
            dve.wait_ge(packs_ready, 6)

            a_step = Steps(dve, a_own, 2)
            d_step = Steps(dve, d_own, 10)

            def statistics(b):
                a_step.begin(b)
                for j in range(2):
                    last = nc.vector.bn_stats(stats[:, j], x[:, b * 2 + j])
                a_step(last, made)
                for j in range(2):
                    last = nc.vector.bn_aggr(mv[:, j], stats[:, j])
                a_step(last)
                a_step.end()
                nc.vector.tensor_scalar(var[:], mv[:, :, 1], LN_EPS, None, ALU.add).then_inc(var_ready, 1)

            statistics(0)

            def maxima(B, u, par):
                dve.wait_ge(s_ready, B * STEPS + u + 1)
                j, m0, n = (1, 2 * u, 2) if u < 16 else (0, 4 * (u - 16), 4)
                nc.vector.tensor_reduce(q_pack[:, par, j, m0:m0 + n, 3 * HD], s_ps[:, u % 2].rearrange("p (m k) -> p m k", m=n),
                                        op=ALU.max, axis=AX.X, negate=True).then_inc(max_ready, 1)

            def weigh(b, half):
                d_step.begin(b)
                d_step.k = 5 * half
                dve.wait_ge(o_in_psum, b * 2 + half + 1)
                om = m_ps[:].rearrange("p j (m d) -> p j m d", d=PACK)
                d_step(nc.vector.reciprocal(inv[:], om[:, :, :, HD]))
                br = branch[:, 8 * half:8 * half + 8].rearrange("p h r -> p (h r)").unsqueeze(1).broadcast_to([P, 2, 16])
                d_step(nc.vector.tensor_tensor(inv[:], inv[:], br, ALU.mult))
                nc.vector.tensor_tensor(weighted[:, :, 16 * half:16 * half + 16], om[:, :, :, 0:HD],
                                        inv[:].unsqueeze(3).broadcast_to([P, 2, 16, HD]), ALU.mult).then_inc(o_weighted, 1)

            def combine(b, half):
                dve.wait_ge(o_weighted, b * 2 + half + 1)
                heads = slice(8 * half, 8 * half + 8)
                both = weighted[:, :, 16 * half:16 * half + 16].rearrange("p j (h r) d -> p j h r d", r=2)
                om, sq = o[:, :, heads], osq[:, :, heads]
                d_step(nc.vector.tensor_tensor(om, both[:, :, :, 0], both[:, :, :, 1], ALU.add))
                d_step(nc.vector.tensor_tensor(sq, om, om, ALU.mult))
                d_step(nc.vector.tensor_reduce(ms[:, :, heads], sq, op=ALU.add, axis=AX.X))
                nc.vector.tensor_scalar(ms[:, :, heads], ms[:, :, heads], 1.0 / HD, RMS_EPS, ALU.mult, ALU.add).then_inc(ms_ready, 1)

            def turn(A, B, C, D, par):
                for u in range(STEPS):
                    if B is not None:
                        maxima(B, u, 1 - par)
                    if A is not None:
                        if u == 20:
                            statistics(A + 1)
                        if u == 0:
                            dve.wait_ge(rstd_ready, A + 1)
                            for j in range(2):
                                last = nc.vector.tensor_scalar(xn[:, j], x[:, A * 2 + j], mv[:, j, 0:1], rstd[:, j:j + 1],
                                                               ALU.subtract, ALU.mult)
                            last.then_inc(xn_ready, 1)
                        if u == 3:
                            dve.wait_ge(xT_hi_ready, A + 1)
                            nc.vector.tensor_tensor(xT_lo[:], m_ps[:, 0, 0:S], xT_hi[:].bitcast(F32),
                                                    ALU.subtract).then_inc(xT_ready, 1)
                        if u in (8, 10):
                            j = (u - 8) // 2
                            dve.wait_ge(qkv_in_psum, A * 2 + j + 1)
                            if B is not None:
                                dve.wait_ge(v_ready, B + 1)
                            flat = qk[:, j].rearrange("p m d -> p (m d)")
                            nc.vector.tensor_tensor(flat[:, 0:W2], m_ps[:, 0, 0:W2], qkv_bias[:, 0:W2], ALU.add)
                            nc.vector.tensor_tensor(flat[:, W2:512], m_ps[:, 1, 0:512 - W2], qkv_bias[:, W2:512], ALU.add)
                            nc.vector.tensor_tensor(v_new[:, j].rearrange("p h d -> p (h d)"), m_ps[:, 1, 512 - W2:W2],
                                                    qkv_bias[:, 512:], ALU.add).then_inc(qkv_ready, 1)
                        if u == 11:
                            dve.wait_ge(qkv_ready, A * 2 + 2)
                            hf = HD // 2
                            for lo, hi in ((0, hf), (hf, 0)):
                                last = nc.vector.tensor_tensor(by_sin[:, :, :, lo:lo + hf], qk[:, :, :, hi:hi + hf],
                                                               rope_sin[:, :, lo:lo + hf].unsqueeze(2).broadcast_to([P, 2, 2 * MAPS, hf]),
                                                               ALU.mult)
                            last.then_inc(sin_ready, 1)
                        if u == 13:
                            dve.wait_ge(sin_ready, A + 1)
                            dve.wait_ge(cos_ready, A * 2 + 2)
                            flat = "p j m d -> p (j m d)"
                            nc.vector.tensor_tensor(rot[:].rearrange(flat), by_cos[:].rearrange(flat), by_sin[:].rearrange(flat),
                                                    ALU.add).then_inc(rot_ready, 1)
                        if u == 16:
                            dve.wait_ge(pack_hi, A * 4 + 4)
                            nc.vector.memset(q_pack[:, par, :, :, 3 * HD], 0.0)
                            for j in range(2):
                                nc.vector.tensor_tensor(q_pack[:, par, j, :, HD:2 * HD], rot[:, j, 0:MAPS],
                                                        q_pack[:, par, j, :, 0:HD], ALU.subtract)
                                last = nc.vector.tensor_tensor(k_pack[:, j, :, 2 * HD:3 * HD], rot[:, j, MAPS:],
                                                               k_pack[:, j, :, 0:HD], ALU.subtract)
                            last.then_inc(pack_lo, 1)
                    if (u == 2 and D is not None) or (u == 14 and C is not None):
                        dve.wait_ge(pv_done, (D + 1) * STEPS if u == 2 else C * STEPS + HALF)
                        if u == 2:
                            dve.wait_ge(o_in_psum, D * 2 + 1)
                        elif not below(C, 1):
                            dve.wait_ge(o_in_psum, C * 2)
                        nc.vector.tensor_copy(oT[:, 1], ot_ps[:, 1]).then_inc(oT_copied, 1)
                    if D is not None:
                        if u == 6:
                            weigh(D, 1)
                            combine(D, 1)
                            d_step.end()
                        if u == 10:
                            dve.wait_ge(rms_ready, D * 4 + 4)
                            nc.vector.tensor_tensor(on[:].rearrange("p j h d -> p (j h) d"), o[:].rearrange("p j h d -> p (j h) d"),
                                                    rms[:].rearrange("p j h -> p (j h)").unsqueeze(2).broadcast_to([P, 2 * HEADS, HD]),
                                                    ALU.mult).then_inc(on_ready, 1)
                        if u == 14:
                            dve.wait_ge(y_in_psum, D + 1)
                            xs = x[:, bass.ds(D * 2, 2)]
                            nc.vector.tensor_tensor(xs, xs, m_ps[:, 1, 0:S].rearrange("p (j d) -> p j d", d=P),
                                                    ALU.add).then_inc(x_added, 1)
                            dve.wait_ge(x_added, D * 2 + 1)
                            nc.vector.tensor_tensor(xs, xs, wo_bias[:].unsqueeze(1).broadcast_to([P, 2, P]),
                                                    ALU.add).then_inc(x_added, 1)
                    if C is not None and u == 17:
                        weigh(C, 0)
                    if C is not None and u == 18:
                        combine(C, 0)

            turns(dve, turn)
            dve.wait_ge(x_added, 2 * NB)

        @block.tensor
        def _(pe):
            pe.wait_ge(prepared, 1)

            def scores(B, u, par):
                if not (below(B, 1) and u < 2):
                    pe.wait_ge(max_ready, B * STEPS + u - 1)
                if u == 0:
                    pe.wait_ge(packT_ready, B * 4 + 3)
                    pe.wait_ge(k_one_ready[0], B * 64 + 64)
                if u == 8:
                    pe.wait_ge(k_one_ready[1], B * 64 + 64)
                out = s_ps[:, u % 2]
                j, m0, n = (1, 2 * u, 2) if u < 16 else (0, 4 * (u - 16), 4)
                if j:
                    nc.tensor.matmul(out.rearrange("p (m k) -> p m k", k=P)[:, 1::2], ident_bf[:], mask[:, 0:2], start=True, stop=False,
                                     skip_group_check=True)
                else:
                    nc.tensor.matmul(out, ident_bf[:], mask[:].rearrange("p a b -> p (a b)"), start=True, stop=False,
                                     skip_group_check=True)
                wd = 512 // n
                for i in range(n):
                    c, r = divmod(m0 + i, 4)
                    last = nc.tensor.matmul(out[:, i * wd:(i + 1) * wd], qT[:, par, c, j * P:(j + 1) * P],
                                            k_one[:, par, r, c, 0:wd], start=False, stop=True, skip_group_check=True)
                last.then_inc(s_ready, 1)

            def scores_T(C, u, par):
                if not (below(C, 1) and u < 2):
                    pe.wait_ge(exp_ready, C * STEPS + u - 1)
                if u == 0:
                    pe.wait_ge(qmT_ready, C * 2 + 1)
                if u == 4:
                    pe.wait_ge(qmT_ready, C * 2 + 2)
                key, m0, n = unit(u)
                wd = 512 // n
                for i in range(n):
                    c, r = divmod(m0 + i, 4)
                    q0 = P if key else 0
                    last = nc.tensor.matmul(st_ps[:, u % 2, i * wd:(i + 1) * wd], k_one[:, par, r, c, key * P:(key + 1) * P],
                                            qmT[:, par, c, q0:q0 + wd], start=True, stop=True)
                last.then_inc(st_ready, 1)

            def values(b, u, par):
                pe.wait_ge(prob_ready, b * STEPS + u + 1)
                if u == 0:
                    pe.wait_ge(v_ready, b + 1)
                    if not below(b, 1):
                        pe.wait_ge(oT_copied, b * 4)
                if u == HALF:
                    pe.wait_ge(oT_copied, b * 4 + 2)
                key, m0, n = unit(u)
                for part in ((1,) if key else (1, 0)):
                    for i in range(n):
                        c, r = divmod((m0 + i) % 16, 4)
                        col = (c % 2) * S + part * P
                        pr = prob[:, u % RING].rearrange("p (m q) -> p m q", m=n)
                        src = pr[:, i, 0:P] if key else pr[:, i, part * P:(part + 1) * P]
                        last = nc.tensor.matmul(ot_ps[32 * r:32 * r + 32, c // 2, col:col + P],
                                                v[:, par, key, (m0 + i) // 2], src,
                                                start=bool(key) and c % 2 == 0, stop=not key, skip_group_check=True)
                last.then_inc(pv_done, 1)

            def turn(A, B, C, D, par):
                for u in range(STEPS):
                    if B is not None:
                        scores(B, u, 1 - par)
                    if C is not None:
                        if u == 0:
                            pe.wait_ge(max_ready, (C + 1) * STEPS)
                            pe.wait_ge(qmT_ready, C * 2 + 1)
                            for c in range(CH):
                                last = nc.tensor.transpose(m16[1][:, c * P:(c + 1) * P],
                                                           q_pack[:, par, 0, 4 * c:4 * c + 4].rearrange("p m e -> p (m e)"), ident_h[:])
                            last.then_inc(qmT_in_psum, 1)
                        scores_T(C, u, par)
                    if u >= LAG and C is not None:
                        values(C, u - LAG, par)
                    if u < LAG and D is not None:
                        values(D, STEPS - LAG + u, 1 - par)
                    if u == 2 and A is not None:
                        pe.wait_ge(xn_ready, A + 1)
                        if not below(A, 1):
                            pe.wait_ge(packT_ready, A * 4)
                        for j in range(2):
                            last = nc.tensor.transpose(m_ps[:, 0, j * P:(j + 1) * P], xn[:, j], ident[:])
                        last.then_inc(xT_in_psum, 1)
                    if (u == 5 and D is not None) or (u == 16 and C is not None):
                        b, half = (D, 1) if u == 5 else (C, 0)
                        pe.wait_ge(oT_copied, (b * 2 + half + 1) * 2)
                        if u == 5:
                            if A is not None:
                                pe.wait_ge(xT_ready, A + 1)
                            if C is not None:
                                pe.wait_ge(qmT_ready, C * 2 + 2)
                            pe.wait_ge(o_weighted, D * 2 + 1)
                        else:
                            if D is not None:
                                pe.wait_ge(onT_ready, D + 1)
                                pe.wait_ge(x_added, D * 2 + 1)
                            elif A is not None:
                                pe.wait_ge(qkv_ready, A * 2 + 2)
                        for j in range(2):
                            for c in range(4):
                                last = nc.tensor.transpose(m_ps[:, j, c * P:(c + 1) * P],
                                                           oT[:, c // 2, (c % 2) * S + j * P:(c % 2) * S + (j + 1) * P], ident[:])
                        last.then_inc(o_in_psum, 1)
                    if u in (7, 9) and A is not None:
                        j = (u - 7) // 2
                        pe.wait_ge(xT_ready, A + 1)
                        if j == 1:
                            pe.wait_ge(qkv_ready, A * 2 + 1)
                        else:
                            if C is not None:
                                pe.wait_ge(qmT_ready, C * 2 + 2)
                            if D is not None:
                                pe.wait_ge(o_weighted, D * 2 + 2)
                        for part in range(2):
                            for i, (xt, wt) in enumerate(((xT_hi, wqkv_hi), (xT_hi, wqkv_lo), (xT_lo, wqkv_hi))):
                                last = nc.tensor.matmul(m_ps[:, part, 0:W2], xt[:, j * P:(j + 1) * P],
                                                        wt[:, part * W2:(part + 1) * W2], start=(i == 0), stop=(i == 2))
                        last.then_inc(qkv_in_psum, 1)
                    if u == 11 and D is not None:
                        pe.wait_ge(on_ready, D + 1)
                        if A is not None:
                            pe.wait_ge(qkv_ready, A * 2 + 2)
                        for j in range(2):
                            last = nc.tensor.transpose(m_ps[:, 0, j * P:(j + 1) * P], on[:, j].rearrange("p h d -> p (h d)"), ident[:])
                        last.then_inc(onT_in_psum, 1)
                    if u == 13 and D is not None:
                        pe.wait_ge(onT_ready, D + 1)
                        for j in range(2):
                            last = nc.tensor.matmul(m_ps[:, 1, j * P:(j + 1) * P], onT[:, j * P:(j + 1) * P], wo[:], start=True, stop=True)
                        last.then_inc(y_in_psum, 1)
                    if A is not None and u in (18, 22):
                        h4 = 0 if u == 18 else 4
                        if u == 18:
                            pe.wait_ge(pack_lo, A + 1)
                            if C is not None:
                                pe.wait_ge(o_weighted, C * 2 + 1)
                        else:
                            pe.wait_ge(packT_ready, A * 4 + 3)
                        for c in range(4):
                            for j in range(2):
                                last = nc.tensor.transpose(m16[0][:, c * S + j * P:c * S + (j + 1) * P],
                                                           k_pack[:, j, 4 * (h4 + c):4 * (h4 + c) + 4].rearrange("p m e -> p (m e)"), ident_h[:])
                        last.then_inc(packT_in_psum, 1)
                    if A is not None and u in (19, 20):
                        j = u - 19
                        if j == 1:
                            pe.wait_ge(packT_ready, A * 4 + 1)
                        for c in range(CH):
                            last = nc.tensor.transpose(m16[1 - j][:, c * P:(c + 1) * P],
                                                       q_pack[:, par, j, 4 * c:4 * c + 4].rearrange("p m e -> p (m e)"), ident_h[:])
                        last.then_inc(packT_in_psum, 1)
                    if B is not None and u == 21:
                        pe.wait_ge(max_ready, B * STEPS + 16)
                        if A is not None:
                            pe.wait_ge(packT_ready, A * 4 + 2)
                        elif C is not None:
                            pe.wait_ge(o_weighted, C * 2 + 1)
                        for c in range(CH):
                            last = nc.tensor.transpose(m16[1][:, c * P:(c + 1) * P],
                                                       q_pack[:, 1 - par, 1, 4 * c:4 * c + 4].rearrange("p m e -> p (m e)"), ident_h[:])
                        last.then_inc(qmT_in_psum, 1)

            turns(pe, turn)


def linear_attention(nc, tag, x, ident, neghalf, made, w):
    NF = w["wv_f"].shape[0]
    CS = w["cs_w1T"].shape[1]
    NG = x.shape[1] // TG - 1
    S = 2 * P
    RING = 4
    LAG = 3
    DECAY_MAX = 0.9995
    with ExitStack() as ctx:
        nm = Names(nc, ctx, tag)
        w_in = nm.sb("w_in", [P, 2 + NF, P], F32)
        w_hi = nm.sb("w_hi", [P, 2 + NF, P], F32R)
        w_lo = nm.sb("w_lo", [P, 2 + NF, P], F32R)
        c_in = nm.sb("c_in", [P, CS], F32)
        c_hi = nm.sb("c_hi", [P, CS], F32R)
        c_lo = nm.sb("c_lo", [P, CS], F32R)
        wo = nm.sb("wo", [P, NF, P], F32)
        cs2 = nm.sb("cs2", [CS, P], F32)
        b1 = nm.sb("b1", [CS, 1], F32)
        rows = nm.sb("rows", [P, 2], F32)
        half_b2 = nm.sb("half_b2", [P, 1], F32)
        tbase = nm.sb("tbase", [P, 1], F32)
        lam_scale = nm.sb("lam_scale", [P, 1], F32)
        lam_shift = nm.sb("lam_shift", [P, 1], F32)

        stats = nm.sb("stats", [P, TG, 6], F32)
        mv = nm.sb("mv", [P, TG, 2], F32)
        var = nm.sb("var", [P, TG], F32)
        rstd = nm.sb("rstd", [P, TG], F32)
        xn = nm.sb("xn", [P, TG, P], F32)
        xT_hi = nm.sb("xT_hi", [P, 2, GN], F32R)
        xT_lo = nm.sb("xT_lo", [P, 2, GN], F32R)
        hid = nm.sb("hid", [CS, GN], F32)
        th = nm.sb("th", [P, GN], F32)
        lam = nm.sb("lam", [P, 2, GN], F32)
        kT = nm.sb("kT", [P, 2, GN], F32)
        qT = nm.sb("qT", [P, 2, GN], F32)
        kv = nm.sb("kv", [P, 2, GN], F32)
        state = nm.sb("state", [P, 2, GN], F32)
        y = nm.sb("y", [P, RING, GN], F32)

        t_ps = nm.ps("t_ps", [P, GN], F32)
        c_ps = nm.ps("c_ps", [P, GN], F32)
        kq_ps = nm.ps("kq_ps", [P, GN], F32)
        v_ps = nm.ps("v_ps", [P, 2, GN], F32)
        o_ps = nm.ps("o_ps", [P, 2, GN], F32)

        loaded = nm.sem("loaded")
        base_ready = nm.sem("base_ready")
        prepared = nm.sem("prepared")
        once_own = nm.sem("once_own")
        own = nm.sem("own")
        kv_own = nm.sem("kv_own")
        var_ready = nm.sem("var_ready")
        rstd_ready = nm.sem("rstd_ready")
        xn_ready = nm.sem("xn_ready")
        xT_in_psum = nm.sem("xT_in_psum")
        xT_hi_ready = nm.sem("xT_hi_ready")
        xT_ready = nm.sem("xT_ready")
        hid_in_psum = nm.sem("hid_in_psum")
        hid_ready = nm.sem("hid_ready")
        lc_in_psum = nm.sem("lc_in_psum")
        th_ready = nm.sem("th_ready")
        lam_ready = nm.sem("lam_ready")
        kq_in_psum = nm.sem("kq_in_psum")
        kq_ready = nm.sem("kq_ready")
        v_ready = nm.sem("v_ready")
        state_ready = nm.sem("state_ready")
        y_ready = nm.sem("y_ready")
        y_used = nm.sem("y_used")
        x_added = nm.sem("x_added")
        block = ctx.enter_context(nc.Block())

        def pairs(engine, group):
            group(0, 0, True, True)
            group(1, 1, False, True)
            with engine.Fori(1, NG // 2 - 1) as i:
                group(i * 2, 0, False, True)
                group(i * 2 + 1, 1, False, True)
            group(NG - 2, 0, False, True)
            group(NG - 1, 1, False, False)

        def early(g, n):
            return isinstance(g, int) and g < n

        @block.sync
        def _(sp):
            sp.dma_start(w_in[:, 0:2], w["wkq"]).then_inc(loaded, 16)
            sp.dma_start(c_in[:], w["cs_w1T"]).then_inc(loaded, 16)
            sp.dma_start(cs2[:], w["cs_w2T"]).then_inc(loaded, 16)
            sp.dma_start(b1[:], w["cs_b1"]).then_inc(loaded, 16)
            sp.dma_start(rows[:], w["rows"]).then_inc(loaded, 16)
            sp.dma_start(w_in[:, 2:], w["wv_f"].rearrange("f p n -> p f n")).then_inc(loaded, 16)
            sp.dma_start(wo[:], w["wo_f"].rearrange("f p n -> p f n")).then_inc(loaded, 16)

        LOADS = 7

        @block.gpsimd
        def _(pool):
            def scale_of(g):
                pool.wait_ge(var_ready, g + 1)
                nc.gpsimd.tensor_tensor(rstd[:], var[:], neghalf[:, 0:TG], ALU.pow).then_inc(rstd_ready, 1)

            scale_of(0)

            def group(g, b, is_first, prepares):
                for f in range(NF):
                    n = g * NF + f
                    pool.wait_ge(state_ready, n + 1)
                    if not (is_first and f < RING):
                        pool.wait_ge(y_used, n + 1 - RING)
                    nc.gpsimd.tensor_tensor(y[:, f % RING], state[:, f % 2], qT[:, b], ALU.mult).then_inc(y_ready, 1)
                    if f == 0 and prepares:
                        scale_of(g + 1)

            pairs(pool, group)

        @block.scalar
        def _(a):
            a.wait_ge(loaded, 16 * LOADS)
            nc.scalar.activation(tbase[:], rows[:, 1:2], ACT.Tanh, scale=0.5).then_inc(base_ready, 1)
            a.wait_ge(prepared, 1)

            def high(g, b):
                a.wait_ge(xT_in_psum, g + 1)
                nc.scalar.activation(xT_hi[:, b], t_ps[:], ACT.Copy).then_inc(xT_hi_ready, 1)

            def hidden(g):
                a.wait_ge(hid_in_psum, g + 1)
                nc.scalar.activation(hid[:], c_ps[0:CS], ACT.Tanh, bias=b1[:, 0:1]).then_inc(hid_ready, 1)

            def decay(g):
                a.wait_ge(lc_in_psum, g + 1)
                nc.scalar.activation(th[:], c_ps[:], ACT.Tanh, bias=half_b2[:, 0:1], scale=0.5).then_inc(th_ready, 1)

            def copy_kq(g, b, which):
                a.wait_ge(kq_in_psum, g * 2 + which + 1)
                nc.scalar.activation((kT, qT)[which][:, b], kq_ps[:], ACT.Copy).then_inc(kq_ready, 1)

            high(0, 0)
            hidden(0)
            copy_kq(0, 0, 0)
            decay(0)
            copy_kq(0, 0, 1)

            def group(g, b, is_first, prepares):
                if prepares:
                    high(g + 1, 1 - b)
                    hidden(g + 1)
                    if not early(g, 1):
                        a.wait_ge(y_ready, g * NF)
                    copy_kq(g + 1, 1 - b, 0)
                    decay(g + 1)
                    copy_kq(g + 1, 1 - b, 1)

            pairs(a, group)

        @block.vector
        def _(dve):
            once = Steps(dve, once_own, 0)
            once.begin(0)
            step = Steps(dve, own, 3)

            def statistics(g):
                step.begin(g)
                for t in range(TG):
                    last = nc.vector.bn_stats(stats[:, t], x[:, g * TG + t])
                step(last, made)
                for t in range(TG):
                    last = nc.vector.bn_aggr(mv[:, t], stats[:, t])
                step(last)
                nc.vector.tensor_scalar(var[:], mv[:, :, 1], LN_EPS, None, ALU.add).then_inc(var_ready, 1)

            def normalise(g):
                dve.wait_ge(rstd_ready, g + 1)
                for t in range(TG):
                    last = nc.vector.tensor_scalar(xn[:, t], x[:, g * TG + t], mv[:, t, 0:1], rstd[:, t:t + 1],
                                                   ALU.subtract, ALU.mult)
                last.then_inc(xn_ready, 1)

            def low(g, b):
                dve.wait_ge(xT_hi_ready, g + 1)
                nc.vector.tensor_tensor(xT_lo[:, b], t_ps[:], xT_hi[:, b].bitcast(F32), ALU.subtract).then_inc(xT_ready, 1)

            def make_lam(g, b):
                dve.wait_ge(th_ready, g + 1)
                step(nc.vector.tensor_scalar(lam[:, b], th[:], lam_scale[:, 0:1], lam_shift[:, 0:1], ALU.mult, ALU.add))
                nc.vector.tensor_scalar(lam[:, b], lam[:, b], 0.0, DECAY_MAX, ALU.max, ALU.min).then_inc(lam_ready, 1)
                step.end()

            statistics(0)
            normalise(0)
            dve.wait_ge(loaded, 16 * LOADS)
            once(nc.vector.memset(state[:], 0.0))
            once(nc.vector.tensor_copy(w_hi[:], w_in[:]))
            once(nc.vector.tensor_tensor(w_lo[:], w_in[:], w_hi[:].bitcast(F32), ALU.subtract))
            once(nc.vector.tensor_copy(c_hi[:], c_in[:]))
            once(nc.vector.tensor_tensor(c_lo[:], c_in[:], c_hi[:].bitcast(F32), ALU.subtract))
            dve.wait_ge(base_ready, 1)
            once(nc.vector.tensor_scalar(tbase[:], tbase[:], 0.5, 0.5, ALU.mult, ALU.add))
            once(nc.vector.tensor_scalar(lam_scale[:], tbase[:], 0.1, None, ALU.mult))
            once(nc.vector.tensor_scalar(lam_shift[:], tbase[:], 1.1, None, ALU.mult))
            nc.vector.tensor_scalar(half_b2[:], rows[:, 0:1], 0.5, None, ALU.mult).then_inc(prepared, 1)
            low(0, 0)
            make_lam(0, 0)

            def outer(g, b, f):
                n = g * NF + f
                if f == 0:
                    dve.wait_ge(kq_ready, g * 2 + 1)
                dve.wait_ge(v_ready, n + 1)
                if not (early(g, 1) and f < 2):
                    dve.wait_ge(state_ready, n - 1)
                nc.vector.tensor_tensor(kv[:, f % 2], v_ps[:, f % 2], kT[:, b], ALU.mult).then_inc(kv_own, 1)

            def scan(g, b, f):
                n = g * NF + f
                if f == 0:
                    dve.wait_ge(lam_ready, g + 1)
                    dve.wait_ge(kq_ready, g * 2 + 2)
                dve.wait_ge(kv_own, n + 1)
                if not (early(g, 1) and f < 2):
                    dve.wait_ge(y_ready, n - 1)
                for s in range(GN // S):
                    cols = slice(s * S, (s + 1) * S)
                    last = nc.vector.tensor_tensor_scan(state[:, f % 2, cols], lam[:, b, cols], kv[:, f % 2, cols],
                                                        0.0, ALU.mult, ALU.add)
                last.then_inc(state_ready, 1)

            def add_out(g, b):
                dve.wait_ge(y_used, (g + 1) * NF)
                xs = x[:, bass.ds(g * TG, TG)].rearrange("p t d -> p (t d)")
                nc.vector.tensor_tensor(xs, xs, o_ps[:, b], ALU.add).then_inc(x_added, 1)

            def group(g, b, is_first, prepares):
                for f in range(NF):
                    outer(g, b, f)
                    if f >= 1:
                        scan(g, b, f - 1)
                    if prepares:
                        if f == 0:
                            statistics(g + 1)
                        if f == 1:
                            normalise(g + 1)
                        if f == 3:
                            low(g + 1, 1 - b)
                        if f == 7:
                            make_lam(g + 1, 1 - b)
                    if f == 5 and not is_first:
                        add_out(g - 1, 1 - b)
                scan(g, b, NF - 1)

            pairs(dve, group)
            add_out(NG - 1, 1)
            dve.wait_ge(x_added, NG)

        @block.tensor
        def _(pe):
            def transpose_x(g):
                pe.wait_ge(xn_ready, g + 1)
                for t in range(TG):
                    last = nc.tensor.transpose(t_ps[:, t * P:(t + 1) * P], xn[:, t], ident[:])
                last.then_inc(xT_in_psum, 1)

            def three(out, hi, lo, b):
                for i, (wt, xt) in enumerate(((hi, xT_hi), (hi, xT_lo), (lo, xT_hi))):
                    last = nc.tensor.matmul(out, wt, xt[:, b], start=(i == 0), stop=(i == 2))
                return last

            def hidden(g, b):
                pe.wait_ge(xT_ready, g + 1)
                if not early(g, 1):
                    pe.wait_ge(th_ready, g)
                three(c_ps[0:CS], c_hi[:], c_lo[:], b).then_inc(hid_in_psum, 1)

            def project(g, b, which):
                if not (early(g, 1) and which == 0):
                    pe.wait_ge(kq_ready, g * 2 + which)
                three(kq_ps[:], w_hi[:, which], w_lo[:, which], b).then_inc(kq_in_psum, 1)

            def decay(g):
                pe.wait_ge(hid_ready, g + 1)
                nc.tensor.matmul(c_ps[:], cs2[:], hid[:], start=True, stop=True).then_inc(lc_in_psum, 1)

            def project_v(g, b, f):
                if not (early(g, 1) and f < 2):
                    pe.wait_ge(kv_own, g * NF + f - 1)
                three(v_ps[:, f % 2], w_hi[:, 2 + f], w_lo[:, 2 + f], b).then_inc(v_ready, 1)

            def output(g, b, f):
                pe.wait_ge(y_ready, g * NF + f + 1)
                if f == 0 and not early(g, 2):
                    pe.wait_ge(x_added, g - 1)
                for t in range(TG):
                    last = nc.tensor.matmul(o_ps[:, b, t * P:(t + 1) * P], y[:, f % RING, t * P:(t + 1) * P], wo[:, f],
                                            start=(f == 0 and t == 0), stop=(f == NF - 1), skip_group_check=True)
                last.then_inc(y_used, 1)

            transpose_x(0)
            pe.wait_ge(prepared, 1)
            hidden(0, 0)
            project(0, 0, 0)
            decay(0)
            project(0, 0, 1)

            def group(g, b, is_first, prepares):
                for f in range(NF):
                    project_v(g, b, f)
                    if prepares:
                        if f == 2:
                            transpose_x(g + 1)
                        if f == 4:
                            hidden(g + 1, 1 - b)
                            project(g + 1, 1 - b, 0)
                        if f == 5:
                            decay(g + 1)
                        if f == 6:
                            project(g + 1, 1 - b, 1)
                    if f >= LAG:
                        output(g, b, f - LAG)
                    elif not is_first:
                        output(g - 1, 1 - b, NF - LAG + f)

            pairs(pe, group)
            for f in range(NF - LAG, NF):
                output(NG - 1, 1, f)


def build(nc, phases, x_d, const, ins, out_d):
    T = x_d.shape[0] * x_d.shape[1] // P
    with ExitStack() as ctx:
        nm = Names(nc, ctx, "all")
        x = nm.sb("x", [P, T + TG, P], F32)
        ident = nm.sb("ident", [P, P], F32)
        neghalf = nm.sb("neghalf", [P, 64], F32)
        loaded = nm.sem("loaded")
        stored = nm.sem("stored")
        made = nm.sem("made")
        x_tiles = x_d.rearrange("b (t p) d -> p (b t) d", p=P)
        out_tiles = out_d.rearrange("b (t p) d -> p (b t) d", p=P)
        with nc.Block() as block:
            @block.sync
            def _(sp):
                sp.dma_start(ident[:], const["ident"]).then_inc(loaded, 16)
                for q in range(4):
                    sp.dma_start(x[:, q * T // 4:(q + 1) * T // 4], x_tiles[:, q * T // 4:(q + 1) * T // 4]).then_inc(loaded, 16)
                sp.wait_ge(loaded, 16 * 5)

            @block.vector
            def _(dve):
                nc.vector.memset(neghalf[:], -0.5)
                nc.vector.memset(x[:, T:], 0.0).then_inc(made, 1)
                dve.wait_ge(made, 1)
        if "a" in phases:
            moe_ffn(nc, "moe0", x, ident, neghalf, made, ins)
        if "b" in phases:
            diff_attention(nc, "diff", x, ident, neghalf, made, ins)
        if "c" in phases:
            moe_ffn(nc, "moe1", x, ident, neghalf, made, ins)
        if "d" in phases or "f" in phases:
            dequantized = dequantized_weights(nc, ctx, ins)
        if "d" in phases:
            quantized_ffn(nc, "ffn0", x, ident, neghalf, made, dequantized)
        if "e" in phases:
            linear_attention(nc, "lin", x, ident, neghalf, made, ins)
        if "f" in phases:
            quantized_ffn(nc, "ffn1", x, ident, neghalf, made, dequantized)
        with nc.Block() as block:
            @block.sync
            def _(sp):
                sp.dma_start(out_tiles, x[:, 0:T]).then_inc(stored, 16)
                sp.wait_ge(stored, 16)


_NAMES = ['L0_attn_x', 'L0_attn_Wq', 'L0_attn_bq', 'L0_attn_Wk', 'L0_attn_bk', 'L0_attn_Wv', 'L0_attn_bv', 'L0_attn_Wo', 'L0_attn_bo', 'L0_attn_head_norm_w', 'L0_attn_lq1', 'L0_attn_lk1', 'L0_attn_lq2', 'L0_attn_lk2', 'L0_ffn_router_w', 'L0_ffn_experts_bias', 'L0_ffn_w1', 'L0_ffn_w3', 'L0_ffn_w2', 'L0_ffn_sw1', 'L0_ffn_sw3', 'L0_ffn_sw2', 'L1_attn_q_w', 'L1_attn_k_w', 'L1_attn_v_w', 'L1_attn_o_w', 'L1_attn_cs_w1', 'L1_attn_cs_b1', 'L1_attn_cs_w2', 'L1_attn_cs_b2', 'L1_attn_decay_params', 'L1_ffn_ln_gamma', 'L1_ffn_ln_beta', 'L1_ffn_fc1_q', 'L1_ffn_fc1_scales', 'L1_ffn_fc1_bias', 'L1_ffn_fc2_q', 'L1_ffn_fc2_scales', 'L1_ffn_fc2_bias']


def layout(inputs):
    d = {}
    a = {k: np.asarray(v) for k, v in inputs.items()}
    d["x"] = a["L0_attn_x"]
    d["ident"] = np.eye(P, dtype=np.float32)
    d["router_T"] = a["L0_ffn_router_w"].T
    d["router_bias"] = a["L0_ffn_experts_bias"].reshape(-1, 1)
    d["wqkv"] = np.concatenate([a["L0_attn_Wq"], a["L0_attn_Wk"], a["L0_attn_Wv"]], axis=0).T
    d["qkv_bias"] = np.concatenate([a["L0_attn_bq"], a["L0_attn_bk"], a["L0_attn_bv"]]).reshape(1, -1)
    d["wo_T"] = a["L0_attn_Wo"].T
    d["wo_bias"] = a["L0_attn_bo"].reshape(1, -1)
    d["head_w"] = a["L0_attn_head_norm_w"].reshape(-1, 1)
    d["lam"] = np.stack([a["L0_attn_lq1"], a["L0_attn_lq2"], a["L0_attn_lk1"], a["L0_attn_lk2"]])
    half = a["L0_attn_head_norm_w"].shape[1] // 2
    freq = (1.0 / np.float32(10000.0) ** (np.arange(half, dtype=np.float32) / np.float32(half))).astype(np.float32)
    angle = np.arange(2 * P, dtype=np.float32)[:, None] * freq[None]
    cos, sin = np.cos(angle), np.sin(angle)
    d["rope_cos"] = np.concatenate([cos, cos], axis=1).reshape(2, P, -1).transpose(1, 0, 2)
    d["rope_sin"] = np.concatenate([-sin, sin], axis=1).reshape(2, P, -1).transpose(1, 0, 2)
    d["causal"] = np.triu(np.full((P, P), -1e30, np.float32), 1)
    H1, E1 = a["L1_attn_decay_params"].shape
    d["wkq"] = np.stack([a["L1_attn_k_w"].T, a["L1_attn_q_w"].T], axis=1)
    d["wv_f"] = np.repeat(a["L1_attn_v_w"].reshape(H1, E1, P).transpose(1, 2, 0), E1, axis=2)
    d["wo_f"] = np.repeat(a["L1_attn_o_w"].reshape(P, H1, E1).transpose(2, 1, 0), E1, axis=1)
    d["cs_w1T"] = a["L1_attn_cs_w1"].T
    d["cs_w2T"] = np.repeat(a["L1_attn_cs_w2"].T, E1, axis=1)
    d["cs_b1"] = a["L1_attn_cs_b1"].reshape(-1, 1)
    d["rows"] = np.stack([np.repeat(a["L1_attn_cs_b2"], E1), a["L1_attn_decay_params"].reshape(-1)], axis=1)
    for k in ("fc1_q", "fc1_scales", "fc2_q", "fc2_scales"):
        d[k] = a["L1_ffn_" + k]
    chunks = a["L1_ffn_fc1_bias"].reshape(-1, P)
    d["ffn1_cols"] = np.stack([a["L1_ffn_ln_gamma"], a["L1_ffn_ln_beta"], *chunks], axis=1)
    d["fc2_bias"] = a["L1_ffn_fc2_bias"].reshape(1, -1)
    for k in ("w1", "w3", "w2", "sw1", "sw3", "sw2"):
        d[k] = a["L0_ffn_" + k]
    return {k: np.ascontiguousarray(v) for k, v in d.items()}


def program(nc, arrays, phases="abcdef"):
    ins = {k: nc.dram_tensor(f"in_{k}", v.shape, mybir.dt.from_np(v.dtype), kind="ExternalInput").ap()
           for k, v in arrays.items()}
    out = nc.dram_tensor("out_0", arrays["x"].shape, F32, kind="ExternalOutput").ap()
    build(nc, phases, ins["x"], ins, ins, out)


def kernel(**inputs):
    import concourse.bacc as bacc
    from concourse.bass_utils import run_bass_kernel_spmd

    arrays = layout(inputs)
    nc = bacc.Bacc("TRN2", target_bir_lowering=False, num_devices=1)
    program(nc, arrays)
    r = run_bass_kernel_spmd(nc, [{f"in_{k}": v for k, v in arrays.items()}], core_ids=[0])
    return r.results[0]["out_0"]
```

```python
from contextlib import ExitStack

import numpy as np
import concourse.bass as bass
from concourse import mybir

F32 = mybir.dt.float32
F32R = mybir.dt.float32r
F16 = mybir.dt.float16
BF16 = mybir.dt.bfloat16
I32 = mybir.dt.int32
ALU = mybir.AluOpType
ACT = mybir.ActivationFunctionType
AX = mybir.AxisListType

P = 128
TG = 4
GN = TG * P
LN_EPS = 1e-5
LOADS_OF_X = 5
LAMBDA_INIT = 0.8 - 0.6


class Names:

    def __init__(self, nc, ctx, prefix):
        self.nc, self.ctx, self.prefix = nc, ctx, prefix
        self.sems = []
        ctx.callback(self.clear)

    def clear(self):
        self.nc.clear_and_free_semaphores(self.sems)
        self.nc.all_engine_barrier()

    def sem(self, name):
        sem = self.nc.alloc_semaphore(f"{self.prefix}_{name}")
        self.sems.append(sem)
        return sem

    def sb(self, name, shape, dt):
        return self.ctx.enter_context(self.nc.sbuf_tensor(f"{self.prefix}_{name}", shape, dt))

    def ps(self, name, shape, dt):
        return self.ctx.enter_context(self.nc.psum_tensor(f"{self.prefix}_{name}", shape, dt))


def wait_apart(engine, sem, value, made):
    if not isinstance(value, int):
        value = engine.compute_val(value)
        engine.wait_ge(made, 1)
    engine.wait_ge(sem, value)


class Steps:

    def __init__(self, engine, sem, per_round):
        self.engine, self.sem, self.per_round = engine, sem, per_round

    def begin(self, g):
        self.g, self.k = g, 0

    def __call__(self, instruction, apart=None):
        instruction.then_inc(self.sem, 1)
        self.k += 1
        value = self.g * self.per_round + self.k
        if apart is None:
            self.engine.wait_ge(self.sem, value)
        else:
            wait_apart(self.engine, self.sem, value, apart)

    def end(self):
        assert self.k == self.per_round, self.k


def moe_ffn(nc, tag, x, ident, neghalf, made, w, x_loaded=None, later=None):
    E = w["router_T"].shape[1]
    NE = E + 1
    H = w["w1"].shape[2]
    NC = H // P
    NG = x.shape[1] // TG - 1

    LAG = 2
    HB = 3
    assert NE % HB == 0

    with ExitStack() as ctx:
        nm = Names(nc, ctx, tag)
        up = nm.sb("up", [P, NE, 2, H], F32)
        up_hi = nm.sb("up_hi", [P, NE, 2, H], F32R)
        up_lo = nm.sb("up_lo", [P, NE, 2, H], F32R)
        down = nm.sb("down", [P, NE, NC, P], F32)
        down_hi = nm.sb("down_hi", [P, NE, NC, P], F16)
        down_lo = nm.sb("down_lo", [P, NE, NC, P], F16)
        router = nm.sb("router", [P, E], F32)
        router_hi = nm.sb("router_hi", [P, E], F32R)
        router_lo = nm.sb("router_lo", [P, E], F32R)
        rbias = nm.sb("rbias", [E, 1], F32)
        earlier = nm.sb("earlier", [P, E, E], F32)
        xT_hi = nm.sb("xT_hi", [P, NG, GN], F32R)
        xT_lo = nm.sb("xT_lo", [P, NG, GN], F32R)
        gate = nm.sb("gate", [P, NG, TG, E], F32)
        stats = nm.sb("stats", [P, TG, 6], F32)
        mv = nm.sb("mv", [P, TG, 2], F32)
        var = nm.sb("var", [P, TG], F32)
        rstd = nm.sb("rstd", [P, TG], F32)
        xn = nm.sb("xn", [P, TG, P], F32)
        logT = nm.sb("logT", [E, GN], F32)
        logits = nm.sb("logits", [P, TG, E], F32)
        above = nm.sb("above", [P, TG, E, E], F32)
        equal = nm.sb("equal", [P, TG, E, E], F32)
        rank = nm.sb("rank", [P, TG, E], F32)
        first = nm.sb("first", [P, TG, E], F32)
        second = nm.sb("second", [P, TG, E], F32)
        either = nm.sb("either", [P, TG, E], F32)
        signed = nm.sb("signed", [P, TG, E], F32)
        prod = nm.sb("prod", [P, TG, E], F32)
        gap = nm.sb("gap", [P, TG], F32)
        tgap = nm.sb("tgap", [P, TG], F32)
        mix = nm.sb("mix", [P, TG, E], F32)
        act = nm.sb("act", [P, NC, GN], F32)
        h = nm.sb("h", [P, NC, GN], F32)
        h_hi = nm.sb("h_hi", [P, HB, NC, GN], F16)
        h_lo = nm.sb("h_lo", [P, HB, NC, GN], F16)

        g_ps = nm.ps("g_ps", [P, NC, GN], F32)
        u_ps = nm.ps("u_ps", [P, NC, GN], F32)
        o_ps = nm.ps("o_ps", [P, 2, GN], F32)
        t_ps = nm.ps("t_ps", [P, GN], F32)
        r_ps = nm.ps("r_ps", [P, GN], F32)

        up_in = [nm.sem(f"up_in{e}") for e in range(NE)]
        down_in = nm.sem("down_in")
        router_in = nm.sem("router_in")
        up_hi_done = nm.sem("up_hi_done")
        up_split = nm.sem("up_split")
        down_hi_done = nm.sem("down_hi_done")
        down_split = nm.sem("down_split")
        router_split = nm.sem("router_split")
        consts = nm.sem("consts")
        dve_own = nm.sem("dve_own")
        dve_once = nm.sem("dve_once")
        var_ready = nm.sem("var_ready")
        rstd_ready = nm.sem("rstd_ready")
        xn_ready = nm.sem("xn_ready")
        xT_in_psum = nm.sem("xT_in_psum")
        xT_hi_ready = nm.sem("xT_hi_ready")
        xT_ready = nm.sem("xT_ready")
        logT_in_psum = nm.sem("logT_in_psum")
        logT_ready = nm.sem("logT_ready")
        logits_in_psum = nm.sem("logits_in_psum")
        gap_ready = nm.sem("gap_ready")
        tgap_ready = nm.sem("tgap_ready")
        g_ready = nm.sem("g_ready")
        u_ready = nm.sem("u_ready")
        act_ready = nm.sem("act_ready")
        h_ready = nm.sem("h_ready")
        h_hi_ready = nm.sem("h_hi_ready")
        h_lo_ready = nm.sem("h_lo_ready")
        down_done = nm.sem("down_done")
        added = nm.sem("added")
        block = ctx.enter_context(nc.Block())

        def groups(engine, group):
            group(0, True, True)
            with engine.Fori(1, NG - 1) as g:
                group(g, False, True)
            group(NG - 1, False, False)

        @block.sync
        def _(sp):
            for e in range(NE):
                w1, w3 = (w["sw1"][0], w["sw3"][0]) if e == E else (w["w1"][e], w["w3"][e])
                sp.dma_start(up[:, e, 0, :], w1).then_inc(up_in[e], 16)
                sp.dma_start(up[:, e, 1, :], w3).then_inc(up_in[e], 16)
                if e == 0:
                    sp.dma_start(router[:, :], w["router_T"]).then_inc(router_in, 16)
                    sp.dma_start(rbias[:, :], w["router_bias"]).then_inc(router_in, 16)
            sp.dma_start(down[:, 0:E, :, :], w["w2"].rearrange("e (c p) d -> p e c d", p=P)).then_inc(down_in, 16)
            sp.dma_start(down[:, E, :, :], w["sw2"][0].rearrange("(c p) d -> p c d", p=P)).then_inc(down_in, 16)
            if later:
                later.load(sp)

        @block.gpsimd
        def _(pool):
            def rstd_of(g):
                pool.wait_ge(var_ready, g + 1)
                nc.gpsimd.tensor_tensor(rstd[:, :], var[:, :], neghalf[:, 0:TG], ALU.pow).then_inc(rstd_ready, 1)

            rstd_of(0)
            for e in range(NE):
                pool.wait_ge(up_hi_done, e + 1)
                nc.gpsimd.tensor_tensor(up_lo[:, e], up[:, e], up_hi[:, e].bitcast(F32), ALU.subtract).then_inc(up_split, 1)

            def group(g, is_first, prepares):
                for e in range(NE):
                    for c in range(NC):
                        k = NC * e + c
                        pool.wait_ge(h_hi_ready, g * (NC * NE) + k + 1)
                        if not (is_first and e < HB):
                            pool.wait_ge(down_done, g * NE + e + 1 - HB)
                        nc.gpsimd.tensor_tensor(h_lo[:, e % HB, c], h[:, c], h_hi[:, e % HB, c],
                                                ALU.subtract).then_inc(h_lo_ready, 1)
                    if e == 0 and prepares:
                        rstd_of(g + 1)

            groups(pool, group)

        @block.scalar
        def _(a):
            def xT_high(g):
                a.wait_ge(xT_in_psum, g + 1)
                nc.scalar.activation(xT_hi[:, g], t_ps[:, :], ACT.Copy).then_inc(xT_hi_ready, 1)

            def gate_tanh(g):
                a.wait_ge(gap_ready, g + 1)
                nc.scalar.activation(tgap[:, :], gap[:, :], ACT.Tanh, scale=0.5).then_inc(tgap_ready, 1)

            for e in range(NE):
                a.wait_ge(up_in[e], 32)
                nc.scalar.activation(up_hi[:, e], up[:, e], ACT.Copy).then_inc(up_hi_done, 1)
                if e == 0:
                    xT_high(0)
            gate_tanh(0)

            def group(g, is_first, prepares):
                for e in range(NE):
                    for c in range(NC):
                        k = NC * e + c
                        a.wait_ge(g_ready, g * (NC * NE) + k + 1)
                        if not (is_first and e == 0):
                            a.wait_ge(h_ready, g * (NC * NE) + k + 1 - NC)
                        nc.scalar.activation(act[:, c], g_ps[:, c], ACT.Silu).then_inc(act_ready, 1)
                    for c in range(NC):
                        k = NC * e + c
                        a.wait_ge(h_ready, g * (NC * NE) + k + 1)
                        if not (is_first and e < HB):
                            a.wait_ge(down_done, g * NE + e + 1 - HB)
                        nc.scalar.activation(h_hi[:, e % HB, c], h[:, c], ACT.Copy).then_inc(h_hi_ready, 1)
                    if prepares:
                        if e == 2:
                            xT_high(g + 1)
                        if e == 7:
                            gate_tanh(g + 1)

            groups(a, group)

        @block.vector
        def _(dve):
            once = Steps(dve, dve_once, 0)
            once.begin(0)
            step = Steps(dve, dve_own, 13)

            def norm_stats(g):
                step.begin(g)
                for t in range(TG):
                    last = nc.vector.bn_stats(stats[:, t], x[:, g * TG + t])
                step(last, made)
                for t in range(TG):
                    last = nc.vector.bn_aggr(mv[:, t], stats[:, t])
                step(last)
                nc.vector.tensor_scalar(var[:, :], mv[:, :, 1], LN_EPS, None, ALU.add).then_inc(var_ready, 1)

            def norm(g):
                dve.wait_ge(rstd_ready, g + 1)
                for t in range(TG):
                    last = nc.vector.tensor_scalar(xn[:, t], x[:, g * TG + t], mv[:, t, 0:1], rstd[:, t:t + 1],
                                                   ALU.subtract, ALU.mult)
                last.then_inc(xn_ready, 1)

            def xT_low(g):
                dve.wait_ge(xT_hi_ready, g + 1)
                nc.vector.tensor_tensor(xT_lo[:, g], t_ps[:, :], xT_hi[:, g].bitcast(F32),
                                        ALU.subtract).then_inc(xT_ready, 1)

            def add_router_bias(g):
                dve.wait_ge(logT_in_psum, g + 1)
                nc.vector.tensor_scalar(logT[:, :], r_ps[0:E, :], rbias[:, 0:1], None, ALU.add).then_inc(logT_ready, 1)

            def compare(g):
                dve.wait_ge(logits_in_psum, g + 1)
                step(nc.vector.tensor_copy(logits[:], t_ps[:, 0:TG * E].rearrange("p (t e) -> p t e", e=E)))
                of_e = logits[:].unsqueeze(3).broadcast_to([P, TG, E, E])
                of_j = logits[:].unsqueeze(2).broadcast_to([P, TG, E, E])
                nc.vector.tensor_tensor(above[:], of_j, of_e, ALU.is_gt)
                step(nc.vector.tensor_tensor(equal[:], of_j, of_e, ALU.is_equal))

            def ranks(g):
                step(nc.vector.tensor_tensor(equal[:], equal[:], earlier[:].unsqueeze(1).broadcast_to([P, TG, E, E]), ALU.mult))
                step(nc.vector.tensor_tensor(above[:], above[:], equal[:], ALU.add))
                step(nc.vector.tensor_reduce(rank[:], above[:], op=ALU.add, axis=AX.X))

            def choose(g):
                nc.vector.tensor_scalar(first[:], rank[:], 0.0, None, ALU.is_equal)
                step(nc.vector.tensor_scalar(second[:], rank[:], 1.0, None, ALU.is_equal))
                nc.vector.tensor_tensor(either[:], first[:], second[:], ALU.add)
                step(nc.vector.tensor_tensor(signed[:], first[:], second[:], ALU.subtract))
                step(nc.vector.tensor_tensor(prod[:], signed[:], logits[:], ALU.mult))
                nc.vector.tensor_reduce(gap[:], prod[:], op=ALU.add, axis=AX.X).then_inc(gap_ready, 1)

            def make_gate(g):
                dve.wait_ge(tgap_ready, g + 1)
                step(nc.vector.tensor_tensor(mix[:], signed[:], tgap[:].unsqueeze(2).broadcast_to([P, TG, E]), ALU.mult))
                step(nc.vector.tensor_tensor(mix[:], mix[:], either[:], ALU.add))
                step(nc.vector.tensor_scalar(gate[:, g], mix[:], 0.25, None, ALU.mult))
                step.end()

            if x_loaded:
                dve.wait_ge(x_loaded, 16 * LOADS_OF_X)
            norm_stats(0)
            for e in range(E):
                last = nc.vector.memset(earlier[:, e, :], 0.0)
            once(last)
            for e in range(1, E):
                last = nc.vector.memset(earlier[:, e, 0:e], 1.0)
            once(last)
            norm(0)
            dve.wait_ge(router_in, 32)
            once(nc.vector.tensor_copy(router_hi[:], router[:]))
            nc.vector.tensor_tensor(router_lo[:], router[:], router_hi[:].bitcast(F32), ALU.subtract).then_inc(router_split, 1)
            xT_low(0)
            add_router_bias(0)
            compare(0)
            ranks(0)
            choose(0)

            def add_onto_x(g, e, value):
                dve.wait_ge(down_done, value)
                if not (isinstance(value, int) and value == 1):
                    dve.wait_ge(added, value - 1)
                o = o_ps[:, e % 2].rearrange("p (t d) -> p t d", d=P)
                for t in range(TG):
                    if e < E:
                        last = nc.vector.scalar_tensor_tensor(x[:, g * TG + t], o[:, t], gate[:, g, t, e:e + 1],
                                                              x[:, g * TG + t], ALU.mult, ALU.add)
                    else:
                        last = nc.vector.scalar_tensor_tensor(x[:, g * TG + t], o[:, t], 0.5, x[:, g * TG + t],
                                                              ALU.mult, ALU.add)
                last.then_inc(added, 1)

            def group(g, is_first, prepares):
                for e in range(NE):
                    for c in range(NC):
                        k = NC * e + c
                        dve.wait_ge(act_ready, g * (NC * NE) + k + 1)
                        dve.wait_ge(u_ready, g * (NC * NE) + k + 1)
                        if not (is_first and e == 0):
                            dve.wait_ge(h_lo_ready, g * (NC * NE) + k + 1 - NC)
                        nc.vector.tensor_tensor(h[:, c], act[:, c], u_ps[:, c], ALU.mult).then_inc(h_ready, 1)
                    if is_first and e == 0:
                        make_gate(0)
                        dve.wait_ge(down_in, 32)
                    if is_first and e < 3:
                        part = slice(3 * e, 3 * e + 3)
                        nc.vector.tensor_copy(down_hi[:, part], down[:, part]).then_inc(down_hi_done, 1)
                        dve.wait_ge(down_hi_done, e + 1)
                        nc.vector.tensor_tensor(down_lo[:, part], down[:, part], down_hi[:, part], ALU.subtract).then_inc(down_split, 1)
                    if e >= LAG:
                        add_onto_x(g, e - LAG, g * NE + e + 1 - LAG)
                    elif not is_first:
                        add_onto_x(g - 1, NE - LAG + e, g * NE + e + 1 - LAG)
                    if prepares:
                        if e == 0:
                            norm_stats(g + 1)
                        if e == 1:
                            norm(g + 1)
                        if e == 2:
                            xT_low(g + 1)
                        if e == 4:
                            add_router_bias(g + 1)
                        if e == 5:
                            compare(g + 1)
                        if e == 6:
                            ranks(g + 1)
                        if e == 7:
                            choose(g + 1)
                        if e == 8:
                            make_gate(g + 1)

            groups(dve, group)
            for e in range(NE - LAG, NE):
                add_onto_x(NG - 1, e, (NG - 1) * NE + e + 1)
            dve.wait_ge(added, NG * NE)

        @block.tensor
        def _(pe):
            def transpose_x(g):
                pe.wait_ge(xn_ready, g + 1)
                for t in range(TG):
                    last = nc.tensor.transpose(t_ps[:, t * P:(t + 1) * P], xn[:, t], ident[:, :])
                last.then_inc(xT_in_psum, 1)

            def route(g):
                pe.wait_ge(xT_ready, g + 1)
                parts = [(router_hi, xT_hi), (router_hi, xT_lo), (router_lo, xT_hi)]
                for i, (r, xt) in enumerate(parts):
                    last = nc.tensor.matmul(r_ps[0:E, :], r[:, :], xt[:, g], start=(i == 0), stop=(i == 2))
                last.then_inc(logT_in_psum, 1)

            def transpose_logits(g):
                wait_apart(pe, logT_ready, g + 1, made)
                for t in range(TG):
                    last = nc.tensor.transpose(t_ps[:, t * E:(t + 1) * E], logT[:, t * P:(t + 1) * P], ident[0:E, 0:E])
                last.then_inc(logits_in_psum, 1)

            def up_product(ps, which, g, e, c, done):
                cols = slice(c * P, (c + 1) * P)
                parts = [(up_hi, xT_hi), (up_hi, xT_lo), (up_lo, xT_hi)]
                for i, (wt, xt) in enumerate(parts):
                    last = nc.tensor.matmul(ps[:, c], wt[:, e, which, cols], xt[:, g], start=(i == 0), stop=(i == 2))
                last.then_inc(done, 1)

            def down_product(g, e, is_first):
                pe.wait_ge(h_lo_ready, g * (NC * NE) + NC * (e + 1))
                if not (is_first and e < 2):
                    pe.wait_ge(added, g * NE + (e - 1 if e >= 2 else 0 if e == 0 else -1))
                for t in range(TG):
                    n = 0
                    for c in range(NC):
                        for hp, wp in ((h_hi, down_hi), (h_hi, down_lo), (h_lo, down_hi)):
                            last = nc.tensor.matmul(o_ps[:, e % 2, t * P:(t + 1) * P],
                                                    hp[:, e % HB, c, t * P:(t + 1) * P], wp[:, e, c],
                                                    start=(n == 0), stop=(n == 3 * NC - 1))
                            n += 1
                last.then_inc(down_done, 1)

            transpose_x(0)
            pe.wait_ge(router_split, 1)
            route(0)
            transpose_logits(0)

            def group(g, is_first, prepares):
                for e in range(NE):
                    if is_first:
                        pe.wait_ge(up_split, e + 1)
                    for c in range(NC):
                        k = NC * e + c
                        if not (is_first and e == 0):
                            pe.wait_ge(act_ready, g * (NC * NE) + k + 1 - NC)
                        up_product(g_ps, 0, g, e, c, g_ready)
                        if not (is_first and e == 0):
                            pe.wait_ge(h_ready, g * (NC * NE) + k + 1 - NC)
                        up_product(u_ps, 1, g, e, c, u_ready)
                    if prepares:
                        if e == 2:
                            transpose_x(g + 1)
                        if e == 3:
                            route(g + 1)
                        if e == 5:
                            transpose_logits(g + 1)
                    if is_first and e % 3 == 2:
                        pe.wait_ge(down_split, e // 3 + 1)
                    if e >= LAG:
                        down_product(g, e - LAG, is_first)
                    elif not is_first:
                        down_product(g - 1, NE - LAG + e, False)

            groups(pe, group)
            for e in range(NE - LAG, NE):
                down_product(NG - 1, e, False)


class LaterWeights:

    def __init__(self, nc, ctx, w):
        self.w = w
        F = w["fc1_q"].shape[1]
        NF, (D, CS) = w["wv_f"].shape[0], w["cs_w1T"].shape
        nm = Names(nc, ctx, "later")
        self.q1 = nm.sb("q1", [P, F], I32)
        self.q2 = nm.sb("q2", [P, F // P, P], I32)
        self.s1 = nm.sb("s1", [P, F], F32)
        self.s2 = nm.sb("s2", [P, F // P, P], F32)
        self.cols = nm.sb("cols", [P, 2 + F // P], F32)
        self.bias2 = nm.sb("bias2", [P, P], F32)
        self.lin_w = nm.sb("lin_w", [P, 2 + NF, P], F32)
        self.lin_c = nm.sb("lin_c", [P, CS], F32)
        self.lin_wo = nm.sb("lin_wo", [P, NF, P], F32)
        self.lin_cs2 = nm.sb("lin_cs2", [CS, P], F32)
        self.lin_b1 = nm.sb("lin_b1", [CS, 1], F32)
        self.lin_rows = nm.sb("lin_rows", [P, 2], F32)
        D, QKV = w["wqkv"].shape
        HD = w["rope_cos"].shape[2]
        self.wqkv = nm.sb("wqkv", [P, QKV], F32)
        self.qkv_bias = nm.sb("qkv_bias", [P, QKV], F32)
        self.diff_wo = nm.sb("diff_wo", [P, P], F32)
        self.wo_bias = nm.sb("wo_bias", [P, P], F32)
        self.head_w = nm.sb("head_w", [P, 1], F32)
        self.rope_cos = nm.sb("rope_cos", [P, 2, HD], F32)
        self.rope_sin = nm.sb("rope_sin", [P, 2, HD], F32)
        self.causal = nm.sb("causal", [P, P], F32)
        self.lam_in = nm.sb("lam_in", [P, *w["lam"].shape], F32)
        self.diff_in = nm.sem("diff_in")
        self.ffn_in = nm.sem("ffn_in")
        self.lin_in = nm.sem("lin_in")

    def load(self, sp):
        w = self.w
        sp.dma_start(self.wqkv[:], w["wqkv"]).then_inc(self.diff_in, 16)
        sp.dma_start(self.qkv_bias[:], w["qkv_bias"].broadcast_to(self.qkv_bias.shape)).then_inc(self.diff_in, 16)
        sp.dma_start(self.diff_wo[:], w["wo_T"]).then_inc(self.diff_in, 16)
        sp.dma_start(self.wo_bias[:], w["wo_bias"].broadcast_to([P, P])).then_inc(self.diff_in, 16)
        sp.dma_start(self.head_w[:], w["head_w"]).then_inc(self.diff_in, 16)
        sp.dma_start(self.rope_cos[:], w["rope_cos"]).then_inc(self.diff_in, 16)
        sp.dma_start(self.rope_sin[:], w["rope_sin"]).then_inc(self.diff_in, 16)
        sp.dma_start(self.causal[:], w["causal"]).then_inc(self.diff_in, 16)
        sp.dma_start(self.lam_in[:], w["lam"].unsqueeze(0).broadcast_to(self.lam_in.shape)).then_inc(self.diff_in, 16)
        sp.dma_start(self.q1[:], w["fc1_q"]).then_inc(self.ffn_in, 16)
        sp.dma_start(self.s1[:], w["fc1_scales"].broadcast_to(self.s1.shape)).then_inc(self.ffn_in, 16)
        sp.dma_start(self.q2[:], w["fc2_q"].rearrange("(c p) d -> p c d", p=P)).then_inc(self.ffn_in, 16)
        sp.dma_start(self.s2[:], w["fc2_scales"].unsqueeze(0).broadcast_to(self.s2.shape)).then_inc(self.ffn_in, 16)
        sp.dma_start(self.cols[:], w["ffn1_cols"]).then_inc(self.ffn_in, 16)
        sp.dma_start(self.bias2[:], w["fc2_bias"].broadcast_to([P, P])).then_inc(self.ffn_in, 16)
        sp.dma_start(self.lin_w[:, 0:2], w["wkq"]).then_inc(self.lin_in, 16)
        sp.dma_start(self.lin_c[:], w["cs_w1T"]).then_inc(self.lin_in, 16)
        sp.dma_start(self.lin_cs2[:], w["cs_w2T"]).then_inc(self.lin_in, 16)
        sp.dma_start(self.lin_b1[:], w["cs_b1"]).then_inc(self.lin_in, 16)
        sp.dma_start(self.lin_rows[:], w["rows"]).then_inc(self.lin_in, 16)
        sp.dma_start(self.lin_w[:, 2:], w["wv_f"].rearrange("f p n -> p f n")).then_inc(self.lin_in, 16)
        sp.dma_start(self.lin_wo[:], w["wo_f"].rearrange("f p n -> p f n")).then_inc(self.lin_in, 16)

    DIFF_LOADS, FFN_LOADS, LIN_LOADS = 9 * 16, 6 * 16, 7 * 16


def dequantized_weights(nc, ctx, later):
    F = later.q1.shape[1]
    NC = F // P
    nm = Names(nc, ctx, "deq")
    q1, q2, s1, s2, cols, bias2 = later.q1, later.q2, later.s1, later.s2, later.cols, later.bias2
    hi1 = nm.sb("fc1_hi", [P, F], F32R)
    lo1 = nm.sb("fc1_lo", [P, F], F32R)
    hi2 = nm.sb("fc2_hi", [P, NC, P], F16)
    lo2 = nm.sb("fc2_lo", [P, NC, P], F16)
    with ExitStack() as inner:
        tm = Names(nc, inner, "deq")
        w1 = tm.sb("w1", [P, F], F32)
        w2 = tm.sb("w2", [P, NC, P], F32)
        own = tm.sem("own")
        block = inner.enter_context(nc.Block())

        @block.vector
        def _(dve):
            dve.wait_ge(later.ffn_in, later.FFN_LOADS)
            nc.vector.scalar_tensor_tensor(w1[:], q1[:], -128.0, s1[:], ALU.add, ALU.mult).then_inc(own, 1)
            nc.vector.scalar_tensor_tensor(w2[:], q2[:], -128.0, s2[:], ALU.add, ALU.mult).then_inc(own, 1)
            nc.vector.tensor_scalar(bias2[:], bias2[:], 0.25, None, ALU.mult).then_inc(own, 1)
            dve.wait_ge(own, 3)
            nc.vector.tensor_copy(hi1[:], w1[:]).then_inc(own, 1)
            nc.vector.tensor_copy(hi2[:], w2[:]).then_inc(own, 1)
            dve.wait_ge(own, 5)
            nc.vector.tensor_tensor(lo1[:], w1[:], hi1[:].bitcast(F32), ALU.subtract).then_inc(own, 1)
            nc.vector.tensor_tensor(lo2[:], w2[:], hi2[:], ALU.subtract).then_inc(own, 1)
            dve.wait_ge(own, 7)
    return dict(hi1=hi1, lo1=lo1, hi2=hi2, lo2=lo2, cols=cols, bias2=bias2)


def quantized_ffn(nc, tag, x, ident, neghalf, made, w, out_tiles=None, stored=None):
    NC = w["hi1"].shape[1] // P
    NG = x.shape[1] // TG - 1
    with ExitStack() as ctx:
        nm = Names(nc, ctx, tag)
        stats = nm.sb("stats", [P, TG, 6], F32)
        mv = nm.sb("mv", [P, 2, TG, 2], F32)
        var = nm.sb("var", [P, TG], F32)
        r0 = nm.sb("r0", [P, 2, TG], F32)
        r1 = nm.sb("r1", [P, 2, TG], F32)
        r01 = nm.sb("r01", [P, 2, TG], F32)
        v1 = nm.sb("v1", [P, TG], F32)
        keep = nm.sb("keep", [P, 2, TG], F32)
        shift = nm.sb("shift", [P, 2, TG], F32)
        hn = nm.sb("hn", [P, TG, P], F32)
        hT = nm.sb("hT", [P, GN], F32)
        hT_hi = nm.sb("hT_hi", [P, 2, GN], F32R)
        hT_lo = nm.sb("hT_lo", [P, 2, GN], F32R)
        y = nm.sb("y", [P, NC, GN], F32)
        y_hi = nm.sb("y_hi", [P, 2, NC, GN], F16)
        y_lo = nm.sb("y_lo", [P, 2, NC, GN], F16)
        y_ps = nm.ps("y_ps", [P, NC, GN], F32)
        z_ps = nm.ps("z_ps", [P, 2, GN], F32)
        t_ps = nm.ps("t_ps", [P, GN], F32)

        stats_own = nm.sem("stats_own")
        scales_own = nm.sem("scales_own")
        r01_ready = nm.sem("r01_ready")
        var_ready = nm.sem("var_ready")
        r0_ready = nm.sem("r0_ready")
        v1_ready = nm.sem("v1_ready")
        r1_ready = nm.sem("r1_ready")
        hn_ready = nm.sem("hn_ready")
        hT_in_psum = nm.sem("hT_in_psum")
        hT_copied = nm.sem("hT_copied")
        hT_hi_ready = nm.sem("hT_hi_ready")
        hT_ready = nm.sem("hT_ready")
        y_in_psum = nm.sem("y_in_psum")
        y_ready = nm.sem("y_ready")
        y_hi_ready = nm.sem("y_hi_ready")
        y_lo_pool = nm.sem("y_lo_pool")
        y_lo_dve = nm.sem("y_lo_dve")
        z_ready = nm.sem("z_ready")
        z_added = nm.sem("z_added")
        x_biased = nm.sem("x_biased")
        x_kept = nm.sem("x_kept")
        block = ctx.enter_context(nc.Block())
        POOL_C = NC - 1

        def pairs(engine, group):
            group(0, 0, True, True)
            group(1, 1, False, True)
            with engine.Fori(1, NG // 2 - 1) as i:
                group(i * 2, 0, False, True)
                group(i * 2 + 1, 1, False, True)
            group(NG - 2, 0, False, True)
            group(NG - 1, 1, False, False)

        @block.sync
        def _(sp):
            if out_tiles is None:
                return
            for g in range(NG):
                sp.wait_ge(z_added, g + 1)
                tiles = slice(g * TG, (g + 1) * TG)
                sp.dma_start(out_tiles[:, tiles], x[:, tiles]).then_inc(stored, 16)
            sp.wait_ge(stored, 16 * NG)

        @block.gpsimd
        def _(pool):
            def scale_0(g, b):
                pool.wait_ge(var_ready, g + 1)
                nc.gpsimd.tensor_tensor(r0[:, b], var[:], neghalf[:, 0:TG], ALU.pow).then_inc(r0_ready, 1)

            def scale_1(g, b):
                pool.wait_ge(v1_ready, g + 1)
                nc.gpsimd.tensor_tensor(r1[:, b], v1[:], neghalf[:, 0:TG], ALU.pow).then_inc(r1_ready, 1)

            def add_bias(g):
                pool.wait_ge(x_kept, g + 1)
                xs = x[:, bass.ds(g * TG, TG)]
                nc.gpsimd.tensor_tensor(xs, xs, w["bias2"][:].unsqueeze(1).broadcast_to([P, TG, P]),
                                        ALU.add).then_inc(x_biased, 1)

            for g in range(2):
                scale_0(g, g)
                scale_1(g, g)

            def group(g, b, is_first, prepares):
                for c in range(POOL_C):
                    pool.wait_ge(y_hi_ready, g * NC + c + 1)
                    if c == 0 and not (isinstance(g, int) and g < 2):
                        pool.wait_ge(z_ready, g - 1)
                    nc.gpsimd.tensor_tensor(y_lo[:, b, c], y[:, c], y_hi[:, b, c], ALU.subtract).then_inc(y_lo_pool, 1)
                    if c == 0 and prepares:
                        scale_0(g + 2, b)
                    if c == 1:
                        if prepares:
                            scale_1(g + 2, b)
                        add_bias(g)

            pairs(pool, group)

        @block.scalar
        def _(a):
            def high(g, b):
                a.wait_ge(hT_copied, g + 1)
                nc.scalar.activation(hT_hi[:, b], hT[:], ACT.Copy).then_inc(hT_hi_ready, 1)

            high(0, 0)

            def group(g, b, is_first, prepares):
                for c in range(NC):
                    a.wait_ge(y_in_psum, g * NC + c + 1)
                    if not is_first:
                        if c < POOL_C:
                            a.wait_ge(y_lo_pool, g * POOL_C + c + 1 - POOL_C)
                        else:
                            a.wait_ge(y_lo_dve, g)
                    nc.scalar.activation(y[:, c], y_ps[:, c], ACT.Silu, bias=w["cols"][:, 2 + c:3 + c]).then_inc(y_ready, 1)
                    a.wait_ge(y_ready, g * NC + c + 1)
                    if c == 0 and not (isinstance(g, int) and g < 2):
                        a.wait_ge(z_ready, g - 1)
                    nc.scalar.activation(y_hi[:, b, c], y[:, c], ACT.Copy).then_inc(y_hi_ready, 1)
                    if prepares and c == 1:
                        high(g + 1, 1 - b)

            pairs(a, group)

        @block.vector
        def _(dve):
            stats_step = Steps(dve, stats_own, 2)
            scales_step = Steps(dve, scales_own, 5)

            def statistics(g, b):
                stats_step.begin(g)
                for t in range(TG):
                    last = nc.vector.bn_stats(stats[:, t], x[:, g * TG + t])
                stats_step(last, made)
                for t in range(TG):
                    last = nc.vector.bn_aggr(mv[:, b, t], stats[:, t])
                stats_step(last)
                stats_step.end()
                nc.vector.tensor_scalar(var[:], mv[:, b, :, 1], LN_EPS, None, ALU.add).then_inc(var_ready, 1)

            def scales(g, b):
                dve.wait_ge(r0_ready, g + 1)
                scales_step.begin(g)
                scales_step(nc.vector.tensor_tensor(v1[:], r0[:, b], r0[:, b], ALU.mult))
                scales_step(nc.vector.tensor_tensor(v1[:], v1[:], mv[:, b, :, 1], ALU.mult))
                nc.vector.tensor_scalar(v1[:], v1[:], LN_EPS, None, ALU.add).then_inc(v1_ready, 1)
                scales_step(nc.vector.tensor_scalar(keep[:, b], r0[:, b], 0.5, None, ALU.mult))
                scales_step(nc.vector.scalar_tensor_tensor(shift[:, b], mv[:, b, :, 0], -1.0, keep[:, b], ALU.mult, ALU.mult))
                scales_step(nc.vector.tensor_scalar(keep[:, b], keep[:, b], 1.0, None, ALU.add))
                scales_step.end()

            def normalise(g, b):
                dve.wait_ge(r1_ready, g + 1)
                nc.vector.tensor_tensor(r01[:, b], r0[:, b], r1[:, b], ALU.mult).then_inc(r01_ready, 1)
                dve.wait_ge(r01_ready, g + 1)
                for t in range(TG):
                    last = nc.vector.tensor_scalar(hn[:, t], x[:, g * TG + t], mv[:, b, t, 0:1], r01[:, b, t:t + 1],
                                                   ALU.subtract, ALU.mult)
                last.then_inc(hn_ready, 1)

            def keep_x(g, b):
                for t in range(TG):
                    last = nc.vector.tensor_scalar(x[:, g * TG + t], x[:, g * TG + t], keep[:, b, t:t + 1],
                                                   shift[:, b, t:t + 1], ALU.mult, ALU.add)
                last.then_inc(x_kept, 1)

            def affine(g):
                dve.wait_ge(hT_in_psum, g + 1)
                nc.vector.tensor_scalar(hT[:], t_ps[:], w["cols"][:, 0:1], w["cols"][:, 1:2],
                                        ALU.mult, ALU.add).then_inc(hT_copied, 1)

            def low(g, b):
                dve.wait_ge(hT_hi_ready, g + 1)
                nc.vector.tensor_tensor(hT_lo[:, b], hT[:], hT_hi[:, b].bitcast(F32), ALU.subtract).then_inc(hT_ready, 1)

            def add_z(g, b):
                dve.wait_ge(z_ready, g + 1)
                dve.wait_ge(x_biased, g + 1)
                xs = x[:, bass.ds(g * TG, TG)].rearrange("p t d -> p (t d)")
                nc.vector.scalar_tensor_tensor(xs, z_ps[:, b], 0.25, xs, ALU.mult, ALU.add).then_inc(z_added, 1)

            for g in range(2):
                statistics(g, g)
                scales(g, g)
                if g == 0:
                    normalise(0, 0)
                    affine(0)
                    low(0, 0)
                    keep_x(0, 0)

            def group(g, b, is_first, prepares):
                if prepares:
                    normalise(g + 1, 1 - b)
                    statistics(g + 2, b)
                    affine(g + 1)
                if not (isinstance(g, int) and g < 2):
                    add_z(g - 2, b)
                if prepares:
                    scales(g + 2, b)
                    low(g + 1, 1 - b)
                    keep_x(g + 1, 1 - b)
                c = NC - 1
                dve.wait_ge(y_hi_ready, g * NC + c + 1)
                if not (isinstance(g, int) and g < 2):
                    dve.wait_ge(z_ready, g - 1)
                nc.vector.tensor_tensor(y_lo[:, b, c], y[:, c], y_hi[:, b, c], ALU.subtract).then_inc(y_lo_dve, 1)

            pairs(dve, group)
            add_z(NG - 2, 0)
            add_z(NG - 1, 1)
            dve.wait_ge(z_added, NG)

        @block.tensor
        def _(pe):
            def transpose_h(g):
                pe.wait_ge(hn_ready, g + 1)
                if not (isinstance(g, int) and g == 0):
                    pe.wait_ge(hT_copied, g)
                for t in range(TG):
                    last = nc.tensor.transpose(t_ps[:, t * P:(t + 1) * P], hn[:, t], ident[:, :])
                last.then_inc(hT_in_psum, 1)

            def up(g, b, c, is_first):
                if c == 0:
                    pe.wait_ge(hT_ready, g + 1)
                if not is_first:
                    pe.wait_ge(y_ready, g * NC + c + 1 - NC)
                parts = [(w["hi1"], hT_hi), (w["hi1"], hT_lo), (w["lo1"], hT_hi)]
                for i, (wt, ht) in enumerate(parts):
                    last = nc.tensor.matmul(y_ps[:, c], wt[:, c * P:(c + 1) * P], ht[:, b], start=(i == 0), stop=(i == 2))
                last.then_inc(y_in_psum, 1)

            def down(g, b):
                pe.wait_ge(y_lo_pool, (g + 1) * POOL_C)
                pe.wait_ge(y_lo_dve, g + 1)
                if not (isinstance(g, int) and g < 2):
                    pe.wait_ge(z_added, g - 1)
                for t in range(TG):
                    n = 0
                    for c in range(NC):
                        for yp, wp in ((y_hi, w["hi2"]), (y_hi, w["lo2"]), (y_lo, w["hi2"])):
                            last = nc.tensor.matmul(z_ps[:, b, t * P:(t + 1) * P], yp[:, b, c, t * P:(t + 1) * P],
                                                    wp[:, c], start=(n == 0), stop=(n == 3 * NC - 1))
                            n += 1
                last.then_inc(z_ready, 1)

            transpose_h(0)

            def group(g, b, is_first, prepares):
                for c in range(NC):
                    up(g, b, c, is_first)
                    if c == 1 and prepares:
                        transpose_h(g + 1)
                if not is_first:
                    down(g - 1, 1 - b)

            pairs(pe, group)
            down(NG - 1, 1)


def diff_attention(nc, tag, x, ident, neghalf, made, later):
    HEADS, HD = 16, 8
    MAPS = 2 * HEADS
    CH = MAPS // 4
    S = 2 * P
    NB = (x.shape[1] - TG) // 2
    STEPS = 24
    HALF = 12
    LAG = 3
    RING = 4
    QKV = 3 * MAPS * HD - MAPS * HD // 2
    W2 = QKV // 2
    SCALE = HD ** -0.5
    PACK = 32
    RMS_EPS = 1e-6

    with ExitStack() as ctx:
        nm = Names(nc, ctx, tag)
        qkv_bias, wo_bias, head_w, lam_in = later.qkv_bias, later.wo_bias, later.head_w, later.lam_in
        rope_cos, rope_sin = later.rope_cos, later.rope_sin
        wqkv_hi = nm.sb("wqkv_hi", [P, QKV], F32R)
        wqkv_lo = nm.sb("wqkv_lo", [P, QKV], F32R)
        wo = nm.sb("wo", [P, P], F32)
        ident_bf = nm.sb("ident_bf", [P, P], BF16)
        ident_h = nm.sb("ident_h", [P, P], F16)
        mask = nm.sb("mask", [P, 4, P], BF16)
        branch = nm.sb("branch", [P, HEADS, 2], F32)
        lam_sum = nm.sb("lam_sum", [P, 2, HEADS], F32)
        lam_exp = nm.sb("lam_exp", [P, 2, HEADS], F32)

        stats = nm.sb("stats", [P, 2, 6], F32)
        mv = nm.sb("mv", [P, 2, 2], F32)
        var = nm.sb("var", [P, 2], F32)
        rstd = nm.sb("rstd", [P, 2], F32)
        xn = nm.sb("xn", [P, 2, P], F32)
        xT_hi = nm.sb("xT_hi", [P, S], F32R)
        xT_lo = nm.sb("xT_lo", [P, S], F32R)
        qk = nm.sb("qk", [P, 2, 2 * MAPS, HD], F32)
        v_new = nm.sb("v_new", [P, 2, HEADS, HD], F32)
        v = nm.sb("v", [P, 2, 2, HEADS, PACK], F32)
        by_cos = nm.sb("by_cos", [P, 2, 2 * MAPS, HD], F32)
        by_sin = nm.sb("by_sin", [P, 2, 2 * MAPS, HD], F32)
        rot = nm.sb("rot", [P, 2, 2 * MAPS, HD], F32)
        q_pack = nm.sb("q_pack", [P, 2, 2, MAPS, PACK], F16)
        k_pack = nm.sb("k_pack", [P, 2, MAPS, PACK], F16)
        qT = nm.sb("qT", [P, 2, CH, S], F16)
        qmT = nm.sb("qmT", [P, 2, CH, S], F16)
        kT = nm.sb("kT", [P, CH, S], F16)
        k_one = nm.sb("k_one", [P, 2, 4, CH, S], F16)
        prob = nm.sb("prob", [P, RING, 512], F32)
        oT = nm.sb("oT", [P, 2, 512], F32)
        inv = nm.sb("inv", [P, 2, MAPS // 2], F32)
        weighted = nm.sb("weighted", [P, 2, MAPS, HD], F32)
        o = nm.sb("o", [P, 2, HEADS, HD], F32)
        osq = nm.sb("osq", [P, 2, HEADS, HD], F32)
        ms = nm.sb("ms", [P, 2, HEADS], F32)
        rms = nm.sb("rms", [P, 2, HEADS], F32)
        on = nm.sb("on", [P, 2, HEADS, HD], F32)
        onT = nm.sb("onT", [P, S], F32)

        s_ps = nm.ps("s_ps", [P, 2, 512], F32)
        st_ps = nm.ps("st_ps", [P, 2, 512], F32)
        ot_ps = nm.ps("ot_ps", [P, 2, 512], F32)
        m_ps = nm.ps("m_ps", [P, 2, 512], F32)
        m16 = [m_ps[:, i].bitcast(F16) for i in range(2)]

        packs_ready = nm.sem("packs_ready")
        prepared = nm.sem("prepared")
        lam_summed = nm.sem("lam_summed")
        lam_exped = nm.sem("lam_exped")
        once_own = nm.sem("once_own")
        a_own = nm.sem("a_own")
        d_own = nm.sem("d_own")
        var_ready = nm.sem("var_ready")
        rstd_ready = nm.sem("rstd_ready")
        xn_ready = nm.sem("xn_ready")
        xT_in_psum = nm.sem("xT_in_psum")
        xT_hi_ready = nm.sem("xT_hi_ready")
        xT_ready = nm.sem("xT_ready")
        qkv_in_psum = nm.sem("qkv_in_psum")
        qkv_ready = nm.sem("qkv_ready")
        cos_ready = nm.sem("cos_ready")
        sin_ready = nm.sem("sin_ready")
        rot_ready = nm.sem("rot_ready")
        pack_hi = nm.sem("pack_hi")
        pack_lo = nm.sem("pack_lo")
        pack_lo_q = nm.sem("pack_lo_q")
        packT_in_psum = nm.sem("packT_in_psum")
        packT_ready = nm.sem("packT_ready")
        k_one_ready = [nm.sem("k_one_ready_0"), nm.sem("k_one_ready_1")]
        s_ready = nm.sem("s_ready")
        max_ready = nm.sem("max_ready")
        qmT_in_psum = nm.sem("qmT_in_psum")
        qmT_ready = nm.sem("qmT_ready")
        st_ready = nm.sem("st_ready")
        exp_ready = nm.sem("exp_ready")
        prob_ready = nm.sem("prob_ready")
        v_ready = nm.sem("v_ready")
        pv_done = nm.sem("pv_done")
        oT_copied = nm.sem("oT_copied")
        o_in_psum = nm.sem("o_in_psum")
        o_weighted = nm.sem("o_weighted")
        ms_ready = nm.sem("ms_ready")
        rms_ready = nm.sem("rms_ready")
        on_ready = nm.sem("on_ready")
        onT_in_psum = nm.sem("onT_in_psum")
        onT_ready = nm.sem("onT_ready")
        y_in_psum = nm.sem("y_in_psum")
        x_added = nm.sem("x_added")
        block = ctx.enter_context(nc.Block())

        def turns(engine, turn):
            def peeled(it):
                turn(*[b if 0 <= b < NB else None for b in (it, it - 1, it - 2, it - 3)], it % 2)

            for it in range(4):
                peeled(it)
            with engine.Fori(2, NB // 2) as i:
                for half in range(2):
                    it = i * 2 + half
                    turn(it, it - 1, it - 2, it - 3, half)
            for it in range(NB, NB + 3):
                peeled(it)

        def below(b, n):
            return isinstance(b, int) and b < n

        def unit(u):
            half, k = divmod(u, HALF)
            if k < 4:
                return 1, 16 * half + 4 * k, 4
            return 0, 16 * half + 2 * (k - 4), 2

        @block.sync
        def _(sp):
            sp.wait_ge(packs_ready, 6)

            def turn(A, B, C, D, par):
                if A is None:
                    return
                if below(A, 2) and A == 1:
                    sp.wait_ge(packs_ready, 7)
                for half in range(2):
                    wait_apart(sp, packT_ready, A * 4 + (4 if half else 1), made)
                    if C is not None:
                        wait_apart(sp, st_ready, C * STEPS + HALF * (half + 1), made)
                    for r in range(4):
                        rows, ch = slice(32 * r, 32 * r + 32), slice(4 * half, 4 * half + 4)
                        sp.dma_start(k_one[rows, par, r, ch], kT[rows, ch]).then_inc(k_one_ready[half], 16)

            turns(sp, turn)
            for half in range(2):
                sp.wait_ge(k_one_ready[half], NB * 64)

        @block.gpsimd
        def _(pool):
            def scale_of(b):
                pool.wait_ge(var_ready, b + 1)
                nc.gpsimd.tensor_tensor(rstd[:], var[:], neghalf[:, 0:2], ALU.pow).then_inc(rstd_ready, 1)

            def rms_of(b, half, j):
                if j == 0:
                    pool.wait_ge(ms_ready, b * 2 + half + 1)
                heads = slice(8 * half, 8 * half + 8)
                nc.gpsimd.tensor_tensor(rms[:, j, heads], ms[:, j, heads], neghalf[:, 0:8], ALU.pow).then_inc(rms_ready, 1)

            scale_of(0)
            nc.gpsimd.memset(v[:], 0.0).then_inc(packs_ready, 1)
            nc.gpsimd.memset(k_one[:, 0].bitcast(F32), 0.0).then_inc(packs_ready, 1)
            pool.wait_ge(packs_ready, 4)
            nc.gpsimd.memset(v[:, :, :, :, HD:HD + 1].rearrange("p a b c d -> p (a b c) d"), 1.0).then_inc(packs_ready, 1)
            nc.gpsimd.memset(k_pack[:, :, :, 3 * HD:3 * HD + 1].rearrange("p a b c -> p (a b) c"), 1.0).then_inc(packs_ready, 1)

            def turn(A, B, C, D, par):
                for u in range(STEPS):
                    if C is not None:
                        key, m0, n = unit(u)
                        wait_apart(pool, exp_ready, C * STEPS + u + 1, made)
                        pr = prob[:, u % RING].rearrange("p (m q) -> p m q", m=n)[:, :, 0:P]
                        nc.gpsimd.affine_select(out=pr, in_=pr, compare_op=ALU.is_ge, fill=0.0, base=0,
                                                pattern=[[0, n], [1, P]], channel_multiplier=-1).then_inc(prob_ready, 1)
                    if A is not None:
                        if u == 15:
                            wait_apart(pool, pack_hi, A * 4 + 2, made)
                            nc.gpsimd.memset(q_pack[:, par, :, :, 3 * HD], 0.0)
                            for j in range(2):
                                last = nc.gpsimd.tensor_tensor(q_pack[:, par, j, :, HD:2 * HD], rot[:, j, 0:MAPS],
                                                               q_pack[:, par, j, :, 0:HD], ALU.subtract)
                            last.then_inc(pack_lo_q, 1)
                        if u == 21:
                            scale_of(A + 1)
                        if u in (9, 12):
                            j = (u - 9) // 3
                            pool.wait_ge(qkv_ready, A * 2 + j + 1)
                            nc.gpsimd.tensor_tensor(by_cos[:, j], qk[:, j],
                                                    rope_cos[:, j].unsqueeze(1).broadcast_to([P, 2 * MAPS, HD]),
                                                    ALU.mult).then_inc(cos_ready, 1)
                    if below(A, 1) and u == STEPS - 1:
                        nc.gpsimd.memset(k_one[:, 1].bitcast(F32), 0.0).then_inc(packs_ready, 1)
                    if B is not None and u == 4:
                        if D is not None:
                            wait_apart(pool, pv_done, (D + 1) * STEPS, made)
                        wait_apart(pool, qkv_ready, B * 2 + 2, made)
                        nc.gpsimd.tensor_copy(v[:, 1 - par, :, :, 0:HD].rearrange("p j h d -> p (j h) d"),
                                              v_new[:].rearrange("p j h d -> p (j h) d")).then_inc(v_ready, 1)
                    if D is not None and u in (7, 8):
                        rms_of(D, 1, u - 7)
                    if C is not None and u in (20, 22):
                        rms_of(C, 0, (u - 20) // 2)

            turns(pool, turn)

        @block.scalar
        def _(a):
            a.wait_ge(lam_summed, 1)
            nc.scalar.activation(lam_exp[:], lam_sum[:], ACT.Exp).then_inc(lam_exped, 1)
            def turn(A, B, C, D, par):
                for u in range(STEPS):
                    if D is not None and u == 2:
                        a.wait_ge(pv_done, (D + 1) * STEPS)
                        a.wait_ge(o_in_psum, D * 2 + 1)
                        nc.scalar.activation(oT[:, 0], ot_ps[:, 0], ACT.Copy).then_inc(oT_copied, 1)
                    if C is not None:
                        a.wait_ge(st_ready, C * STEPS + u + 1)
                        if not (below(C, 1) and u < RING):
                            a.wait_ge(pv_done, C * STEPS + u + 1 - RING)
                        nc.scalar.activation(prob[:, u % RING], st_ps[:, u % 2], ACT.Exp, scale=SCALE).then_inc(exp_ready, 1)
                        if u == 1:
                            a.wait_ge(qmT_in_psum, C * 2 + 2)
                            nc.scalar.activation(qmT[:, par, :, 0:P], m16[1].rearrange("p (c q) -> p c q", q=P),
                                                 ACT.Copy).then_inc(qmT_ready, 1)
                        if u == 14:
                            a.wait_ge(pv_done, C * STEPS + HALF)
                            if not below(C, 1):
                                a.wait_ge(o_in_psum, C * 2)
                            nc.scalar.activation(oT[:, 0], ot_ps[:, 0], ACT.Copy).then_inc(oT_copied, 1)
                    if D is not None:
                        if u == 13:
                            a.wait_ge(onT_in_psum, D + 1)
                            nc.scalar.activation(onT[:], m_ps[:, 0, 0:S], ACT.Copy).then_inc(onT_ready, 1)
                    if A is not None:
                        if u == 3:
                            a.wait_ge(xT_in_psum, A + 1)
                            nc.scalar.activation(xT_hi[:], m_ps[:, 0, 0:S], ACT.Copy).then_inc(xT_hi_ready, 1)
                        if u == 14:
                            a.wait_ge(rot_ready, A + 1)
                            if below(A, 1):
                                a.wait_ge(packs_ready, 6)
                            if C is not None:
                                a.wait_ge(qmT_in_psum, C * 2 + 2)
                            for j in range(2):
                                src = rot[:, j, 0:MAPS].unsqueeze(2).broadcast_to([P, MAPS, 2, HD])
                                dst = q_pack[:, par, j].rearrange("p m (r d) -> p m r d", d=2 * HD)[:, :, :, 0:HD]
                                nc.scalar.activation(dst, src, ACT.Copy).then_inc(pack_hi, 1)
                        if u == 15:
                            if not below(A, 1):
                                a.wait_ge(packT_in_psum, A * 4)
                            for j in range(2):
                                src = rot[:, j, MAPS:].unsqueeze(2).broadcast_to([P, MAPS, 2, HD])
                                dst = k_pack[:, j, :, 0:2 * HD].rearrange("p m (r d) -> p m r d", d=HD)
                                nc.scalar.activation(dst, src, ACT.Copy).then_inc(pack_hi, 1)
                        if u == 19:
                            a.wait_ge(packT_in_psum, A * 4 + 1)
                            if not below(A, 1):
                                for half in range(2):
                                    a.wait_ge(k_one_ready[half], A * 64)
                            nc.scalar.activation(kT[:, 0:4], m16[0].rearrange("p (c q) -> p c q", q=S),
                                                 ACT.Copy).then_inc(packT_ready, 1)
                        if u in (20, 21):
                            j = u - 20
                            a.wait_ge(packT_in_psum, A * 4 + 2 + j)
                            nc.scalar.activation(qT[:, par, :, j * P:(j + 1) * P], m16[1 - j].rearrange("p (c q) -> p c q", q=P),
                                                 ACT.Copy).then_inc(packT_ready, 1)
                    if B is not None and u == 22:
                        a.wait_ge(qmT_in_psum, B * 2 + 1)
                        nc.scalar.activation(qmT[:, 1 - par, :, P:], m16[1].rearrange("p (c q) -> p c q", q=P),
                                             ACT.Copy).then_inc(qmT_ready, 1)
                    if A is not None and u == 23:
                        a.wait_ge(packT_in_psum, A * 4 + 4)
                        nc.scalar.activation(kT[:, 4:8], m16[0].rearrange("p (c q) -> p c q", q=S),
                                             ACT.Copy).then_inc(packT_ready, 1)

            turns(a, turn)

        @block.vector
        def _(dve):
            once = Steps(dve, once_own, 0)
            once.begin(0)
            a_step = Steps(dve, a_own, 2)
            d_step = Steps(dve, d_own, 10)

            def statistics(b):
                a_step.begin(b)
                for j in range(2):
                    last = nc.vector.bn_stats(stats[:, j], x[:, b * 2 + j])
                a_step(last, made)
                for j in range(2):
                    last = nc.vector.bn_aggr(mv[:, j], stats[:, j])
                a_step(last)
                a_step.end()
                nc.vector.tensor_scalar(var[:], mv[:, :, 1], LN_EPS, None, ALU.add).then_inc(var_ready, 1)

            statistics(0)
            dve.wait_ge(later.diff_in, later.DIFF_LOADS)
            nc.vector.tensor_tensor(lam_in[:, 0:2], lam_in[:, 0:2], lam_in[:, 2:4], ALU.mult)
            once(nc.vector.tensor_copy(wqkv_hi[:], later.wqkv[:]))
            nc.vector.tensor_reduce(lam_sum[:], lam_in[:, 0:2], op=ALU.add, axis=AX.X).then_inc(lam_summed, 1)
            nc.vector.tensor_tensor(wqkv_lo[:], later.wqkv[:], wqkv_hi[:].bitcast(F32), ALU.subtract)
            nc.vector.tensor_scalar(wo[:], later.diff_wo[:], head_w[:, 0:1], 1.0 - LAMBDA_INIT, ALU.mult, ALU.mult)
            nc.vector.tensor_copy(ident_bf[:], ident[:])
            nc.vector.tensor_copy(ident_h[:], ident[:])
            nc.vector.memset(branch[:, :, 0], 1.0)
            nc.vector.tensor_copy(mask[:], later.causal[:].unsqueeze(1).broadcast_to([P, 4, P]))
            dve.wait_ge(lam_exped, 1)
            once(nc.vector.tensor_tensor(branch[:, :, 1], lam_exp[:, 1], lam_exp[:, 0], ALU.subtract))
            nc.vector.tensor_scalar(branch[:, :, 1], branch[:, :, 1], -LAMBDA_INIT, None, ALU.add).then_inc(prepared, 1)
            nc.vector.memset(q_pack[:].bitcast(F32), 0.0).then_inc(packs_ready, 1)
            nc.vector.memset(k_pack[:].bitcast(F32), 0.0).then_inc(packs_ready, 1)

            def maxima(B, u, par):
                dve.wait_ge(s_ready, B * STEPS + u + 1)
                j, m0, n = (1, 2 * u, 2) if u < 16 else (0, 4 * (u - 16), 4)
                nc.vector.tensor_reduce(q_pack[:, par, j, m0:m0 + n, 3 * HD], s_ps[:, u % 2].rearrange("p (m k) -> p m k", m=n),
                                        op=ALU.max, axis=AX.X, negate=True).then_inc(max_ready, 1)

            def weigh(b, half):
                d_step.begin(b)
                d_step.k = 5 * half
                dve.wait_ge(o_in_psum, b * 2 + half + 1)
                om = m_ps[:].rearrange("p j (m d) -> p j m d", d=PACK)
                d_step(nc.vector.reciprocal(inv[:], om[:, :, :, HD]))
                br = branch[:, 8 * half:8 * half + 8].rearrange("p h r -> p (h r)").unsqueeze(1).broadcast_to([P, 2, 16])
                d_step(nc.vector.tensor_tensor(inv[:], inv[:], br, ALU.mult))
                nc.vector.tensor_tensor(weighted[:, :, 16 * half:16 * half + 16], om[:, :, :, 0:HD],
                                        inv[:].unsqueeze(3).broadcast_to([P, 2, 16, HD]), ALU.mult).then_inc(o_weighted, 1)

            def combine(b, half):
                dve.wait_ge(o_weighted, b * 2 + half + 1)
                heads = slice(8 * half, 8 * half + 8)
                both = weighted[:, :, 16 * half:16 * half + 16].rearrange("p j (h r) d -> p j h r d", r=2)
                om, sq = o[:, :, heads], osq[:, :, heads]
                d_step(nc.vector.tensor_tensor(om, both[:, :, :, 0], both[:, :, :, 1], ALU.add))
                d_step(nc.vector.tensor_tensor(sq, om, om, ALU.mult))
                d_step(nc.vector.tensor_reduce(ms[:, :, heads], sq, op=ALU.add, axis=AX.X))
                nc.vector.tensor_scalar(ms[:, :, heads], ms[:, :, heads], 1.0 / HD, RMS_EPS, ALU.mult, ALU.add).then_inc(ms_ready, 1)

            def turn(A, B, C, D, par):
                for u in range(STEPS):
                    if (u == 2 and D is not None) or (u == 14 and C is not None):
                        dve.wait_ge(pv_done, (D + 1) * STEPS if u == 2 else C * STEPS + HALF)
                        if u == 2:
                            dve.wait_ge(o_in_psum, D * 2 + 1)
                        elif not below(C, 1):
                            dve.wait_ge(o_in_psum, C * 2)
                        nc.vector.tensor_copy(oT[:, 1], ot_ps[:, 1]).then_inc(oT_copied, 1)
                    if B is not None:
                        maxima(B, u, 1 - par)
                    if A is not None:
                        if u == 20:
                            statistics(A + 1)
                        if u == 0:
                            dve.wait_ge(rstd_ready, A + 1)
                            for j in range(2):
                                last = nc.vector.tensor_scalar(xn[:, j], x[:, A * 2 + j], mv[:, j, 0:1], rstd[:, j:j + 1],
                                                               ALU.subtract, ALU.mult)
                            last.then_inc(xn_ready, 1)
                        if u == 3:
                            dve.wait_ge(xT_hi_ready, A + 1)
                            nc.vector.tensor_tensor(xT_lo[:], m_ps[:, 0, 0:S], xT_hi[:].bitcast(F32),
                                                    ALU.subtract).then_inc(xT_ready, 1)
                        if u in (8, 11):
                            j = (u - 8) // 3
                            dve.wait_ge(qkv_in_psum, A * 2 + j + 1)
                            if B is not None:
                                dve.wait_ge(v_ready, B + 1)
                            flat = qk[:, j].rearrange("p m d -> p (m d)")
                            nc.vector.tensor_tensor(flat[:, 0:W2], m_ps[:, 0, 0:W2], qkv_bias[:, 0:W2], ALU.add)
                            nc.vector.tensor_tensor(flat[:, W2:512], m_ps[:, 1, 0:512 - W2], qkv_bias[:, W2:512], ALU.add)
                            nc.vector.tensor_tensor(v_new[:, j].rearrange("p h d -> p (h d)"), m_ps[:, 1, 512 - W2:W2],
                                                    qkv_bias[:, 512:], ALU.add).then_inc(qkv_ready, 1)
                        if u == 12:
                            dve.wait_ge(qkv_ready, A * 2 + 2)
                            hf = HD // 2
                            for lo, hi in ((0, hf), (hf, 0)):
                                last = nc.vector.tensor_tensor(by_sin[:, :, :, lo:lo + hf], qk[:, :, :, hi:hi + hf],
                                                               rope_sin[:, :, lo:lo + hf].unsqueeze(2).broadcast_to([P, 2, 2 * MAPS, hf]),
                                                               ALU.mult)
                            last.then_inc(sin_ready, 1)
                        if u == 13:
                            dve.wait_ge(sin_ready, A + 1)
                            dve.wait_ge(cos_ready, A * 2 + 2)
                            flat = "p j m d -> p (j m d)"
                            nc.vector.tensor_tensor(rot[:].rearrange(flat), by_cos[:].rearrange(flat), by_sin[:].rearrange(flat),
                                                    ALU.add).then_inc(rot_ready, 1)
                        if u == 16:
                            dve.wait_ge(pack_hi, A * 4 + 4)
                            for j in range(2):
                                last = nc.vector.tensor_tensor(k_pack[:, j, :, 2 * HD:3 * HD], rot[:, j, MAPS:],
                                                               k_pack[:, j, :, 0:HD], ALU.subtract)
                            last.then_inc(pack_lo, 1)
                    if D is not None:
                        if u == 6:
                            weigh(D, 1)
                            combine(D, 1)
                            d_step.end()
                        if u == 10:
                            dve.wait_ge(rms_ready, D * 4 + 4)
                            nc.vector.tensor_tensor(on[:].rearrange("p j h d -> p (j h) d"), o[:].rearrange("p j h d -> p (j h) d"),
                                                    rms[:].rearrange("p j h -> p (j h)").unsqueeze(2).broadcast_to([P, 2 * HEADS, HD]),
                                                    ALU.mult).then_inc(on_ready, 1)
                        if u == 15:
                            dve.wait_ge(y_in_psum, D + 1)
                            xs = x[:, bass.ds(D * 2, 2)]
                            nc.vector.tensor_tensor(xs, xs, m_ps[:, 1, 0:S].rearrange("p (j d) -> p j d", d=P),
                                                    ALU.add).then_inc(x_added, 1)
                            dve.wait_ge(x_added, D * 2 + 1)
                            nc.vector.tensor_tensor(xs, xs, wo_bias[:].unsqueeze(1).broadcast_to([P, 2, P]),
                                                    ALU.add).then_inc(x_added, 1)
                    if C is not None and u == 17:
                        weigh(C, 0)
                    if C is not None and u == 18:
                        combine(C, 0)

            turns(dve, turn)
            dve.wait_ge(x_added, 2 * NB)

        @block.tensor
        def _(pe):
            pe.wait_ge(prepared, 1)

            def scores(B, u, par):
                if not (below(B, 1) and u < 2):
                    pe.wait_ge(max_ready, B * STEPS + u - 1)
                if u == 0:
                    pe.wait_ge(packT_ready, B * 4 + 3)
                    pe.wait_ge(k_one_ready[0], B * 64 + 64)
                if u == 8:
                    pe.wait_ge(k_one_ready[1], B * 64 + 64)
                out = s_ps[:, u % 2]
                j, m0, n = (1, 2 * u, 2) if u < 16 else (0, 4 * (u - 16), 4)
                if j:
                    nc.tensor.matmul(out.rearrange("p (m k) -> p m k", k=P)[:, 1::2], ident_bf[:], mask[:, 0:2], start=True, stop=False,
                                     skip_group_check=True)
                else:
                    nc.tensor.matmul(out, ident_bf[:], mask[:].rearrange("p a b -> p (a b)"), start=True, stop=False,
                                     skip_group_check=True)
                wd = 512 // n
                for i in range(n):
                    c, r = divmod(m0 + i, 4)
                    last = nc.tensor.matmul(out[:, i * wd:(i + 1) * wd], qT[:, par, c, j * P:(j + 1) * P],
                                            k_one[:, par, r, c, 0:wd], start=False, stop=True, skip_group_check=True)
                last.then_inc(s_ready, 1)

            def scores_T(C, u, par):
                if not (below(C, 1) and u < 2):
                    pe.wait_ge(exp_ready, C * STEPS + u - 1)
                if u == 0:
                    pe.wait_ge(qmT_ready, C * 2 + 1)
                if u == 4:
                    pe.wait_ge(qmT_ready, C * 2 + 2)
                key, m0, n = unit(u)
                wd = 512 // n
                for i in range(n):
                    c, r = divmod(m0 + i, 4)
                    q0 = P if key else 0
                    last = nc.tensor.matmul(st_ps[:, u % 2, i * wd:(i + 1) * wd], k_one[:, par, r, c, key * P:(key + 1) * P],
                                            qmT[:, par, c, q0:q0 + wd], start=True, stop=True)
                last.then_inc(st_ready, 1)

            def values(b, u, par):
                pe.wait_ge(prob_ready, b * STEPS + u + 1)
                if u == 0:
                    pe.wait_ge(v_ready, b + 1)
                    if not below(b, 1):
                        pe.wait_ge(oT_copied, b * 4)
                if u == HALF:
                    pe.wait_ge(oT_copied, b * 4 + 2)
                key, m0, n = unit(u)
                for part in ((1,) if key else (1, 0)):
                    for i in range(n):
                        c, r = divmod((m0 + i) % 16, 4)
                        col = (c % 2) * S + part * P
                        pr = prob[:, u % RING].rearrange("p (m q) -> p m q", m=n)
                        src = pr[:, i, 0:P] if key else pr[:, i, part * P:(part + 1) * P]
                        last = nc.tensor.matmul(ot_ps[32 * r:32 * r + 32, c // 2, col:col + P],
                                                v[:, par, key, (m0 + i) // 2], src,
                                                start=bool(key) and c % 2 == 0, stop=not key, skip_group_check=True)
                last.then_inc(pv_done, 1)

            def turn(A, B, C, D, par):
                for u in range(STEPS):
                    if B is not None:
                        scores(B, u, 1 - par)
                    if C is not None:
                        if u == 0:
                            pe.wait_ge(max_ready, (C + 1) * STEPS)
                            pe.wait_ge(qmT_ready, C * 2 + 1)
                            for c in range(CH):
                                last = nc.tensor.transpose(m16[1][:, c * P:(c + 1) * P],
                                                           q_pack[:, par, 0, 4 * c:4 * c + 4].rearrange("p m e -> p (m e)"), ident_h[:])
                            last.then_inc(qmT_in_psum, 1)
                        scores_T(C, u, par)
                    if u >= LAG and C is not None:
                        values(C, u - LAG, par)
                    if u < LAG and D is not None:
                        values(D, STEPS - LAG + u, 1 - par)
                    if u == 2 and A is not None:
                        pe.wait_ge(xn_ready, A + 1)
                        if not below(A, 1):
                            pe.wait_ge(packT_ready, A * 4)
                        for j in range(2):
                            last = nc.tensor.transpose(m_ps[:, 0, j * P:(j + 1) * P], xn[:, j], ident[:])
                        last.then_inc(xT_in_psum, 1)
                    if (u == 5 and D is not None) or (u == 16 and C is not None):
                        b, half = (D, 1) if u == 5 else (C, 0)
                        pe.wait_ge(oT_copied, (b * 2 + half + 1) * 2)
                        if u == 5:
                            if A is not None:
                                pe.wait_ge(xT_ready, A + 1)
                            if C is not None:
                                pe.wait_ge(qmT_ready, C * 2 + 2)
                            pe.wait_ge(o_weighted, D * 2 + 1)
                        else:
                            if D is not None:
                                pe.wait_ge(onT_ready, D + 1)
                                pe.wait_ge(x_added, D * 2 + 1)
                            elif A is not None:
                                pe.wait_ge(qkv_ready, A * 2 + 2)
                        for j in range(2):
                            for c in range(4):
                                last = nc.tensor.transpose(m_ps[:, j, c * P:(c + 1) * P],
                                                           oT[:, c // 2, (c % 2) * S + j * P:(c % 2) * S + (j + 1) * P], ident[:])
                        last.then_inc(o_in_psum, 1)
                    if u in (7, 10) and A is not None:
                        j = (u - 7) // 3
                        pe.wait_ge(xT_ready, A + 1)
                        if j == 1:
                            pe.wait_ge(qkv_ready, A * 2 + 1)
                        else:
                            if C is not None:
                                pe.wait_ge(qmT_ready, C * 2 + 2)
                            if D is not None:
                                pe.wait_ge(o_weighted, D * 2 + 2)
                        for part in range(2):
                            for i, (xt, wt) in enumerate(((xT_hi, wqkv_hi), (xT_hi, wqkv_lo), (xT_lo, wqkv_hi))):
                                last = nc.tensor.matmul(m_ps[:, part, 0:W2], xt[:, j * P:(j + 1) * P],
                                                        wt[:, part * W2:(part + 1) * W2], start=(i == 0), stop=(i == 2))
                        last.then_inc(qkv_in_psum, 1)
                    if u == 12 and D is not None:
                        pe.wait_ge(on_ready, D + 1)
                        if A is not None:
                            pe.wait_ge(qkv_ready, A * 2 + 2)
                        for j in range(2):
                            last = nc.tensor.transpose(m_ps[:, 0, j * P:(j + 1) * P], on[:, j].rearrange("p h d -> p (h d)"), ident[:])
                        last.then_inc(onT_in_psum, 1)
                    if u == 14 and D is not None:
                        pe.wait_ge(onT_ready, D + 1)
                        for j in range(2):
                            last = nc.tensor.matmul(m_ps[:, 1, j * P:(j + 1) * P], onT[:, j * P:(j + 1) * P], wo[:], start=True, stop=True)
                        last.then_inc(y_in_psum, 1)
                    if A is not None and u in (18, 22):
                        h4 = 0 if u == 18 else 4
                        if u == 18:
                            pe.wait_ge(pack_lo, A + 1)
                            if C is not None:
                                pe.wait_ge(o_weighted, C * 2 + 1)
                        else:
                            pe.wait_ge(packT_ready, A * 4 + 3)
                        for c in range(4):
                            for j in range(2):
                                last = nc.tensor.transpose(m16[0][:, c * S + j * P:c * S + (j + 1) * P],
                                                           k_pack[:, j, 4 * (h4 + c):4 * (h4 + c) + 4].rearrange("p m e -> p (m e)"), ident_h[:])
                        last.then_inc(packT_in_psum, 1)
                    if A is not None and u in (19, 20):
                        j = u - 19
                        pe.wait_ge(pack_lo_q, A + 1)
                        if j == 1:
                            pe.wait_ge(packT_ready, A * 4 + 1)
                        for c in range(CH):
                            last = nc.tensor.transpose(m16[1 - j][:, c * P:(c + 1) * P],
                                                       q_pack[:, par, j, 4 * c:4 * c + 4].rearrange("p m e -> p (m e)"), ident_h[:])
                        last.then_inc(packT_in_psum, 1)
                    if B is not None and u == 21:
                        pe.wait_ge(max_ready, B * STEPS + 16)
                        if A is not None:
                            pe.wait_ge(packT_ready, A * 4 + 2)
                        elif C is not None:
                            pe.wait_ge(o_weighted, C * 2 + 1)
                        for c in range(CH):
                            last = nc.tensor.transpose(m16[1][:, c * P:(c + 1) * P],
                                                       q_pack[:, 1 - par, 1, 4 * c:4 * c + 4].rearrange("p m e -> p (m e)"), ident_h[:])
                        last.then_inc(qmT_in_psum, 1)

            turns(pe, turn)


def linear_attention(nc, tag, x, ident, neghalf, made, later):
    NF = later.lin_wo.shape[1]
    CS = later.lin_c.shape[1]
    NG = x.shape[1] // TG - 1
    S = 2 * P
    RING = 4
    LAG = 3
    DECAY_MAX = 0.9995
    with ExitStack() as ctx:
        nm = Names(nc, ctx, tag)
        w_in, c_in, wo, cs2, b1, rows = later.lin_w, later.lin_c, later.lin_wo, later.lin_cs2, later.lin_b1, later.lin_rows
        w_hi = nm.sb("w_hi", [P, 2 + NF, P], F32R)
        w_lo = nm.sb("w_lo", [P, 2 + NF, P], F32R)
        c_hi = nm.sb("c_hi", [P, CS], F32R)
        c_lo = nm.sb("c_lo", [P, CS], F32R)
        half_b2 = nm.sb("half_b2", [P, 1], F32)
        tbase = nm.sb("tbase", [P, 1], F32)
        lam_scale = nm.sb("lam_scale", [P, 1], F32)
        lam_shift = nm.sb("lam_shift", [P, 1], F32)

        stats = nm.sb("stats", [P, TG, 6], F32)
        mv = nm.sb("mv", [P, 2, TG, 2], F32)
        var = nm.sb("var", [P, TG], F32)
        rstd = nm.sb("rstd", [P, 2, TG], F32)
        xn = nm.sb("xn", [P, TG, P], F32)
        xT_hi = nm.sb("xT_hi", [P, 2, GN], F32R)
        xT_lo = nm.sb("xT_lo", [P, 2, GN], F32R)
        hid = nm.sb("hid", [CS, GN], F32)
        th = nm.sb("th", [P, GN], F32)
        lam = nm.sb("lam", [P, 2, GN], F32)
        kT = nm.sb("kT", [P, 2, GN], F32)
        qT = nm.sb("qT", [P, 2, GN], F32)
        kv = nm.sb("kv", [P, 2, GN], F32)
        state = nm.sb("state", [P, 2, GN], F32)
        y = nm.sb("y", [P, RING, GN], F32)

        t_ps = nm.ps("t_ps", [P, GN], F32)
        c_ps = nm.ps("c_ps", [P, GN], F32)
        kq_ps = nm.ps("kq_ps", [P, GN], F32)
        v_ps = nm.ps("v_ps", [P, 2, GN], F32)
        o_ps = nm.ps("o_ps", [P, 2, GN], F32)

        base_ready = nm.sem("base_ready")
        prepared = nm.sem("prepared")
        once_own = nm.sem("once_own")
        stats_own = nm.sem("stats_own")
        lam_own = nm.sem("lam_own")
        kv_own = nm.sem("kv_own")
        var_ready = nm.sem("var_ready")
        rstd_ready = nm.sem("rstd_ready")
        xn_ready = nm.sem("xn_ready")
        xT_in_psum = nm.sem("xT_in_psum")
        xT_hi_ready = nm.sem("xT_hi_ready")
        xT_ready = nm.sem("xT_ready")
        hid_in_psum = nm.sem("hid_in_psum")
        hid_ready = nm.sem("hid_ready")
        lc_in_psum = nm.sem("lc_in_psum")
        th_ready = nm.sem("th_ready")
        lam_ready = nm.sem("lam_ready")
        kq_in_psum = nm.sem("kq_in_psum")
        kq_ready = nm.sem("kq_ready")
        v_ready = nm.sem("v_ready")
        state_ready = nm.sem("state_ready")
        y_ready = nm.sem("y_ready")
        y_used = nm.sem("y_used")
        x_added = nm.sem("x_added")
        block = ctx.enter_context(nc.Block())

        def pairs(engine, group):
            group(0, 0, True, True)
            group(1, 1, False, True)
            with engine.Fori(1, NG // 2 - 1) as i:
                group(i * 2, 0, False, True)
                group(i * 2 + 1, 1, False, True)
            group(NG - 2, 0, False, True)
            group(NG - 1, 1, False, False)

        def early(g, n):
            return isinstance(g, int) and g < n

        @block.gpsimd
        def _(pool):
            def scale_of(g, b):
                pool.wait_ge(var_ready, g + 1)
                nc.gpsimd.tensor_tensor(rstd[:, b], var[:], neghalf[:, 0:TG], ALU.pow).then_inc(rstd_ready, 1)

            scale_of(0, 0)
            scale_of(1, 1)

            def group(g, b, is_first, prepares):
                for f in range(NF):
                    n = g * NF + f
                    pool.wait_ge(state_ready, n + 1)
                    if not (is_first and f < RING):
                        pool.wait_ge(y_used, n + 1 - RING)
                    nc.gpsimd.tensor_tensor(y[:, f % RING], state[:, f % 2], qT[:, b], ALU.mult).then_inc(y_ready, 1)
                    if f == 2 and prepares:
                        scale_of(g + 2, b)

            pairs(pool, group)

        @block.scalar
        def _(a):
            a.wait_ge(later.lin_in, later.LIN_LOADS)
            nc.scalar.activation(tbase[:], rows[:, 1:2], ACT.Tanh, scale=0.5).then_inc(base_ready, 1)
            a.wait_ge(prepared, 1)

            def high(g, b):
                a.wait_ge(xT_in_psum, g + 1)
                nc.scalar.activation(xT_hi[:, b], t_ps[:], ACT.Copy).then_inc(xT_hi_ready, 1)

            def hidden(g):
                a.wait_ge(hid_in_psum, g + 1)
                nc.scalar.activation(hid[:], c_ps[0:CS], ACT.Tanh, bias=b1[:, 0:1]).then_inc(hid_ready, 1)

            def decay(g):
                a.wait_ge(lc_in_psum, g + 1)
                nc.scalar.activation(th[:], c_ps[:], ACT.Tanh, bias=half_b2[:, 0:1], scale=0.5).then_inc(th_ready, 1)

            def copy_kq(g, b, which):
                a.wait_ge(kq_in_psum, g * 2 + which + 1)
                nc.scalar.activation((kT, qT)[which][:, b], kq_ps[:], ACT.Copy).then_inc(kq_ready, 1)

            high(0, 0)
            hidden(0)
            copy_kq(0, 0, 0)
            decay(0)
            copy_kq(0, 0, 1)

            def group(g, b, is_first, prepares):
                if prepares:
                    high(g + 1, 1 - b)
                    hidden(g + 1)
                    if not early(g, 1):
                        a.wait_ge(y_ready, g * NF)
                    copy_kq(g + 1, 1 - b, 0)
                    decay(g + 1)
                    copy_kq(g + 1, 1 - b, 1)

            pairs(a, group)

        @block.vector
        def _(dve):
            once = Steps(dve, once_own, 0)
            once.begin(0)
            stats_step = Steps(dve, stats_own, 2)

            def statistics(g, b):
                stats_step.begin(g)
                for t in range(TG):
                    last = nc.vector.bn_stats(stats[:, t], x[:, g * TG + t])
                stats_step(last, made)
                for t in range(TG):
                    last = nc.vector.bn_aggr(mv[:, b, t], stats[:, t])
                stats_step(last)
                stats_step.end()
                nc.vector.tensor_scalar(var[:], mv[:, b, :, 1], LN_EPS, None, ALU.add).then_inc(var_ready, 1)

            def normalise(g, b):
                dve.wait_ge(rstd_ready, g + 1)
                for t in range(TG):
                    last = nc.vector.tensor_scalar(xn[:, t], x[:, g * TG + t], mv[:, b, t, 0:1], rstd[:, b, t:t + 1],
                                                   ALU.subtract, ALU.mult)
                last.then_inc(xn_ready, 1)

            def low(g, b):
                dve.wait_ge(xT_hi_ready, g + 1)
                nc.vector.tensor_tensor(xT_lo[:, b], t_ps[:], xT_hi[:, b].bitcast(F32), ALU.subtract).then_inc(xT_ready, 1)

            def make_lam(g, b):
                dve.wait_ge(th_ready, g + 1)
                nc.vector.tensor_scalar(lam[:, b], th[:], lam_scale[:, 0:1], lam_shift[:, 0:1], ALU.mult, ALU.add).then_inc(lam_own, 1)
                dve.wait_ge(lam_own, g + 1)
                nc.vector.tensor_scalar(lam[:, b], lam[:, b], 0.0, DECAY_MAX, ALU.max, ALU.min).then_inc(lam_ready, 1)

            statistics(0, 0)
            normalise(0, 0)
            statistics(1, 1)
            dve.wait_ge(later.lin_in, later.LIN_LOADS)
            once(nc.vector.tensor_copy(w_hi[:], w_in[:]))
            once(nc.vector.tensor_tensor(w_lo[:], w_in[:], w_hi[:].bitcast(F32), ALU.subtract))
            once(nc.vector.tensor_copy(c_hi[:], c_in[:]))
            once(nc.vector.tensor_tensor(c_lo[:], c_in[:], c_hi[:].bitcast(F32), ALU.subtract))
            dve.wait_ge(base_ready, 1)
            once(nc.vector.tensor_scalar(tbase[:], tbase[:], 0.5, 0.5, ALU.mult, ALU.add))
            once(nc.vector.tensor_scalar(lam_scale[:], tbase[:], 0.1, None, ALU.mult))
            once(nc.vector.tensor_scalar(lam_shift[:], tbase[:], 1.1, None, ALU.mult))
            nc.vector.tensor_scalar(half_b2[:], rows[:, 0:1], 0.5, None, ALU.mult).then_inc(prepared, 1)
            low(0, 0)
            make_lam(0, 0)

            def outer(g, b, f):
                n = g * NF + f
                if f == 0:
                    dve.wait_ge(kq_ready, g * 2 + 1)
                dve.wait_ge(v_ready, n + 1)
                if not (early(g, 1) and f < 2):
                    dve.wait_ge(state_ready, n - 1)
                nc.vector.tensor_tensor(kv[:, f % 2], v_ps[:, f % 2], kT[:, b], ALU.mult).then_inc(kv_own, 1)

            def scan(g, b, f):
                n = g * NF + f
                if f == 0:
                    dve.wait_ge(lam_ready, g + 1)
                    dve.wait_ge(kq_ready, g * 2 + 2)
                dve.wait_ge(kv_own, n + 1)
                if not (early(g, 1) and f < 2):
                    dve.wait_ge(y_ready, n - 1)
                for s in range(GN // S):
                    cols = slice(s * S, (s + 1) * S)
                    last = nc.vector.tensor_tensor_scan(state[:, f % 2, cols], lam[:, b, cols], kv[:, f % 2, cols],
                                                        0.0, ALU.mult, ALU.add)
                last.then_inc(state_ready, 1)

            def add_out(g, b):
                dve.wait_ge(y_used, (g + 1) * NF)
                xs = x[:, bass.ds(g * TG, TG)].rearrange("p t d -> p (t d)")
                nc.vector.tensor_tensor(xs, xs, o_ps[:, b], ALU.add).then_inc(x_added, 1)

            def group(g, b, is_first, prepares):
                for f in range(NF):
                    outer(g, b, f)
                    if f >= 1:
                        scan(g, b, f - 1)
                    if prepares:
                        if f == 0:
                            normalise(g + 1, 1 - b)
                        if f == 3:
                            statistics(g + 2, b)
                        if f == 2:
                            low(g + 1, 1 - b)
                        if f == 7:
                            make_lam(g + 1, 1 - b)
                    if f == 5 and not is_first:
                        add_out(g - 1, 1 - b)
                scan(g, b, NF - 1)

            pairs(dve, group)
            add_out(NG - 1, 1)
            dve.wait_ge(x_added, NG)

        @block.tensor
        def _(pe):
            def transpose_x(g):
                pe.wait_ge(xn_ready, g + 1)
                for t in range(TG):
                    last = nc.tensor.transpose(t_ps[:, t * P:(t + 1) * P], xn[:, t], ident[:])
                last.then_inc(xT_in_psum, 1)

            def three(out, hi, lo, b):
                for i, (wt, xt) in enumerate(((hi, xT_hi), (hi, xT_lo), (lo, xT_hi))):
                    last = nc.tensor.matmul(out, wt, xt[:, b], start=(i == 0), stop=(i == 2))
                return last

            def hidden(g, b):
                pe.wait_ge(xT_ready, g + 1)
                if not early(g, 1):
                    pe.wait_ge(th_ready, g)
                three(c_ps[0:CS], c_hi[:], c_lo[:], b).then_inc(hid_in_psum, 1)

            def project(g, b, which):
                if not (early(g, 1) and which == 0):
                    pe.wait_ge(kq_ready, g * 2 + which)
                three(kq_ps[:], w_hi[:, which], w_lo[:, which], b).then_inc(kq_in_psum, 1)

            def decay(g):
                pe.wait_ge(hid_ready, g + 1)
                nc.tensor.matmul(c_ps[:], cs2[:], hid[:], start=True, stop=True).then_inc(lc_in_psum, 1)

            def project_v(g, b, f):
                if not (early(g, 1) and f < 2):
                    pe.wait_ge(kv_own, g * NF + f - 1)
                three(v_ps[:, f % 2], w_hi[:, 2 + f], w_lo[:, 2 + f], b).then_inc(v_ready, 1)

            def output(g, b, f):
                pe.wait_ge(y_ready, g * NF + f + 1)
                if f == 0 and not early(g, 2):
                    pe.wait_ge(x_added, g - 1)
                for t in range(TG):
                    last = nc.tensor.matmul(o_ps[:, b, t * P:(t + 1) * P], y[:, f % RING, t * P:(t + 1) * P], wo[:, f],
                                            start=(f == 0 and t == 0), stop=(f == NF - 1), skip_group_check=True)
                last.then_inc(y_used, 1)

            transpose_x(0)
            pe.wait_ge(prepared, 1)
            hidden(0, 0)
            project(0, 0, 0)
            decay(0)
            project(0, 0, 1)

            def group(g, b, is_first, prepares):
                for f in range(NF):
                    project_v(g, b, f)
                    if prepares:
                        if f == 2:
                            transpose_x(g + 1)
                        if f == 5:
                            hidden(g + 1, 1 - b)
                            project(g + 1, 1 - b, 0)
                        if f == min(7, 5 + 1):
                            decay(g + 1)
                        if f == min(7, 5 + 2):
                            project(g + 1, 1 - b, 1)
                    if f >= LAG:
                        output(g, b, f - LAG)
                    elif not is_first:
                        output(g - 1, 1 - b, NF - LAG + f)

            pairs(pe, group)
            for f in range(NF - LAG, NF):
                output(NG - 1, 1, f)


def build(nc, phases, x_d, const, ins, out_d):
    T = x_d.shape[0] * x_d.shape[1] // P
    with ExitStack() as ctx:
        nm = Names(nc, ctx, "all")
        x = nm.sb("x", [P, T + TG, P], F32)
        ident = nm.sb("ident", [P, P], F32)
        neghalf = nm.sb("neghalf", [P, 64], F32)
        loaded = nm.sem("loaded")
        stored = nm.sem("stored")
        made = nm.sem("made")
        x_tiles = x_d.rearrange("b (t p) d -> p (b t) d", p=P)
        out_tiles = out_d.rearrange("b (t p) d -> p (b t) d", p=P)
        later = LaterWeights(nc, ctx, ins)
        with nc.Block() as block:
            @block.sync
            def _(sp):
                sp.dma_start(ident[:], const["ident"]).then_inc(loaded, 16)
                for q in range(4):
                    sp.dma_start(x[:, q * T // 4:(q + 1) * T // 4], x_tiles[:, q * T // 4:(q + 1) * T // 4]).then_inc(loaded, 16)
                if "a" not in phases:
                    sp.wait_ge(loaded, 16 * LOADS_OF_X)
                    later.load(sp)

            @block.vector
            def _(dve):
                nc.vector.memset(neghalf[:], -0.5)
                nc.vector.memset(x[:, T:], 0.0).then_inc(made, 1)
                dve.wait_ge(made, 1)
        if "a" in phases:
            moe_ffn(nc, "moe0", x, ident, neghalf, made, ins, loaded, later)
        if "b" in phases:
            diff_attention(nc, "diff", x, ident, neghalf, made, later)
        if "c" in phases:
            moe_ffn(nc, "moe1", x, ident, neghalf, made, ins)
        if "d" in phases or "f" in phases:
            dequantized = dequantized_weights(nc, ctx, later)
        if "d" in phases:
            quantized_ffn(nc, "ffn0", x, ident, neghalf, made, dequantized)
        if "e" in phases:
            linear_attention(nc, "lin", x, ident, neghalf, made, later)
        if "f" in phases:
            quantized_ffn(nc, "ffn1", x, ident, neghalf, made, dequantized, out_tiles, stored)
        else:
            with nc.Block() as block:
                @block.sync
                def _(sp):
                    sp.dma_start(out_tiles, x[:, 0:T]).then_inc(stored, 16)
                    sp.wait_ge(stored, 16)


_NAMES = ['L0_attn_x', 'L0_attn_Wq', 'L0_attn_bq', 'L0_attn_Wk', 'L0_attn_bk', 'L0_attn_Wv', 'L0_attn_bv', 'L0_attn_Wo', 'L0_attn_bo', 'L0_attn_head_norm_w', 'L0_attn_lq1', 'L0_attn_lk1', 'L0_attn_lq2', 'L0_attn_lk2', 'L0_ffn_router_w', 'L0_ffn_experts_bias', 'L0_ffn_w1', 'L0_ffn_w3', 'L0_ffn_w2', 'L0_ffn_sw1', 'L0_ffn_sw3', 'L0_ffn_sw2', 'L1_attn_q_w', 'L1_attn_k_w', 'L1_attn_v_w', 'L1_attn_o_w', 'L1_attn_cs_w1', 'L1_attn_cs_b1', 'L1_attn_cs_w2', 'L1_attn_cs_b2', 'L1_attn_decay_params', 'L1_ffn_ln_gamma', 'L1_ffn_ln_beta', 'L1_ffn_fc1_q', 'L1_ffn_fc1_scales', 'L1_ffn_fc1_bias', 'L1_ffn_fc2_q', 'L1_ffn_fc2_scales', 'L1_ffn_fc2_bias']


def layout(inputs):
    d = {}
    a = {k: np.asarray(v) for k, v in inputs.items()}
    d["x"] = a["L0_attn_x"]
    d["ident"] = np.eye(P, dtype=np.float32)
    d["router_T"] = a["L0_ffn_router_w"].T
    d["router_bias"] = a["L0_ffn_experts_bias"].reshape(-1, 1)
    d["wqkv"] = np.concatenate([a["L0_attn_Wq"], a["L0_attn_Wk"], a["L0_attn_Wv"]], axis=0).T
    d["qkv_bias"] = np.concatenate([a["L0_attn_bq"], a["L0_attn_bk"], a["L0_attn_bv"]]).reshape(1, -1)
    d["wo_T"] = a["L0_attn_Wo"].T
    d["wo_bias"] = a["L0_attn_bo"].reshape(1, -1)
    d["head_w"] = a["L0_attn_head_norm_w"].reshape(-1, 1)
    d["lam"] = np.stack([a["L0_attn_lq1"], a["L0_attn_lq2"], a["L0_attn_lk1"], a["L0_attn_lk2"]])
    half = a["L0_attn_head_norm_w"].shape[1] // 2
    freq = (1.0 / np.float32(10000.0) ** (np.arange(half, dtype=np.float32) / np.float32(half))).astype(np.float32)
    angle = np.arange(2 * P, dtype=np.float32)[:, None] * freq[None]
    cos, sin = np.cos(angle), np.sin(angle)
    d["rope_cos"] = np.concatenate([cos, cos], axis=1).reshape(2, P, -1).transpose(1, 0, 2)
    d["rope_sin"] = np.concatenate([-sin, sin], axis=1).reshape(2, P, -1).transpose(1, 0, 2)
    d["causal"] = np.triu(np.full((P, P), -1e30, np.float32), 1)
    H1, E1 = a["L1_attn_decay_params"].shape
    d["wkq"] = np.stack([a["L1_attn_k_w"].T, a["L1_attn_q_w"].T], axis=1)
    d["wv_f"] = np.repeat(a["L1_attn_v_w"].reshape(H1, E1, P).transpose(1, 2, 0), E1, axis=2)
    d["wo_f"] = np.repeat(a["L1_attn_o_w"].reshape(P, H1, E1).transpose(2, 1, 0), E1, axis=1)
    d["cs_w1T"] = a["L1_attn_cs_w1"].T
    d["cs_w2T"] = np.repeat(a["L1_attn_cs_w2"].T, E1, axis=1)
    d["cs_b1"] = a["L1_attn_cs_b1"].reshape(-1, 1)
    d["rows"] = np.stack([np.repeat(a["L1_attn_cs_b2"], E1), a["L1_attn_decay_params"].reshape(-1)], axis=1)
    for k in ("fc1_q", "fc1_scales", "fc2_q", "fc2_scales"):
        d[k] = a["L1_ffn_" + k]
    chunks = a["L1_ffn_fc1_bias"].reshape(-1, P)
    d["ffn1_cols"] = np.stack([a["L1_ffn_ln_gamma"], a["L1_ffn_ln_beta"], *chunks], axis=1)
    d["fc2_bias"] = a["L1_ffn_fc2_bias"].reshape(1, -1)
    for k in ("w1", "w3", "w2", "sw1", "sw3", "sw2"):
        d[k] = a["L0_ffn_" + k]
    return {k: np.ascontiguousarray(v) for k, v in d.items()}


def program(nc, arrays, phases="abcdef"):
    ins = {k: nc.dram_tensor(f"in_{k}", v.shape, mybir.dt.from_np(v.dtype), kind="ExternalInput").ap()
           for k, v in arrays.items()}
    out = nc.dram_tensor("out_0", arrays["x"].shape, F32, kind="ExternalOutput").ap()
    build(nc, phases, ins["x"], ins, ins, out)


def kernel(**inputs):
    import concourse.bacc as bacc
    from concourse.bass_utils import run_bass_kernel_spmd

    arrays = layout(inputs)
    nc = bacc.Bacc("TRN2", target_bir_lowering=False, num_devices=1)
    program(nc, arrays)
    r = run_bass_kernel_spmd(nc, [{f"in_{k}": v for k, v in arrays.items()}], core_ids=[0])
    return r.results[0]["out_0"]
```
